# Optimizing a Trainium2 kernel written in Bass

```python
import numpy as np
import jax
import jax.numpy as jnp

def _softmax(x, axis=-1):
    return jax.nn.softmax(x, axis=axis)
def _gelu(x):
    return jax.nn.gelu(x, approximate=True)
def _silu(x):
    return jax.nn.silu(x)
def _sigmoid(x):
    return jax.nn.sigmoid(x)
def _layernorm(x, axis=-1, eps=1e-5):
    m = jnp.mean(x, axis=axis, keepdims=True)
    v = jnp.var(x, axis=axis, keepdims=True)
    return (x - m) / jnp.sqrt(v + eps)
def _scatter_add(tgt, idx, src, axis=0):
    return tgt.at[idx].add(src)
def _segment_sum(src, seg, n):
    return jax.ops.segment_sum(src, seg, n)

kernel_name = 'mk_conv_attn_hybrid_d2_conv_nchw512_5f5704'

def setup_inputs(seed: int = 0):
    np.random.seed(seed)
    _w = jnp.asarray
    def _rec_inputs():
        import jax
        import jax.numpy as jnp
        _gk = jax.random.key(seed)
        x = -0.0002928 + 1 * jax.random.normal(jax.random.fold_in(_gk, 1), (8, 512, 32, 32), jnp.float32)
        return x
    x = _rec_inputs()
    def _L0_conv_setup():
        import jax, jax.numpy as jnp
        import numpy as np
        from jax import lax
        B = 8
        C_IN = 512
        C_OUT = 512
        H = 32
        W = 32
        L = H * W
        D_STATE = 64
        D_CONV = 4
        EXPAND = 2
        HEADDIM = 64
        D_INNER = EXPAND * C_IN
        NHEADS = D_INNER // HEADDIM
        D_XBC = D_INNER + 2 * D_STATE
        D_IN_PROJ = 2 * D_INNER + 2 * D_STATE + NHEADS
        EPS = 1e-05
        key = jax.random.key(seed)
        ks = jax.random.split(key, 16)
        x = jax.random.normal(ks[0], (B, C_IN, H, W), jnp.float32)
        ln_w = jnp.ones((C_IN,), jnp.float32)
        ln_b = jnp.zeros((C_IN,), jnp.float32)
        in_proj_w = jax.random.normal(ks[1], (D_IN_PROJ, C_IN), jnp.float32) * 0.02
        conv1d_w = jax.random.normal(ks[2], (D_XBC, D_CONV), jnp.float32) * 0.2
        conv1d_b = jax.random.normal(ks[3], (D_XBC,), jnp.float32) * 0.02
        dt0 = jax.random.uniform(ks[4], (NHEADS,), jnp.float32, 0.001, 0.1)
        dt_bias = jnp.log(jnp.expm1(dt0))
        A_log = jnp.log(jax.random.uniform(ks[5], (NHEADS,), jnp.float32, 1.0, 16.0))
        D = jax.random.normal(ks[6], (NHEADS,), jnp.float32)
        rms_w = jnp.ones((D_INNER,), jnp.float32)
        out_proj_w = jax.random.normal(ks[7], (C_IN, D_INNER), jnp.float32) * 0.02
        conv2d_w = jax.random.normal(ks[8], (C_OUT, C_IN), jnp.float32) * 0.04
        conv2d_b = jnp.zeros((C_OUT,), jnp.float32)
        bn_g = jnp.ones((C_OUT,), jnp.float32)
        bn_b = jnp.zeros((C_OUT,), jnp.float32)
        bn_mean = jnp.zeros((C_OUT,), jnp.float32)
        bn_var = jnp.ones((C_OUT,), jnp.float32)
        return dict(x=x, ln_w=ln_w, ln_b=ln_b, in_proj_w=in_proj_w, conv1d_w=conv1d_w, conv1d_b=conv1d_b, dt_bias=dt_bias, A_log=A_log, D=D, rms_w=rms_w, out_proj_w=out_proj_w, conv2d_w=conv2d_w, conv2d_b=conv2d_b, bn_g=bn_g, bn_b=bn_b, bn_mean=bn_mean, bn_var=bn_var)
    _L0_conv_all = _L0_conv_setup()
    _L0_conv_in = {k: v for k, v in _L0_conv_all.items() if k in ('ln_w', 'ln_b', 'in_proj_w', 'conv1d_w', 'conv1d_b', 'dt_bias', 'A_log', 'D', 'rms_w', 'out_proj_w', 'conv2d_w', 'conv2d_b', 'bn_g', 'bn_b', 'bn_mean', 'bn_var', )}
    del _L0_conv_all

    def _L1_attn_setup():
        import jax, jax.numpy as jnp
        import numpy as np
        import math
        DIM = 512
        N_HEADS = 8
        N_KV_HEADS = 4
        HEAD_DIM = DIM // N_HEADS
        N_REP = N_HEADS // N_KV_HEADS

        def _rmsnorm(x, g, eps=1e-06):
            var = jnp.mean(jnp.square(x), axis=-1, keepdims=True)
            return x * jax.lax.rsqrt(var + eps) * g

        def _phi(x):
            return jnp.maximum(jax.nn.elu(x), -0.99) + 1.0
        key = jax.random.key(seed)
        ks = jax.random.split(key, 6)
        B, S = (4, 8192)
        x = jax.random.normal(ks[0], (B, S, DIM), dtype=jnp.float32)
        g = jnp.ones((DIM,), dtype=jnp.float32)
        sc = 1.0 / math.sqrt(DIM)
        wq = jax.random.normal(ks[1], (DIM, DIM), dtype=jnp.float32) * sc
        wk = jax.random.normal(ks[2], (N_KV_HEADS * HEAD_DIM, DIM), dtype=jnp.float32) * sc
        wv = jax.random.normal(ks[3], (N_KV_HEADS * HEAD_DIM, DIM), dtype=jnp.float32) * sc
        wo = jax.random.normal(ks[4], (DIM, DIM), dtype=jnp.float32) * sc
        return {'x': x, 'g': g, 'wq': wq, 'wk': wk, 'wv': wv, 'wo': wo}
    _L1_attn_all = _L1_attn_setup()
    _L1_attn_in = {k: v for k, v in _L1_attn_all.items() if k in ('g', 'wq', 'wk', 'wv', 'wo', )}
    del _L1_attn_all

    def _L1_ffn_setup():
        import jax, jax.numpy as jnp
        import numpy as np
        NUM_EXPERTS = 32
        GROUP_SIZE = 4
        NUM_GROUPS = NUM_EXPERTS // GROUP_SIZE
        C_CAP = 1.0
        key = jax.random.key(seed)
        ks = jax.random.split(key, 5)
        B, S, H = (16, 2048, 512)
        D_FF = int(H * 4 * (2.0 / 3.0))
        x = jax.random.normal(ks[0], (B, S, H), dtype=jnp.float32)
        W_router = jax.random.normal(ks[1], (H, NUM_EXPERTS), dtype=jnp.float32) * (1.0 / np.sqrt(H))
        b_router = jnp.zeros((NUM_EXPERTS,), dtype=jnp.float32)
        W_up = jax.random.normal(ks[2], (NUM_GROUPS, H, D_FF), dtype=jnp.float32) * (1.0 / np.sqrt(H))
        b_up = jnp.zeros((NUM_GROUPS, D_FF), dtype=jnp.float32)
        W_down = jax.random.normal(ks[3], (NUM_EXPERTS, D_FF, H), dtype=jnp.float32) * (1.0 / np.sqrt(D_FF))
        b_down = jnp.zeros((NUM_EXPERTS, H), dtype=jnp.float32)
        return {'x': x, 'W_router': W_router, 'b_router': b_router, 'W_up': W_up, 'b_up': b_up, 'W_down': W_down, 'b_down': b_down}
    _L1_ffn_all = _L1_ffn_setup()
    _L1_ffn_in = {k: v for k, v in _L1_ffn_all.items() if k in ('W_router', 'b_router', 'W_up', 'b_up', 'W_down', 'b_down', )}
    del _L1_ffn_all

    return {
        "x": x,
        "L0_conv_ln_w": _L0_conv_in["ln_w"],
        "L0_conv_ln_b": _L0_conv_in["ln_b"],
        "L0_conv_in_proj_w": _L0_conv_in["in_proj_w"],
        "L0_conv_conv1d_w": _L0_conv_in["conv1d_w"],
        "L0_conv_conv1d_b": _L0_conv_in["conv1d_b"],
        "L0_conv_dt_bias": _L0_conv_in["dt_bias"],
        "L0_conv_A_log": _L0_conv_in["A_log"],
        "L0_conv_D": _L0_conv_in["D"],
        "L0_conv_rms_w": _L0_conv_in["rms_w"],
        "L0_conv_out_proj_w": _L0_conv_in["out_proj_w"],
        "L0_conv_conv2d_w": _L0_conv_in["conv2d_w"],
        "L0_conv_conv2d_b": _L0_conv_in["conv2d_b"],
        "L0_conv_bn_g": _L0_conv_in["bn_g"],
        "L0_conv_bn_b": _L0_conv_in["bn_b"],
        "L0_conv_bn_mean": _L0_conv_in["bn_mean"],
        "L0_conv_bn_var": _L0_conv_in["bn_var"],
        "L1_attn_g": _L1_attn_in["g"],
        "L1_attn_wq": _L1_attn_in["wq"],
        "L1_attn_wk": _L1_attn_in["wk"],
        "L1_attn_wv": _L1_attn_in["wv"],
        "L1_attn_wo": _L1_attn_in["wo"],
        "L1_ffn_W_router": _L1_ffn_in["W_router"],
        "L1_ffn_b_router": _L1_ffn_in["b_router"],
        "L1_ffn_W_up": _L1_ffn_in["W_up"],
        "L1_ffn_b_up": _L1_ffn_in["b_up"],
        "L1_ffn_W_down": _L1_ffn_in["W_down"],
        "L1_ffn_b_down": _L1_ffn_in["b_down"],
    }

def reference(x, L0_conv_ln_w, L0_conv_ln_b, L0_conv_in_proj_w, L0_conv_conv1d_w, L0_conv_conv1d_b, L0_conv_dt_bias, L0_conv_A_log, L0_conv_D, L0_conv_rms_w, L0_conv_out_proj_w, L0_conv_conv2d_w, L0_conv_conv2d_b, L0_conv_bn_g, L0_conv_bn_b, L0_conv_bn_mean, L0_conv_bn_var, L1_attn_g, L1_attn_wq, L1_attn_wk, L1_attn_wv, L1_attn_wo, L1_ffn_W_router, L1_ffn_b_router, L1_ffn_W_up, L1_ffn_b_up, L1_ffn_W_down, L1_ffn_b_down):
    import jax
    import jax.numpy as jnp
    def _L0_conv_ref(x, ln_w, ln_b, in_proj_w, conv1d_w, conv1d_b, dt_bias, A_log, D, rms_w, out_proj_w, conv2d_w, conv2d_b, bn_g, bn_b, bn_mean, bn_var):
        import jax, jax.numpy as jnp
        import numpy as np
        from jax import lax
        B = 8
        C_IN = 512
        C_OUT = 512
        H = 32
        W = 32
        L = H * W
        D_STATE = 64
        D_CONV = 4
        EXPAND = 2
        HEADDIM = 64
        D_INNER = EXPAND * C_IN
        NHEADS = D_INNER // HEADDIM
        D_XBC = D_INNER + 2 * D_STATE
        D_IN_PROJ = 2 * D_INNER + 2 * D_STATE + NHEADS
        EPS = 1e-05
        Bb, C, Hh, Ww = x.shape
        Ltok = Hh * Ww
        t = x.reshape(Bb, C, Ltok).transpose(0, 2, 1)
        mu = jnp.mean(t, -1, keepdims=True)
        var = jnp.mean(jnp.square(t - mu), -1, keepdims=True)
        xn = (t - mu) * lax.rsqrt(var + EPS) * ln_w + ln_b
        zxbcdt = jnp.einsum('blc,dc->bld', xn, in_proj_w)
        z = zxbcdt[..., :D_INNER]
        xBC = zxbcdt[..., D_INNER:D_INNER + D_XBC]
        dt = zxbcdt[..., D_INNER + D_XBC:]
        conv = lax.conv_general_dilated(xBC.transpose(0, 2, 1), conv1d_w[:, None, :], window_strides=(1,), padding=[(D_CONV - 1, 0)], feature_group_count=D_XBC)
        xBC = jax.nn.silu(conv.transpose(0, 2, 1) + conv1d_b)
        xh = xBC[..., :D_INNER].reshape(Bb, Ltok, NHEADS, HEADDIM)
        Bm = xBC[..., D_INNER:D_INNER + D_STATE]
        Cm = xBC[..., D_INNER + D_STATE:]
        dt = jax.nn.softplus(dt + dt_bias)
        A = -jnp.exp(A_log)

        def step(h, inp):
            xt, dtt, Bt, Ct = inp
            dA = jnp.exp(dtt * A)
            h = h * dA[..., None, None] + jnp.einsum('bh,bhp,bs->bhps', dtt, xt, Bt)
            y = jnp.einsum('bhps,bs->bhp', h, Ct)
            return (h, y)
        h0 = jnp.zeros((Bb, NHEADS, HEADDIM, D_STATE), x.dtype)
        xs = (xh.transpose(1, 0, 2, 3), dt.transpose(1, 0, 2), Bm.transpose(1, 0, 2), Cm.transpose(1, 0, 2))
        _, ys = lax.scan(step, h0, xs)
        y = ys.transpose(1, 0, 2, 3) + D[None, None, :, None] * xh
        y = y.reshape(Bb, Ltok, D_INNER)
        y = y * jax.nn.silu(z)
        y = y * lax.rsqrt(jnp.mean(y * y, -1, keepdims=True) + EPS) * rms_w
        out = jnp.einsum('bld,cd->blc', y, out_proj_w)
        img = out.transpose(0, 2, 1).reshape(Bb, C, Hh, Ww)
        c = jnp.einsum('bchw,oc->bohw', img, conv2d_w) + conv2d_b[None, :, None, None]
        c = (c - bn_mean[None, :, None, None]) * lax.rsqrt(bn_var + EPS)[None, :, None, None]
        c = c * bn_g[None, :, None, None] + bn_b[None, :, None, None]
        return jax.nn.relu(c)

    def _L1_attn_ref(x, g, wq, wk, wv, wo):
        import jax, jax.numpy as jnp
        import numpy as np
        import math
        DIM = 512
        N_HEADS = 8
        N_KV_HEADS = 4
        HEAD_DIM = DIM // N_HEADS
        N_REP = N_HEADS // N_KV_HEADS

        def _rmsnorm(x, g, eps=1e-06):
            var = jnp.mean(jnp.square(x), axis=-1, keepdims=True)
            return x * jax.lax.rsqrt(var + eps) * g

        def _phi(x):
            return jnp.maximum(jax.nn.elu(x), -0.99) + 1.0
        B, S, _ = x.shape
        h = _rmsnorm(x, g)
        scale = 1.0 / math.sqrt(HEAD_DIM)
        q = (h @ wq.T).reshape(B, S, N_HEADS, HEAD_DIM) * scale
        k = (h @ wk.T).reshape(B, S, N_KV_HEADS, HEAD_DIM) * scale
        v = (h @ wv.T).reshape(B, S, N_KV_HEADS, HEAD_DIM)
        k = jnp.repeat(k, N_REP, axis=2)
        v = jnp.repeat(v, N_REP, axis=2)
        q = q.transpose(0, 2, 1, 3)
        k = k.transpose(0, 2, 1, 3)
        v = v.transpose(0, 2, 1, 3)
        Q = _phi(q)
        K = _phi(k)
        KV = jnp.sum(K * v, axis=2)
        K_sum = jnp.sum(K, axis=2)
        Z = jnp.einsum('bhsd,bhd->bhs', Q, K_sum)[..., None]
        Y = Q * KV[:, :, None, :]
        Y = Y / (Z + 1e-06)
        Y = Y.transpose(0, 2, 1, 3).reshape(B, S, N_HEADS * HEAD_DIM)
        return Y @ wo.T

    def _L1_ffn_ref(x, W_router, b_router, W_up, b_up, W_down, b_down):
        import jax, jax.numpy as jnp
        import numpy as np
        NUM_EXPERTS = 32
        GROUP_SIZE = 4
        NUM_GROUPS = NUM_EXPERTS // GROUP_SIZE
        C_CAP = 1.0
        B, S, H = x.shape
        bs = B * S
        E = NUM_EXPERTS
        k = min(int(bs * C_CAP) // E, bs)
        xf = x.reshape(bs, H)
        h = xf @ W_router + b_router
        Sm = jax.nn.softmax(h, axis=-1)
        G_ek, idx_ek = jax.lax.top_k(Sm.T, k)
        tokens = xf[idx_ek]
        D_FF = W_up.shape[-1]
        tok_g = tokens.reshape(NUM_GROUPS, GROUP_SIZE, k, H)
        up = jnp.einsum('gjkh,ghf->gjkf', tok_g, W_up) + b_up[:, None, None, :]
        act = jax.nn.silu(up).reshape(E, k, D_FF)
        Eout = jnp.einsum('ekf,efh->ekh', act, W_down) + b_down[:, None, :]
        weighted = G_ek[..., None] * Eout
        y = jnp.zeros((bs, H), dtype=x.dtype).at[idx_ek.reshape(-1)].add(weighted.reshape(-1, H))
        return y.reshape(B, S, H)

    def _gn(v, G=32, eps=1e-5):
        B_, C_, H_, W_ = v.shape
        g = v.reshape(B_, G, C_ // G, H_, W_)
        m = jnp.mean(g, axis=(2, 3, 4), keepdims=True)
        s = jnp.var(g, axis=(2, 3, 4), keepdims=True)
        return ((g - m) / jnp.sqrt(s + eps)).reshape(v.shape)

    def _ln_c(v, eps=1e-6):
        m = jnp.mean(v, axis=1, keepdims=True)
        s = jnp.var(v, axis=1, keepdims=True)
        return (v - m) / jnp.sqrt(s + eps)

    def _ln_t(v, eps=1e-5):
        m = jnp.mean(v, axis=-1, keepdims=True)
        s = jnp.var(v, axis=-1, keepdims=True)
        return (v - m) / jnp.sqrt(s + eps)

    def _to_tokens(v):
        B_, C_, H_, W_ = v.shape
        return v.reshape(B_, C_, H_ * W_).transpose(0, 2, 1)
    def _from_tokens(t, like):
        B_, C_, H_, W_ = like.shape
        return t.transpose(0, 2, 1).reshape(B_, C_, H_, W_)

    x = x + _L0_conv_ref(_gn(x), L0_conv_ln_w, L0_conv_ln_b, L0_conv_in_proj_w, L0_conv_conv1d_w, L0_conv_conv1d_b, L0_conv_dt_bias, L0_conv_A_log, L0_conv_D, L0_conv_rms_w, L0_conv_out_proj_w, L0_conv_conv2d_w, L0_conv_conv2d_b, L0_conv_bn_g, L0_conv_bn_b, L0_conv_bn_mean, L0_conv_bn_var)
    t = _to_tokens(x)
    t = t + _L1_attn_ref(_ln_t(t), L1_attn_g, L1_attn_wq, L1_attn_wk, L1_attn_wv, L1_attn_wo)
    t = t + _L1_ffn_ref(_ln_t(t), L1_ffn_W_router, L1_ffn_b_router, L1_ffn_W_up, L1_ffn_b_up, L1_ffn_W_down, L1_ffn_b_down)
    x = _from_tokens(t, x)
    return x


_drawn_inputs = setup_inputs


def setup_inputs(seed=0):
    import zlib

    import numpy as np

    out = dict(_drawn_inputs(seed))
    spreads = {'L0_conv_ln_w': (1.0, 0.2),
     'L0_conv_ln_b': (0.0, 0.1),
     'L0_conv_rms_w': (1.0, 0.2),
     'L0_conv_conv2d_b': (0.0, 0.1),
     'L0_conv_bn_g': (1.0, 0.2),
     'L0_conv_bn_b': (0.0, 0.1),
     'L0_conv_bn_mean': (0.0, 0.1),
     'L0_conv_bn_var': (1.0, 0.2),
     'L1_attn_g': (1.0, 0.6),
     'L1_ffn_b_router': (0.0, 0.595),
     'L1_ffn_b_up': (0.0, 0.794),
     'L1_ffn_b_down': (0.0, 0.484)}
    factors = {'L0_conv_dt_bias': 8.0,
     'L0_conv_A_log': 8.0,
     'L1_attn_wq': 8.0,
     'L1_attn_wk': 8.0,
     'L1_attn_wv': 8.0,
     'L1_attn_wo': 8.0}
    for name, (base, spread) in spreads.items():
        noise = np.random.default_rng([zlib.crc32(name.encode()), seed]).standard_normal(out[name].shape)
        drawn = base * np.exp(spread * noise) if base else spread * noise
        out[name] = jnp.asarray(drawn.astype(out[name].dtype))
    for name, factor in factors.items():
        out[name] = (out[name] * factor).astype(out[name].dtype)
    return out
```

```python
import concourse.bass as bass
import numpy as np
from concourse import mybir
from contextlib import ExitStack

F32 = mybir.dt.float32
BF16 = mybir.dt.bfloat16
I32 = mybir.dt.int32
U32 = mybir.dt.uint32
ALU = mybir.AluOpType
ACT = mybir.ActivationFunctionType
AX = mybir.AxisListType

P = 128
NB, C, L = 8, 512, 1024
KC = C // P
DIN, NS, NH, HD = 1024, 64, 16, 64
DXBC = DIN + 2 * NS
BLK = 512
CH = BLK // P
NBLK = NB * L // BLK
NT = NB * L
E, TOPK = 32, 256
GRP, GS = 8, 4
FF = 1365
FT = (FF + P - 1) // P
FR = FF - (FT - 1) * P
ROW = C + E

_CONSTS1 = ("ident", "tri", "ones", "gmat")


class Count:

    def __init__(self, sem, names):
        self.sem, self.names, self.n = sem, list(names), len(names)
        self.at = {x: i for i, x in enumerate(self.names)}
        assert len(self.at) == self.n
        self.next = 0

    def credit(self, engine):
        engine.sem_inc(self.sem, 2 * self.n)

    def inc(self, ins, name):
        assert self.names[self.next % self.n] == name, (self.names[self.next % self.n], name)
        self.next += 1
        ins.then_inc(self.sem, 1)

    def wait(self, engine, t, name, back=0):
        engine.wait_ge(self.sem, (t + (2 - back)) * self.n + self.at[name] + 1)


def settle(engine, spare):
    engine.sem_inc(spare, 1)
def conv_names():
    return range(DXBC // P)


def first_layer(nc, io, consts, keep, debug=None):
    ctx = ExitStack()
    with ctx:
        def sb(name, shape, dt=F32):
            return ctx.enter_context(nc.sbuf_tensor(name, shape, dt))

        def sem(name):
            return ctx.enter_context(nc.semaphore(name))

        ND = DXBC // P
        win = sb("win", [P, KC, 2192])
        wc = sb("wc", [P, DIN // P, C])
        bias_bc = sb("bias_bc", [P, C])
        gnab = sb("gnab", [P, 2, NB, KC])
        lnw = sb("lnw", [P, KC])
        lnb = sb("lnb", [P, KC])
        cw = sb("cw", [P, ND, 4])
        cb = sb("cb", [P, ND])
        abc = sb("abc", [P, CH, NH])
        dtb = sb("dtb", [P, CH, NH])
        dbc = sb("dbc", [P, NH])
        nhalf = sb("nhalf", [P, 1])
        sel = sb("sel", [48, NH * P], BF16)
        identb = sb("identb", [P, P], BF16)
        ident, tri, ones, gmat = consts["ident"], consts["tri"], consts["ones"], consts["gmat"]

        spare = [sem(f"spare{i}") for i in range(3)]
        with ExitStack() as c0:
            def sb0(name, shape, dt=F32):
                return c0.enter_context(nc.sbuf_tensor(name, shape, dt))
            wo_nat = sb0("wo_nat", [P, KC, DIN])
            w2t = sb0("w2t", [P, KC, C])
            bn = sb0("bn", [P, 5, C])
            rmsw = sb0("rmsw", [P, DIN // P])
            selp = sb0("selp", [48, NH * P])
            gx = sb0("gx", [P, 2, KC, L])
            gst = sb0("gst", [P, KC, 2, 6])
            cmv = sb0("cmv", [P, NB, KC, 2])
            cmv1 = sb0("cmv1", [P, KC, 2])
            gsm = sb0("gsm", [P, 4, NB * KC])
            gps = [c0.enter_context(nc.psum_tensor(f"gps{i}", [P, 512], F32)) for i in range(8)]
            w_in, gx_in, gx_in1 = (c0.enter_context(nc.semaphore(s)) for s in ("w_in", "gx_in0", "gx_in1"))
            gx_ins = [gx_in, gx_in1]
            gx_used = c0.enter_context(nc.semaphore("gx_used"))
            st_done = c0.enter_context(nc.semaphore("st_done"))
            d_s, a_s, p_s, t_s = (c0.enter_context(nc.semaphore(s)) for s in ("setup_dve", "setup_act", "setup_pool", "setup_pe"))
            with nc.Block() as block:
                loads = [
                    (win[:, :, :], io["win_t"].rearrange("(k p) d -> p k d", p=P)),
                    (wo_nat[:, :, :], io["wo"].rearrange("(k p) d -> p k d", p=P)),
                    (w2t[:, :, :], io["w2_t"].rearrange("(k p) d -> p k d", p=P)),
                    (rmsw[:, :], io["rms_w"]), (lnw[:, :], io["ln_w"]), (lnb[:, :], io["ln_b"]),
                    (cw[:, :, :], io["conv_w"]), (cb[:, :], io["conv_b"]),
                    (selp[:, :], io["selp"]),
                    (dbc[:, :], io["D"].partition_broadcast(P)),
                ]
                loads += [(bn[:, i, :], io[k].partition_broadcast(P)) for i, k in enumerate(("bn_g", "bn_b", "bn_mean", "bn_var", "c2b"))]
                loads += [(abc[:, c, :], io["A_log"].partition_broadcast(P)) for c in range(CH)]
                loads += [(dtb[:, c, :], io["dt_bias"].partition_broadcast(P)) for c in range(CH)]
                loads += [(consts[k][:, :], io["c_" + k]) for k in consts]

                @block.sync
                def _(sp):
                    with sp.Fori(0, NB // 2) as h:
                        for q in range(2):
                            sp.wait_ge(gx_used, 2 * h + q + 1)
                            sp.dma_start(gx[:, q], io["x_ch"][bass.ds(2 * h + q, 1)].rearrange("b (k p) n -> p (b k) n", p=P)).then_inc(gx_ins[q], 16)

                @block.gpsimd
                def _(pool):
                    for dst, src in loads:
                        pool.dma_start(dst, src).then_inc(w_in, 16)
                    nc.gpsimd.memset(nhalf[:, :], -0.5).then_inc(p_s, 1)
                    pool.wait_ge(w_in, 16 * len(loads))
                    pool.wait_ge(p_s, 1)
                    nc.gpsimd.tensor_scalar(bn[:, 3, :], bn[:, 3, :], 1e-5, None, ALU.add).then_inc(p_s, 1)
                    pool.wait_ge(p_s, 2)
                    nc.gpsimd.tensor_tensor(bn[:, 3, :], bn[:, 3, :], nhalf[:, 0:1].to_broadcast([P, C]), ALU.pow).then_inc(p_s, 1)
                    pool.wait_ge(d_s, 5)
                    nc.gpsimd.tensor_scalar(gsm[:, 1, :], gsm[:, 1, :], 1e-5, None, ALU.add).then_inc(p_s, 1)
                    pool.wait_ge(p_s, 4)
                    nc.gpsimd.tensor_tensor(gnab[:, 0].rearrange("p b k -> p (b k)"), gsm[:, 1, :],
                                            nhalf[:, 0:1].to_broadcast([P, NB * KC]), ALU.pow).then_inc(p_s, 1)

                @block.scalar
                def _(act):
                    act.wait_ge(w_in, 16 * len(loads))
                    nc.scalar.activation(abc[:, :, :], abc[:, :, :], ACT.Exp).then_inc(a_s, 1)
                    nc.scalar.mul(win[:, :, 0:DIN], win[:, :, 0:DIN], 0.5).then_inc(a_s, 1)
                    nc.scalar.mul(cw[:, :, :], cw[:, :, :], 0.5).then_inc(a_s, 1)
                    nc.scalar.mul(cb[:, :], cb[:, :], 0.5).then_inc(a_s, 1)
                    nc.scalar.copy(sel[:, :], selp[:, :]).then_inc(a_s, 1)
                    nc.scalar.copy(identb[:, :], ident[:, :]).then_inc(a_s, 1)

                @block.tensor
                def _(pe):
                    pe.wait_ge(w_in, 16 * len(loads))
                    for dk in range(DIN // P):
                        for k in range(KC):
                            mm = nc.tensor.matmul(gps[dk][:, :], wo_nat[:, k, dk * P:(dk + 1) * P], w2t[:, k, :], start=(k == 0), stop=(k == KC - 1))
                        mm.then_inc(t_s, 1)
                    pe.wait_ge(d_s, 2)
                    nc.tensor.matmul(gps[0][:, 0:NB * KC], gmat[:, :], gsm[:, 0, :], start=True, stop=True).then_inc(t_s, 1)
                    pe.wait_ge(d_s, 4)
                    nc.tensor.matmul(gps[1][:, 0:NB * KC], gmat[:, :], gsm[:, 3, :], start=True, stop=True).then_inc(t_s, 1)

                @block.vector
                def _(v):
                    v.sem_inc(gx_used, 2)
                    v.sem_inc(st_done, 2)
                    with v.Fori(0, NB // 2) as h:
                        for q in range(2):
                            v.wait_ge(gx_ins[q], 16 * (h + 1))
                            v.wait_ge(st_done, 2 * (2 * h + q) + 2)
                            for k in range(KC):
                                for j in range(2):
                                    ins = nc.vector.bn_stats(gst[:, k, j, :], gx[:, q, k, j * 512:(j + 1) * 512])
                            ins.then_inc(gx_used, 1)
                            v.wait_ge(gx_used, 2 * h + q + 3)
                            settle(v, spare[0])
                            for k in range(KC):
                                ins = nc.vector.bn_aggr(cmv1[:, k, :], gst[:, k].rearrange("p j s -> p (j s)"))
                            ins.then_inc(st_done, 1)
                            v.wait_ge(st_done, 2 * (2 * h + q) + 3)
                            nc.vector.tensor_copy(cmv[:, bass.ds(2 * h + q, 1)].rearrange("p b k t -> p (b k t)"), cmv1[:, :, :].rearrange("p k t -> p (k t)")).then_inc(st_done, 1)
                    v.wait_ge(p_s, 3)
                    v.wait_ge(st_done, 2 * NB + 2)
                    v.wait_ge(a_s, 6)
                    nc.vector.tensor_tensor(bn[:, 3, :], bn[:, 3, :], bn[:, 0, :], ALU.mult).then_inc(d_s, 1)
                    v.wait_ge(d_s, 1)
                    for dk in range(DIN // P):
                        v.wait_ge(t_s, dk + 1)
                        nc.vector.scalar_tensor_tensor(wc[:, dk, :], gps[dk][:, :], rmsw[:, dk:dk + 1], bn[:, 3, :], ALU.mult, ALU.mult)
                    nc.vector.tensor_copy(gsm[:, 0, :], cmv[:, :, :, 0].rearrange("p b k -> p (b k)")).then_inc(d_s, 1)
                    v.wait_ge(t_s, 9)
                    nc.vector.tensor_copy(gsm[:, 2, :], gps[0][:, 0:NB * KC]).then_inc(d_s, 1)
                    v.wait_ge(d_s, 3)
                    nc.vector.tensor_tensor(gsm[:, 3, :], gsm[:, 0, :], gsm[:, 2, :], ALU.subtract).then_inc(st_done, 1)
                    v.wait_ge(st_done, 2 * NB + 3)
                    nc.vector.tensor_tensor(gsm[:, 3, :], gsm[:, 3, :], gsm[:, 3, :], ALU.mult).then_inc(st_done, 1)
                    v.wait_ge(st_done, 2 * NB + 4)
                    nc.vector.tensor_tensor(gsm[:, 3, :], gsm[:, 3, :], cmv[:, :, :, 1].rearrange("p b k -> p (b k)"), ALU.add).then_inc(d_s, 1)
                    v.wait_ge(t_s, 10)
                    nc.vector.tensor_copy(gsm[:, 1, :], gps[1][:, 0:NB * KC]).then_inc(d_s, 1)
                    v.wait_ge(p_s, 5)
                    nc.vector.scalar_tensor_tensor(gnab[:, 1].rearrange("p b k -> p (b k)"), gsm[:, 2, :], -1.0,
                                                   gnab[:, 0].rearrange("p b k -> p (b k)"), ALU.mult, ALU.mult).then_inc(d_s, 1)
                    nc.vector.tensor_scalar(abc[:, :, :], abc[:, :, :], -1.0, None, ALU.mult)
                    nc.vector.tensor_tensor(bias_bc[:, :], bn[:, 4, :], bn[:, 2, :], ALU.subtract).then_inc(d_s, 1)
                    v.wait_ge(d_s, 7)
                    nc.vector.tensor_tensor(bias_bc[:, :], bias_bc[:, :], bn[:, 3, :], ALU.mult).then_inc(d_s, 1)
                    v.wait_ge(d_s, 8)
                    nc.vector.tensor_tensor(bias_bc[:, :], bias_bc[:, :], bn[:, 1, :], ALU.add).then_inc(d_s, 1)

        xc = sb("xc", [P, KC, BLK])
        tn = sb("tn", [P, CH, C])
        xn = sb("xn", [P, 2, KC, BLK])
        raw = sb("raw", [P, ND, 3 + BLK])
        cv = sb("cv", [P, 2, BLK])
        tha = sb("tha", [P, BLK])
        xs = sb("xs", [P, 2, ND - 1, BLK])
        bcm = sb("bcm", [NS, 2, 2, BLK])
        lst = sb("lst", [P, 6])
        lmv = sb("lmv", [P, CH, 2])
        lrs = sb("lrs", [P, CH, 2])
        dtu = sb("dtu", [P, 2, CH * NH])
        sm = sb("sm", [P, 9, CH * NH])
        smb = sb("smb", [P, 2, 4, CH * NH])
        sp3 = sb("sp3", [P, CH, 3 * NH], BF16)
        csT = sb("csT", [48, 2, CH * P], BF16)
        csN = sb("csN", [48, 2, CH * P], BF16)
        th = sb("th", [P, DIN])
        zs = sb("zs", [P, DIN])
        xdt = sb("xdt", [P, DIN])
        xw = th
        dx = sb("dx", [P, DIN])
        yo = sb("yo", [P, DIN])
        gm = sb("gm", [P, P])
        bt = sb("bt", [P, NS])
        es = sb("es", [P, 2, 4 * P])
        ms = sb("ms", [P, 2, 4 * P])
        st = sb("st", [NS, DIN])
        yT = sb("yT", [P, DIN // P, P])
        rr = sb("rr", [P, 4])
        o1 = sb("o1", [P, C])
        xres = sb("xres", [P, 2, C])
        junk = sb("junk", [P, 1])
        psA = [ctx.enter_context(nc.psum_tensor(f"psA{i}", [P, 512], F32)) for i in range(2)]
        psArg = ctx.enter_context(nc.psum_tensor("psArg", [P, 512], F32))
        psM = ctx.enter_context(nc.psum_tensor("psM", [P, 512], F32))
        psY = ctx.enter_context(nc.psum_tensor("psY", [P, DIN], F32))
        psX = ctx.enter_context(nc.psum_tensor("psX", [P, DIN], F32))
        psMb = psM[:, :].bitcast(BF16)
        DA, CSB, WD, E1, D2, SS, QQ, PP, MX = range(9)
        R1, R2 = MX, SS
        DTV, ECS, WEND, ETOT = range(4)

        U = 18
        peA = Count(sem("pe_a"), [f"u{n}" for n in range(U)])
        dveA = Count(sem("dve_a"), ["halo", "gn"] + ["st0", "mv0", "st1", "mv1", "tn0", "st2", "mv2", "tn1", "st3", "mv3", "tn2", "tn3", "dtu"]
                     + sum(([f"ca{d}", f"cb{d}", f"cc{d}"] + ([f"xs{d-1}"] if d else []) for d in range(ND)), []) + ["xsB", "xsC"])
        actA = Count(sem("act_a"), [f"xn{k}" for k in range(KC)] + sum(([f"raw{d}", f"cv{d}"] + ([f"th{d-1}"] if d else []) for d in range(ND)), []) + [f"th{ND-1}"])
        poolA = Count(sem("pool_a"), sum(([f"ve{c}", f"r{c}"] for c in range(CH)), []))
        stepsP = ["p1", "p2", "p3", "p4"]
        stepsB = []
        for c in range(CH):
            stepsB += [(f"s{i}", c) for i in range(1, 7)] + [("s0", c + 1)] * (c + 1 < CH) + [("s7", c), ("s8", c)]

        def names(**per):
            return [f"{x}_{c}" for s, c in stepsB for x in per.get(s, "").split()]
        peP = Count(sem("pe_p"), ["cs", "tr3", "z"])
        dveP = Count(sem("dve_p"), "mx d2 rc s q p15 p13 p11 p9 p7 p5 p3 p1 dt da csb w hi r1 mid r2 lo csT csN zs".split())
        actP = Count(sem("act_p"), "abs e etot ecs wend th".split())
        poolP = Count(sem("pool_p"), ["s0"])
        peB = Count(sem("pe_b"), names(s0="z", s1="a0 xt", s2="gb a1", s3="yoff a2", s4="yd0 a3", s5="yd1 yd2 st yd3", s7="yT", s8="out"))
        dveB = Count(sem("dve_b"), names(s0="zs", s1="xdt dx", s2="gm bt m0", s3="yo m1", s4="m2", s5="m3 s y1", s8="o1 o2"))
        actB = Count(sem("act_b"), names(s0="th", s1="n0 e0", s2="n1 e1", s3="n2 e2", s4="n3 e3", s6="sq", s7="yT"))
        poolB = Count(sem("pool_b"), names(s3="xw", s4="sdec t2", s6="yg", s7="ve r"))
        xc_in = sem("xc_in")
        xres_in = [sem(f"xres_in{i}") for i in range(2)]
        t1_out = [sem(f"t1_out{i}") for i in range(2)]

        after = {("s1", 0): [0], ("s2", 0): [1], ("s3", 0): [2], ("s4", 0): [3], ("s7", 0): [4, 5],
                 ("s1", 1): [6], ("s2", 1): [7], ("s4", 1): [8], ("s7", 1): [9],
                 ("s1", 2): [10], ("s2", 2): [11], ("s4", 2): [12], ("s6", 2): ["p1"], ("s7", 2): [13],
                 ("s1", 3): [14], ("s4", 3): [15], ("s5", 3): ["p2", 16], ("s6", 3): ["p3", 17, 18, "p4"]}

        def walk(engine, stage_a, stage_p, stage_b, before=None):
            if before:
                before()
            for n in range(U + 1):
                stage_a(0, 0, n)
            for s in stepsP:
                stage_p(0, 0, s)

            def step(t, p, last):
                for s, c in stepsB:
                    stage_b(t, p, s, c)
                    for x in [] if last else after.get((s, c), []):
                        stage_p(t + 1, 1 - p, x) if x in stepsP else stage_a(t + 1, 1 - p, x)
            with engine.Fori(0, NB - 1) as b:
                step(b * 2, 0, False)
                step(b * 2 + 1, 1, False)
            step(NBLK - 2, 0, False)
            step(NBLK - 1, 1, True)

        x_ch, x_tok, t1 = io["x_ch"], io["x_tok"], io["t1"]

        def half(t, p):
            return (t - p) // 2 if isinstance(t, int) else (t - p) // 2

        with nc.Block() as block:
            @block.sync
            def _(sp):
                def load_x(t, p):
                    sp.dma_start(xc[:, :, :], x_ch[bass.ds(half(t, p), 1), :, p * BLK:(p + 1) * BLK].rearrange("b (k p) n -> p (b k) n", p=P)).then_inc(xc_in, 16)

                def before():
                    load_x(0, 0)
                    for i in range(2):
                        sp.dma_start(xres[:, i], x_tok[i]).then_inc(t1_out[i], 16)

                def load_res(t, c):
                    sp.wait_ge(t1_out[c % 2], (t * 2 + c // 2 + 1) * 16)
                    sp.dma_start(xres[:, c % 2], x_tok[bass.ds(t * CH + c, 1)].rearrange("a p n -> p (a n)")).then_inc(xres_in[c % 2], 16)

                def stage_p(t, p, s):
                    if s == "p1" and not (isinstance(t, int) and t + 1 >= NBLK):
                        peA.wait(sp, t, "u3")
                        load_x(t + 1, 1 - p)
                    if s == "p4":
                        load_res(t, 0)

                def stage_b(t, p, s, c):
                    if s == "s0":
                        load_res(t, c)
                    if s == "s8":
                        dveB.wait(sp, t, f"o2_{c}")
                        sp.dma_start(t1[bass.ds(t * CH + c, 1)].rearrange("a p n -> p (a n)"), xres[:, c % 2]).then_inc(t1_out[c % 2], 16)

                walk(sp, lambda t, p, n: None, stage_p, stage_b, before)
                for i in range(2):
                    sp.wait_ge(t1_out[i], 16 * (NBLK * CH // 2 + 1))

            @block.gpsimd
            def _(pool):
                for x in (poolA, poolP, poolB):
                    x.credit(pool)

                def stage_a(t, p, n):
                    if n < CH:
                        dveA.wait(pool, t, f"mv{n}")
                        if n == 0:
                            dveA.wait(pool, t, "tn3", 1)
                        settle(pool, spare[1])
                        poolA.inc(nc.gpsimd.tensor_scalar(lrs[:, n, 0:1], lmv[:, n, 1:2], 1e-5, None, ALU.add), f"ve{n}")
                        poolA.wait(pool, t, f"ve{n}")
                        poolA.inc(nc.gpsimd.tensor_tensor(lrs[:, n, 1:2], lrs[:, n, 0:1], nhalf[:, :], ALU.pow), f"r{n}")

                def stage_p(t, p, s):
                    if s == "p4":
                        if p == 0:
                            dveB.wait(pool, t, f"s_{CH-1}", 1)
                            peB.wait(pool, t, f"yoff_{CH-1}", 1)
                            settle(pool, spare[1])
                            poolP.inc(nc.gpsimd.memset(st[:, :], 0.0), "s0")
                        else:
                            poolP.inc(nc.gpsimd.memset(junk[:, :], 0.0), "s0")

                def stage_b(t, p, s, c):
                    if s == "s3":
                        actP.wait(pool, t, "wend")
                        dveB.wait(pool, t, f"xdt_{c}")
                        peB.wait(pool, t, f"st_{c-1}") if c else peB.wait(pool, t, f"st_{CH-1}", 1)
                        w = smb[:, p, WEND, c * NH:(c + 1) * NH].unsqueeze(2).to_broadcast([P, NH, HD])
                        poolB.inc(nc.gpsimd.tensor_tensor(xw[:, :].rearrange("p (h d) -> p h d", h=NH), xdt[:, :].rearrange("p (h d) -> p h d", h=NH), w, ALU.mult), f"xw_{c}")
                    if s == "s4":
                        peB.wait(pool, t, f"yoff_{c}")
                        if c:
                            dveB.wait(pool, t, f"s_{c-1}")
                        elif p == 0:
                            poolP.wait(pool, t, "s0")
                        else:
                            dveB.wait(pool, t, f"s_{CH-1}", 1)
                        e = smb[0:NS, p, ETOT, c * NH:(c + 1) * NH].unsqueeze(2).to_broadcast([NS, NH, HD])
                        poolB.inc(nc.gpsimd.tensor_tensor(st[:, :].rearrange("p (h d) -> p h d", h=NH), st[:, :].rearrange("p (h d) -> p h d", h=NH), e, ALU.mult), f"sdec_{c}")
                        dveB.wait(pool, t, f"yo_{c}")
                        poolB.inc(nc.gpsimd.tensor_tensor(yo[:, :], yo[:, :], dx[:, :], ALU.add), f"t2_{c}")
                    if s == "s6":
                        dveB.wait(pool, t, f"y1_{c}")
                        poolB.inc(nc.gpsimd.tensor_tensor(yo[:, :], yo[:, :], zs[:, :], ALU.mult), f"yg_{c}")
                    if s == "s7":
                        actB.wait(pool, t, f"sq_{c}")
                        settle(pool, spare[1])
                        poolB.inc(nc.gpsimd.tensor_scalar(rr[:, 1:2], rr[:, 0:1], 1.0 / DIN, 1e-5, ALU.mult, ALU.add), f"ve_{c}")
                        poolB.wait(pool, t, f"ve_{c}")
                        dveB.wait(pool, t, f"o1_{c-1}") if c else dveB.wait(pool, t, f"o1_{CH-1}", 1)
                        poolB.inc(nc.gpsimd.tensor_tensor(rr[:, 2:3], rr[:, 1:2], nhalf[:, :], ALU.pow), f"r_{c}")

                walk(pool, stage_a, stage_p, stage_b)

            @block.tensor
            def _(pe):
                for x in (peA, peP, peB):
                    x.credit(pe)

                def free_a(t, n):
                    m, back = (n - 2, 0) if n >= 2 else (n - 2 + U, 1)
                    if m < CH:
                        dveA.wait(pe, t, f"tn{m}", back)
                    elif m < 2 * CH:
                        actA.wait(pe, t, f"xn{m - CH}", back)
                    elif m == 2 * CH:
                        dveA.wait(pe, t, "dtu", back)
                    else:
                        actA.wait(pe, t, f"cv{m - 2 * CH - 1}", back)

                def stage_a(t, p, n):
                    if n == U:
                        return
                    bank = psA[n % 2]
                    free_a(t, n)
                    if n < CH:
                        if n == 0:
                            dveA.wait(pe, t, "gn")
                        for k in range(KC):
                            mm = nc.tensor.transpose(bank[:, k * P:(k + 1) * P], xc[:, k, n * P:(n + 1) * P], ident[:, :])
                    elif n < 2 * CH:
                        k = n - CH
                        if k == 0:
                            dveA.wait(pe, t, "tn3")
                        for c in range(CH):
                            mm = nc.tensor.transpose(bank[:, c * P:(c + 1) * P], tn[:, c, k * P:(k + 1) * P], ident[:, :])
                    elif n > 2 * CH:
                        d = n - 2 * CH - 1
                        for k in range(KC):
                            mm = nc.tensor.matmul(bank[:, :], win[:, k, DIN + d * P:DIN + (d + 1) * P], xn[:, p, k, :], start=(k == 0), stop=(k == KC - 1))
                    else:
                        actA.wait(pe, t, f"xn{KC-1}")
                        for c in range(CH):
                            for k in range(KC):
                                mm = nc.tensor.matmul(bank[:, c * NH:(c + 1) * NH], xn[:, p, k, c * P:(c + 1) * P], win[:, k, DIN + DXBC:],
                                                      start=(k == 0), stop=(k == KC - 1))
                    peA.inc(mm, f"u{n}")

                def args(t, p, c, g):
                    j, i = csN[:, p, c * P:(c + 1) * P], csT[:, p, c * P:(c + 1) * P]
                    nc.tensor.matmul(psArg[:, :], j, sel[:, g * 512:(g + 1) * 512], start=True, stop=False, skip_group_check=True)
                    for h in range(4):
                        mm = nc.tensor.matmul(psArg[:, h * P:(h + 1) * P], sel[:, (4 * g + h) * P:(4 * g + h + 1) * P], i, start=False, stop=True, skip_group_check=True)
                    peB.inc(mm, f"a{g}_{c}")

                def ydiag(t, c, g):
                    dveB.wait(pe, t, f"m{g}_{c}")
                    if g == 0:
                        actB.wait(pe, t, f"yT_{c-1}") if c else actB.wait(pe, t, f"yT_{CH-1}", 1)
                    for h in range(4):
                        hh = 4 * g + h
                        mm = nc.tensor.matmul(psY[:, hh * HD:(hh + 1) * HD], ms[:, g % 2, h * P:(h + 1) * P], xdt[:, hh * HD:(hh + 1) * HD], start=True, stop=True)
                    peB.inc(mm, f"yd{g}_{c}")

                def z_of(t, p, c):
                    for j in range(2):
                        for k in range(KC):
                            mm = nc.tensor.matmul(psX[:, j * 512:(j + 1) * 512], xn[:, p, k, c * P:(c + 1) * P], win[:, k, j * 512:(j + 1) * 512], start=(k == 0), stop=(k == KC - 1))
                    return mm

                def stage_p(t, p, s):
                    if s == "p2":
                        dveP.wait(pe, t, "da")
                        dveB.wait(pe, t, f"m0_{CH-1}", 1)
                        nc.tensor.matmul(psM[:, 0:64], tri[:, :], sm[:, DA, :], start=True, stop=True)
                        mm = nc.tensor.matmul(psM[:, 64:128], ones[:, :], sm[:, DA, :], start=True, stop=True)
                        peP.inc(mm, "cs")
                    if s == "p3":
                        dveP.wait(pe, t, "lo")
                        actP.wait(pe, t, "etot")
                        settle(pe, spare[2])
                        for q in range(CH):
                            mm = nc.tensor.transpose(psMb[0:48, q * P:(q + 1) * P], sp3[:, q, :], identb[:, :])
                        peP.inc(mm, "tr3")
                    if s == "p4":
                        dveP.wait(pe, t, "csN")
                        dveB.wait(pe, t, f"s_{CH-1}", 1)
                        peP.inc(z_of(t, p, 0), "z")

                def stage_b(t, p, s, c):
                    tok = slice(c * P, (c + 1) * P)
                    Bc, Cc = bcm[:, p, 0, tok], bcm[:, p, 1, tok]
                    if s == "s0":
                        dveB.wait(pe, t, f"s_{c-1}")
                        peB.inc(z_of(t, p, c), f"z_{c}")
                    if s == "s1":
                        if c == 0:
                            dveA.wait(pe, t, "xsC")
                        actB.wait(pe, t, f"n3_{c-1}") if c else actB.wait(pe, t, f"n3_{CH-1}", 1)
                        args(t, p, c, 0)
                        dveB.wait(pe, t, f"zs_{c}") if c else dveP.wait(pe, t, "zs")
                        for d in range(DIN // P):
                            mm = nc.tensor.transpose(psX[:, d * P:(d + 1) * P], xs[:, p, d, tok], ident[:, :])
                        peB.inc(mm, f"xt_{c}")
                    if s == "s2":
                        dveB.wait(pe, t, f"o1_{c-1}") if c else dveB.wait(pe, t, f"o1_{CH-1}", 1)
                        nc.tensor.matmul(psM[:, 0:P], Bc, Cc, start=True, stop=True)
                        peB.inc(nc.tensor.transpose(psM[:, P:P + NS], Bc, ident[0:NS, 0:NS]), f"gb_{c}")
                        actB.wait(pe, t, f"n0_{c}")
                        args(t, p, c, 1)
                    if s == "s3":
                        dveB.wait(pe, t, f"dx_{c}")
                        if c:
                            dveB.wait(pe, t, f"s_{c-1}")
                        elif p == 0:
                            poolP.wait(pe, t, "s0")
                        else:
                            dveB.wait(pe, t, f"s_{CH-1}", 1)
                        for j in range(2):
                            mm = nc.tensor.matmul(psX[:, j * 512:(j + 1) * 512], Cc, st[:, j * 512:(j + 1) * 512], start=True, stop=True)
                        peB.inc(mm, f"yoff_{c}")
                        actB.wait(pe, t, f"n1_{c}")
                        args(t, p, c, 2)
                    if s == "s4":
                        ydiag(t, c, 0)
                        actB.wait(pe, t, f"n2_{c}")
                        args(t, p, c, 3)
                    if s == "s5":
                        ydiag(t, c, 1)
                        ydiag(t, c, 2)
                        dveB.wait(pe, t, f"yo_{c}")
                        poolB.wait(pe, t, f"xw_{c}")
                        for j in range(2):
                            mm = nc.tensor.matmul(psX[0:NS, j * 512:(j + 1) * 512], bt[:, :], xw[:, j * 512:(j + 1) * 512], start=True, stop=True)
                        peB.inc(mm, f"st_{c}")
                        ydiag(t, c, 3)
                    if s == "s7":
                        poolB.wait(pe, t, f"yg_{c}")
                        for d in range(DIN // P):
                            mm = nc.tensor.transpose(psY[:, d * P:(d + 1) * P], yo[:, d * P:(d + 1) * P], ident[:, :])
                        peB.inc(mm, f"yT_{c}")
                    if s == "s8":
                        actB.wait(pe, t, f"yT_{c}")
                        for d in range(DIN // P):
                            mm = nc.tensor.matmul(psM[:, :], yT[:, d, :], wc[:, d, :], start=(d == 0), stop=(d == DIN // P - 1))
                        peB.inc(mm, f"out_{c}")

                walk(pe, stage_a, stage_p, stage_b)

            @block.scalar
            def _(act):
                for x in (actA, actP, actB):
                    x.credit(act)

                def tanh_a(t, p, d):
                    dveA.wait(act, t, f"cc{d}")
                    if d == 0:
                        peB.wait(act, t, f"xt_{CH-1}", 2)
                    if d == ND - 1:
                        dveA.wait(act, t, "xsC", 1)
                    out = xs[:, p, d, :] if d < ND - 1 else tha[:, :]
                    actA.inc(nc.scalar.activation(out, cv[:, d % 2], ACT.Tanh), f"th{d}")

                def stage_a(t, p, n):
                    bank = psA[n % 2]
                    if n < CH or n == 2 * CH:
                        return
                    if n < 2 * CH:
                        k = n - CH
                        if k == 0:
                            peB.wait(act, t, f"z_{CH-1}", 2)
                        peA.wait(act, t, f"u{n}")
                        actA.inc(nc.scalar.activation(xn[:, p, k, :], bank[:, :], ACT.Identity, bias=lnb[:, k:k + 1], scale=lnw[:, k:k + 1]), f"xn{k}")
                    elif n < U:
                        d = n - 2 * CH - 1
                        peA.wait(act, t, f"u{n}")
                        dveA.wait(act, t, "halo")
                        actA.inc(nc.scalar.activation(raw[:, d, 3:], bank[:, :], ACT.Identity), f"raw{d}")
                        if d < 2:
                            dveA.wait(act, t, "xsC" if d == 0 else f"xs{ND-2}", 1)
                        else:
                            dveA.wait(act, t, f"xs{d-2}")
                        actA.inc(nc.scalar.activation(cv[:, d % 2], bank[:, :], ACT.Identity, bias=cb[:, d:d + 1], scale=cw[:, d, 3:4]), f"cv{d}")
                        if d:
                            tanh_a(t, p, d - 1)
                    else:
                        tanh_a(t, p, ND - 1)

                def exps(t, c, g):
                    peB.wait(act, t, f"a{g}_{c}")
                    if g >= 2:
                        dveB.wait(act, t, f"m{g-2}_{c}")
                    actB.inc(nc.scalar.activation(es[:, g % 2], psArg[:, :], ACT.Relu, scale=-1.0), f"n{g}_{c}")
                    actB.wait(act, t, f"n{g}_{c}")
                    actB.inc(nc.scalar.activation(es[:, g % 2], es[:, g % 2], ACT.Exp, scale=-1.0), f"e{g}_{c}")

                def stage_p(t, p, s):
                    if s == "p1":
                        dveA.wait(act, t, "dtu")
                        dveP.wait(act, t, "s", 1)
                        actP.inc(nc.scalar.activation(sm[:, E1, :], dtu[:, p], ACT.Abs), "abs")
                        actP.wait(act, t, "abs")
                        actP.inc(nc.scalar.activation(sm[:, E1, :], sm[:, E1, :], ACT.Exp, scale=-1.0), "e")
                    if s == "p2":
                        peP.wait(act, t, "cs")
                        actP.inc(nc.scalar.activation(smb[:, p, ETOT, :], psM[:, 64:128], ACT.Exp), "etot")
                        dveP.wait(act, t, "csb")
                        actP.inc(nc.scalar.activation(smb[:, p, ECS, :], sm[:, CSB, :], ACT.Exp), "ecs")
                        dveP.wait(act, t, "w")
                        actP.inc(nc.scalar.activation(smb[:, p, WEND, :], sm[:, WD, :], ACT.Exp), "wend")
                    if s == "p4":
                        peP.wait(act, t, "z")
                        actB.wait(act, t, f"sq_{CH-1}", 1)
                        actP.inc(nc.scalar.activation(th[:, :], psX[:, :], ACT.Tanh), "th")

                def stage_b(t, p, s, c):
                    if s == "s0":
                        peB.wait(act, t, f"z_{c}")
                        actB.wait(act, t, f"sq_{c-1}")
                        actB.inc(nc.scalar.activation(th[:, :], psX[:, :], ACT.Tanh), f"th_{c}")
                    if s in ("s1", "s2", "s3", "s4"):
                        exps(t, c, int(s[1]) - 1)
                    if s == "s6":
                        poolB.wait(act, t, f"yg_{c}")
                        actB.inc(nc.scalar.activation(th[:, :], yo[:, :], ACT.Square, accum_out=rr[:, 0:1]), f"sq_{c}")
                    if s == "s7":
                        peB.wait(act, t, f"yT_{c}")
                        actB.inc(nc.scalar.activation(yT[:, :, :].rearrange("p a b -> p (a b)"), psY[:, :], ACT.Identity), f"yT_{c}")

                walk(act, stage_a, stage_p, stage_b)

            @block.vector
            def _(v):
                for x in (dveA, dveP, dveB):
                    x.credit(v)

                def norm_tok(t, c):
                    poolA.wait(v, t, f"r{c}")
                    dveA.wait(v, t, f"mv{c}")
                    if c == 0:
                        peA.wait(v, t, f"u{2*CH-1}", 1)
                    dveA.inc(nc.vector.tensor_scalar(tn[:, c, :], psA[c % 2][:, :], lmv[:, c, 0:1], lrs[:, c, 1:2], ALU.subtract, ALU.mult), f"tn{c}")

                def silu_a(t, p, d):
                    actA.wait(v, t, f"th{d}")
                    if d < ND - 1:
                        dveA.inc(nc.vector.scalar_tensor_tensor(xs[:, p, d, :], xs[:, p, d, :], 1.0, cv[:, d % 2], ALU.add, ALU.mult), f"xs{d}")
                    else:
                        peB.wait(v, t, f"yoff_{CH-1}", 2)
                        for j, x in enumerate("BC"):
                            q = slice(j * NS, (j + 1) * NS)
                            dveA.inc(nc.vector.scalar_tensor_tensor(bcm[:, p, j, :], tha[q, :], 1.0, cv[q, d % 2], ALU.add, ALU.mult), f"xs{x}")

                def stage_a(t, p, n):
                    if n < CH:
                        if n == 0:
                            if p == 0:
                                dveA.inc(nc.vector.memset(raw[:, :, 0:3], 0.0), "halo")
                            else:
                                actA.wait(v, t, f"raw{ND-1}", 1)
                                dveA.inc(nc.vector.tensor_copy(raw[:, :, 0:3], raw[:, :, BLK:BLK + 3]), "halo")
                            v.wait_ge(xc_in, t * 16 + 16)
                            for k in range(KC):
                                ins = nc.vector.tensor_scalar(xc[:, k, :], xc[:, k, :], gnab[:, 0, bass.ds(half(t, p), 1), k],
                                                              gnab[:, 1, bass.ds(half(t, p), 1), k], ALU.mult, ALU.add)
                            dveA.inc(ins, "gn")
                        peA.wait(v, t, f"u{n}")
                        if n:
                            dveA.wait(v, t, f"mv{n-1}")
                        dveA.inc(nc.vector.bn_stats(lst[:, :], psA[n % 2][:, :]), f"st{n}")
                        dveA.wait(v, t, f"st{n}")
                        settle(v, spare[0])
                        dveA.inc(nc.vector.bn_aggr(lmv[:, n, :], lst[:, :]), f"mv{n}")
                        if n:
                            norm_tok(t, n - 1)
                    elif n == CH:
                        norm_tok(t, CH - 1)
                    elif n < 2 * CH:
                        pass
                    elif n == 2 * CH:
                        peA.wait(v, t, f"u{n}")
                        actP.wait(v, t, "abs", 2)
                        dveP.wait(v, t, "mx", 2)
                        dveA.inc(nc.vector.tensor_tensor(dtu[:, p], psA[n % 2][:, 0:CH * NH], dtb[:, :, :].rearrange("p c h -> p (c h)"), ALU.add), "dtu")
                    elif n < U:
                        d = n - 2 * CH - 1
                        actA.wait(v, t, f"cv{d}")
                        for j, x in enumerate("abc"):
                            if j:
                                dveA.wait(v, t, f"c{'abc'[j-1]}{d}")
                            dveA.inc(nc.vector.scalar_tensor_tensor(cv[:, d % 2], raw[:, d, j:j + BLK], cw[:, d, j:j + 1], cv[:, d % 2], ALU.mult, ALU.add), f"c{x}{d}")
                        if d:
                            silu_a(t, p, d - 1)
                    else:
                        silu_a(t, p, ND - 1)

                def tt(t, name, out, a, b, op):
                    dveP.inc(nc.vector.tensor_tensor(out, a, b, op), name)
                    dveP.wait(v, t, name)

                def mask(t, c, g):
                    actB.wait(v, t, f"e{g}_{c}")
                    if g >= 2:
                        peB.wait(v, t, f"yd{g-2}_{c}")
                    elif c:
                        peB.wait(v, t, f"yd{g+2}_{c-1}")
                    else:
                        peB.wait(v, t, f"yd{g+2}_{CH-1}", 1)
                    dveB.inc(nc.vector.tensor_tensor(ms[:, g % 2].rearrange("p (h i) -> p h i", h=4), es[:, g % 2].rearrange("p (h i) -> p h i", h=4),
                                                     gm[:, :].unsqueeze(1).to_broadcast([P, 4, P]), ALU.mult), f"m{g}_{c}")

                def heads(x):
                    return x.rearrange("p (h d) -> p h d", h=NH)

                def stage_p(t, p, s):
                    S = lambda i: sm[:, i, :]
                    if s == "p1":
                        dveA.wait(v, t, "dtu")
                        dveP.inc(nc.vector.tensor_scalar(S(MX), dtu[:, p], 0.0, None, ALU.max), "mx")
                        actP.wait(v, t, "e")
                        dveP.inc(nc.vector.tensor_scalar(S(D2), S(E1), 2.0, None, ALU.add), "d2")
                        dveP.wait(v, t, "d2")
                        dveP.inc(nc.vector.reciprocal(S(D2), S(D2)), "rc")
                        dveP.wait(v, t, "rc")
                        tt(t, "s", S(SS), S(E1), S(D2), ALU.mult)
                        tt(t, "q", S(QQ), S(SS), S(SS), ALU.mult)
                        dveP.inc(nc.vector.tensor_scalar(S(PP), S(QQ), 1.0 / 15, None, ALU.mult), "p15")
                        for i in (13, 11, 9, 7, 5, 3):
                            dveP.wait(v, t, f"p{i+2}")
                            dveP.inc(nc.vector.scalar_tensor_tensor(S(PP), S(PP), 1.0 / i, S(QQ), ALU.add, ALU.mult), f"p{i}")
                        dveP.wait(v, t, "p3")
                        dveP.inc(nc.vector.scalar_tensor_tensor(S(PP), S(PP), 1.0, S(SS), ALU.add, ALU.mult), "p1")
                        dveP.wait(v, t, "p1")
                        dveP.inc(nc.vector.scalar_tensor_tensor(smb[:, p, DTV, :], S(PP), 2.0, S(MX), ALU.mult, ALU.add), "dt")
                        dveP.wait(v, t, "dt")
                        tt(t, "da", S(DA), smb[:, p, DTV, :], abc[:, :, :].rearrange("p c h -> p (c h)"), ALU.mult)
                    if s == "p2":
                        peP.wait(v, t, "cs")
                        actP.wait(v, t, "ecs", 1)
                        actP.wait(v, t, "etot")
                        dveP.inc(nc.vector.tensor_copy(S(CSB), psM[:, 0:64]), "csb")
                        dveP.wait(v, t, "csb")
                        actP.wait(v, t, "wend", 1)
                        dveP.inc(nc.vector.tensor_tensor(S(WD), psM[:, 64:128], S(CSB), ALU.subtract), "w")
                        parts = lambda i: sp3[:, :, i * NH:(i + 1) * NH]
                        ch = lambda x: x.rearrange("p (c h) -> p c h", c=CH)
                        dveP.inc(nc.vector.tensor_copy(parts(0), ch(S(CSB))), "hi")
                        dveP.wait(v, t, "hi")
                        tt(t, "r1", ch(S(R1)), ch(S(CSB)), parts(0), ALU.subtract)
                        dveP.inc(nc.vector.tensor_copy(parts(1), ch(S(R1))), "mid")
                        dveP.wait(v, t, "mid")
                        tt(t, "r2", ch(S(R2)), ch(S(R1)), parts(1), ALU.subtract)
                        dveP.inc(nc.vector.tensor_copy(parts(2), ch(S(R2))), "lo")
                    if s == "p3":
                        peP.wait(v, t, "tr3")
                        dveP.inc(nc.vector.tensor_copy(csT[:, p], psMb[0:48, 0:CH * P]), "csT")
                        dveP.inc(nc.vector.tensor_scalar(csN[:, p], psMb[0:48, 0:CH * P], -1.0, None, ALU.mult), "csN")
                    if s == "p4":
                        actP.wait(v, t, "th")
                        poolB.wait(v, t, f"yg_{CH-1}", 1)
                        dveP.inc(nc.vector.scalar_tensor_tensor(zs[:, :], th[:, :], 1.0, psX[:, :], ALU.add, ALU.mult), "zs")

                def stage_b(t, p, s, c):
                    if s == "s0":
                        actB.wait(v, t, f"th_{c}")
                        poolB.wait(v, t, f"yg_{c-1}")
                        dveB.inc(nc.vector.scalar_tensor_tensor(zs[:, :], th[:, :], 1.0, psX[:, :], ALU.add, ALU.mult), f"zs_{c}")
                    if s == "s1":
                        peB.wait(v, t, f"xt_{c}")
                        d = smb[:, p, DTV, c * NH:(c + 1) * NH].unsqueeze(2).to_broadcast([P, NH, HD])
                        dveB.inc(nc.vector.tensor_tensor(heads(xdt[:, :]), heads(psX[:, :]), d, ALU.mult), f"xdt_{c}")
                        poolB.wait(v, t, f"t2_{c-1}") if c else poolB.wait(v, t, f"t2_{CH-1}", 1)
                        dveB.inc(nc.vector.tensor_tensor(heads(dx[:, :]), heads(psX[:, :]), dbc[:, :].unsqueeze(2).to_broadcast([P, NH, HD]), ALU.mult), f"dx_{c}")
                    if s == "s2":
                        peB.wait(v, t, f"gb_{c}")
                        dveB.inc(nc.vector.tensor_tensor(gm[:, :], psM[:, 0:P], tri[:, :], ALU.mult), f"gm_{c}")
                        dveB.inc(nc.vector.tensor_copy(bt[:, :], psM[:, P:P + NS]), f"bt_{c}")
                        dveB.wait(v, t, f"gm_{c}")
                        mask(t, c, 0)
                    if s == "s3":
                        peB.wait(v, t, f"yoff_{c}")
                        actP.wait(v, t, "ecs")
                        peB.wait(v, t, f"yT_{c-1}") if c else peB.wait(v, t, f"yT_{CH-1}", 1)
                        actB.wait(v, t, f"sq_{c-1}") if c else actB.wait(v, t, f"sq_{CH-1}", 1)
                        e = smb[:, p, ECS, c * NH:(c + 1) * NH].unsqueeze(2).to_broadcast([P, NH, HD])
                        dveB.inc(nc.vector.tensor_tensor(heads(yo[:, :]), heads(psX[:, :]), e, ALU.mult), f"yo_{c}")
                        mask(t, c, 1)
                    if s == "s4":
                        mask(t, c, 2)
                    if s == "s5":
                        mask(t, c, 3)
                        peB.wait(v, t, f"st_{c}")
                        poolB.wait(v, t, f"sdec_{c}")
                        dveB.inc(nc.vector.tensor_tensor(st[:, :], psX[0:NS, :], st[:, :], ALU.add), f"s_{c}")
                        peB.wait(v, t, f"yd3_{c}")
                        poolB.wait(v, t, f"t2_{c}")
                        dveB.inc(nc.vector.tensor_tensor(yo[:, :], psY[:, :], yo[:, :], ALU.add), f"y1_{c}")
                    if s == "s8":
                        peB.wait(v, t, f"out_{c}")
                        poolB.wait(v, t, f"r_{c}")
                        dveB.inc(nc.vector.scalar_tensor_tensor(o1[:, :], psM[:, :], rr[:, 2:3], bias_bc[:, :], ALU.mult, ALU.add), f"o1_{c}")
                        dveB.wait(v, t, f"o1_{c}")
                        v.wait_ge(xres_in[c % 2], (t * 2 + c // 2 + 1) * 16)
                        dveB.inc(nc.vector.scalar_tensor_tensor(xres[:, c % 2], o1[:, :], 0.0, xres[:, c % 2], ALU.max, ALU.add), f"o2_{c}")

                walk(v, stage_a, stage_p, stage_b)


def attention(nc, io, consts):
    ctx = ExitStack()
    with ctx:
        def sb(name, shape, dt=F32):
            return ctx.enter_context(nc.sbuf_tensor(name, shape, dt))

        def sem(name):
            return ctx.enter_context(nc.semaphore(name))

        NC8 = L // P
        KV = 256
        wq = sb("wq", [P, KC, C])
        wk = sb("wk", [P, KC, KV])
        wv = sb("wv", [P, KC, KV])
        wo = sb("wo_t", [P, KC, C])
        wr = sb("wr", [P, KC, E])
        br = sb("br", [P, E])
        g = sb("g", [P, KC])
        ag = sb("ag", [P, 2, KC])
        nhalf = sb("nhalf2", [P, 1])
        headblk = sb("headblk", [P, P])
        dup = sb("dup", [P, 2, P])
        tb = sb("tb", [P, 2, NC8, C])
        hb = sb("hb", [P, CH, C])
        hT = sb("hT", [P, KC, BLK])
        q = sb("q", [P, 2, KC, L])
        er = sb("er", [P, 2, BLK])
        kf = sb("kf", [P, 2, BLK])
        kvj = sb("kvj", [P, BLK])
        ks = sb("ks", [P, 2, 2])
        kv = sb("kv", [P, 2, 2])
        kk = sb("kk", [P, 2, 2])
        kd = sb("kd", [P, KC, 2])
        kb = sb("kb", [P, KC, P])
        wop = sb("wop", [P, KC, C])
        zr = sb("zr", [P, 2, BLK])
        first = sb("first", [P, KC])
        st6 = sb("st6", [P, CH, 6])
        mv = sb("mvq", [P, CH, 2])
        rs = sb("rsq", [P, CH, 2])
        st1 = sb("st1", [P, 6])
        mv1 = sb("mv1", [P, 2, 2])
        rs1 = sb("rs1", [P, 2, 2])
        xrow = sb("xrow", [P, 2, ROW])
        xT = sb("xTr", [P, KC * P])
        lg = sb("lg", [P, E])
        sx = sb("sx", [P, 4])
        pall = sb("pall", [P, NT // P // 4, 4, E])
        prt = sb("prt", [P, 512])
        psA = [ctx.enter_context(nc.psum_tensor(f"qA{i}", [P, 512], F32)) for i in range(2)]
        psZ = [ctx.enter_context(nc.psum_tensor(f"qZ{i}", [P, 512], F32)) for i in range(2)]
        psT = [ctx.enter_context(nc.psum_tensor(f"qT{i}", [P, 512], F32)) for i in range(2)]
        spare = [sem(f"spareq{i}") for i in range(3)]
        w_in, s_act, s_pool = sem("wq_in"), sem("fold_act"), sem("fold_pool")
        tb_in = [sem(f"tb_in{i}") for i in range(2)]
        y_out = sem("y_out")
        row_out = [sem(f"row_out{i}") for i in range(2)]
        p_out = sem("p_out")

        UH = 12
        U = 2 * UH
        hs = range(2)
        peA = Count(sem("pe_qa"), [f"u{n}" for n in range(U)])
        dveA = Count(sem("dve_qa"), sum(([f"st_{h}", f"mv_{h}", f"hb_{h}"] + [f"{x}{m}_{h}" for m in range(6) for x in ("c", "f")] + [f"v{m}_{h}" for m in range(2)] for h in hs), []))
        actA = Count(sem("act_qa"), sum(([f"hT{k}_{h}" for k in range(KC)] + [f"{x}{m}_{h}" for m in range(6) for x in ("n", "e")] for h in hs), []))
        poolA = Count(sem("pool_qa"), sum(([f"ve_{h}", f"r_{h}"] for h in hs), []))
        zs = [(h, k) for h in hs for k in range(KC)]
        stepsB = ["prep"] + [("z", i) for i in range(len(zs))]
        for c in range(NC8 + 2):
            stepsB += [("o", c)] * (c < NC8) + [("x", c - 1)] * (1 <= c <= NC8) + [("r", c - 2)] * (c >= 2)

        def names(per):
            return sum(([f"{x}_{s[1]}" for x in per.get(s[0], ())] if not isinstance(s, str) else list(per.get(s, ())) for s in stepsB), [])
        peB = Count(sem("pe_qb"), names({"prep": ["dup"], "z": ["z"], "o": ["o"], "x": ["xt"], "r": ["rt"]}))
        dveB = Count(sem("dve_qb"), names({"prep": ["kk0", "kk1", "kd", "kb", "wop"], "z": ["ze", "zr", "y"], "o": ["t2", "st", "mv"], "x": ["xn"],
                                           "r": ["lg", "mx", "nm", "rc", "p", "pa"]}))
        actB = Count(sem("act_qb"), names({"x": ["xT"], "r": ["ex"]}))
        poolB = Count(sem("pool_qb"), names({"o": ["ve", "r"]}))
        order = []
        na = 0
        for i, s in enumerate(stepsB):
            order.append(("B", s))
            while na < U * (i + 1) // len(stepsB):
                order.append(("A", na))
                na += 1

        def walk(engine, stage_a, stage_b, before=None):
            if before:
                before()
            for n in range(U):
                stage_a(0, 0, n)

            def step(t, p, last):
                for kind, s in order:
                    if kind == "B":
                        stage_b(t, p, *((s, 0) if isinstance(s, str) else s))
                    elif not last:
                        stage_a(t + 1, 1 - p, s)
            with engine.Fori(0, NB // 2 - 1) as b:
                step(b * 2, 0, False)
                step(b * 2 + 1, 1, False)
            step(NB - 2, 0, False)
            step(NB - 1, 1, True)

        t1, y, table = io["t1"], io["y"], io["table"]
        with nc.Block() as block:
            loads = [(wq[:, :, :], io["wq_t"].rearrange("(k p) d -> p k d", p=P)), (wk[:, :, :], io["wk_t"].rearrange("(k p) d -> p k d", p=P)),
                     (wv[:, :, :], io["wv_t"].rearrange("(k p) d -> p k d", p=P)), (wo[:, :, :], io["wo_t"].rearrange("(k p) d -> p k d", p=P)),
                     (wr[:, :, :], io["wr"].rearrange("(k p) d -> p k d", p=P)), (br[:, :], io["br"].partition_broadcast(P)), (g[:, :], io["g"]),
                     (headblk[:, :], io["c_headblk"]), (dup[:, 0], io["c_dup0"]), (dup[:, 1], io["c_dup1"])]

            @block.sync
            def _(sp):
                def load_t(t, p):
                    sp.dma_start(tb[:, p], t1[bass.ds(t * NC8, NC8)].rearrange("c p n -> p c n")).then_inc(tb_in[p], 16)

                def before():
                    for dst, src in loads:
                        sp.dma_start(dst, src).then_inc(w_in, 16)
                    load_t(0, 0)
                    for i in range(2):
                        sp.dma_start(xrow[:, i, 0:C], t1[i]).then_inc(row_out[i], 16)
                    sp.dma_start(first[:, :], io["g"]).then_inc(y_out, 16)

                def stage_b(t, p, s, c):
                    if s == "prep" and not (isinstance(t, int) and t + 1 >= NB):
                        sp.wait_ge(y_out, t * NC8 * 16 + 16)
                        load_t(t + 1, 1 - p)
                    if s == "o":
                        dveB.wait(sp, t, f"t2_{c}")
                        sp.dma_start(y[bass.ds(t * NC8 + c, 1)].rearrange("a p n -> p (a n)"), tb[:, p, c]).then_inc(y_out, 16)
                    if s == "r":
                        dveB.wait(sp, t, f"p_{c}")
                        sp.dma_start(table[bass.ds(t * NC8 + c, 1)].rearrange("a p n -> p (a n)"), xrow[:, c % 2]).then_inc(row_out[c % 2], 16)

                sp_order = lambda t, p, n: None
                walk(sp, sp_order, stage_b, before)
                for i in range(2):
                    sp.wait_ge(row_out[i], 16 * (NT // P // 2 + 1))
                sp.wait_ge(y_out, 16 * (NT // P + 1))

            @block.gpsimd
            def _(pool):
                poolA.credit(pool)
                poolB.credit(pool)
                nc.gpsimd.memset(nhalf[:, :], -0.5).then_inc(s_pool, 1)
                pool.wait_ge(s_pool, 1)

                def stage_a(t, p, n):
                    if n % UH == 0:
                        h = n // UH
                        dveA.wait(pool, t, f"mv_{h}")
                        dveA.wait(pool, t, "hb_0") if h else dveA.wait(pool, t, "hb_1", 1)
                        settle(pool, spare[0])
                        poolA.inc(nc.gpsimd.tensor_scalar(rs[:, :, 0], mv[:, :, 1], 1.0 + 1e-6, 1e-11, ALU.mult, ALU.add), f"ve_{h}")
                        poolA.wait(pool, t, f"ve_{h}")
                        poolA.inc(nc.gpsimd.tensor_tensor(rs[:, :, 1], rs[:, :, 0], nhalf[:, 0:1].to_broadcast([P, CH]), ALU.pow), f"r_{h}")

                def stage_b(t, p, s, c):
                    if s == "o":
                        dveB.wait(pool, t, f"mv_{c}")
                        settle(pool, spare[0])
                        poolB.inc(nc.gpsimd.tensor_scalar(rs1[:, c % 2, 0:1], mv1[:, c % 2, 1:2], 1e-5, None, ALU.add), f"ve_{c}")
                        poolB.wait(pool, t, f"ve_{c}")
                        poolB.inc(nc.gpsimd.tensor_tensor(rs1[:, c % 2, 1:2], rs1[:, c % 2, 0:1], nhalf[:, :], ALU.pow), f"r_{c}")

                walk(pool, stage_a, stage_b)

            @block.tensor
            def _(pe):
                peA.credit(pe)
                peB.credit(pe)
                pe.wait_ge(w_in, 16 * len(loads))
                pe.wait_ge(s_act, 2 * KC + KC + 1)

                def taken(n):
                    h, m = n // UH, n % UH
                    return (actA, f"hT{m}_{h}") if m < KC else (dveA, f"f{m-KC}_{h}") if m < 10 else (dveA, f"v{m-10}_{h}")

                def stage_a(t, p, n):
                    h, m = n // UH, n % UH
                    bank = psA[n % 2]
                    count, name = taken(n - 2 if n >= 2 else n - 2 + U)
                    count.wait(pe, t, name, 0 if n >= 2 else 1)
                    if m < KC:
                        if m == 0:
                            dveA.wait(pe, t, f"hb_{h}")
                        for c in range(CH):
                            mm = nc.tensor.transpose(bank[:, c * P:(c + 1) * P], hb[:, c, m * P:(m + 1) * P], consts["ident"][:, :])
                    else:
                        if m == KC:
                            actA.wait(pe, t, f"hT{KC-1}_{h}")
                        w, i = (wq, m - KC) if m < 8 else (wk, m - 8) if m < 10 else (wv, m - 10)
                        for k in range(KC):
                            mm = nc.tensor.matmul(bank[:, :], w[:, k, i * P:(i + 1) * P], hT[:, k, :], start=(k == 0), stop=(k == KC - 1))
                    peA.inc(mm, f"u{n}")

                def stage_b(t, p, s, c):
                    if s == "prep":
                        dveB.wait(pe, t, "kk1")
                        actB.wait(pe, t, f"xT_{NC8-1}", 1)
                        for k in range(KC):
                            mm = nc.tensor.matmul(psT[0][:, 2 * k:2 * k + 2], dup[:, k % 2], kk[:, k // 2, :], start=True, stop=True)
                        peB.inc(mm, "dup")
                    if s == "z":
                        h, k = zs[c]
                        dveB.wait(pe, t, "kb")
                        if c >= 2:
                            dveB.wait(pe, t, f"ze_{c-2}")
                        else:
                            dveB.wait(pe, t, f"t2_{NC8-2+c}", 1)
                        peB.inc(nc.tensor.matmul(psZ[c % 2][:, :], kb[:, k, :], q[:, p, k, h * BLK:(h + 1) * BLK], start=True, stop=True), f"z_{c}")
                    if s == "o":
                        dveB.wait(pe, t, f"y_{(c // CH) * KC + KC - 1}")
                        dveB.wait(pe, t, f"ze_{len(zs)-2+c}") if c < 2 else dveB.wait(pe, t, f"t2_{c-2}")
                        for k in range(KC):
                            mm = nc.tensor.matmul(psZ[c % 2][:, :], q[:, p, k, c * P:(c + 1) * P], wop[:, k, :], start=(k == 0), stop=(k == KC - 1))
                        peB.inc(mm, f"o_{c}")
                    if s == "x":
                        dveB.wait(pe, t, f"xn_{c}")
                        actB.wait(pe, t, f"xT_{c-1}") if c else dveB.wait(pe, t, "kd")
                        for k in range(KC):
                            mm = nc.tensor.transpose(psT[0][:, k * P:(k + 1) * P], xrow[:, c % 2, k * P:(k + 1) * P], consts["ident"][:, :])
                        peB.inc(mm, f"xt_{c}")
                    if s == "r":
                        actB.wait(pe, t, f"xT_{c}")
                        dveB.wait(pe, t, f"lg_{c-1}") if c else dveB.wait(pe, t, f"lg_{NC8-1}", 1)
                        for k in range(KC):
                            mm = nc.tensor.matmul(psT[1][:, 0:E], xT[:, k * P:(k + 1) * P], wr[:, k, :], start=(k == 0), stop=(k == KC - 1))
                        peB.inc(mm, f"rt_{c}")

                walk(pe, stage_a, stage_b)
                for i in range(4):
                    pe.wait_ge(p_out, i + 1)
                    for j in range(4):
                        r = 4 * i + j
                        mm = nc.tensor.transpose(psA[0][:, j * P:(j + 1) * P], pall[:, r].rearrange("p a e -> p (a e)"), consts["ident"][:, :])
                    mm.then_inc(s_pool, 1)

            @block.scalar
            def _(act):
                actA.credit(act)
                actB.credit(act)
                act.wait_ge(w_in, 16 * len(loads))
                nc.scalar.mul(ag[:, 0], g[:, :], float(HD) ** -0.5).then_inc(s_act, 1)
                act.wait_ge(s_act, 1)
                for k in range(KC):
                    nc.scalar.activation(wq[:, k, :], wq[:, k, :], ACT.Copy, scale=ag[:, 0, k:k + 1]).then_inc(s_act, 1)
                    nc.scalar.activation(wk[:, k, :], wk[:, k, :], ACT.Copy, scale=ag[:, 0, k:k + 1]).then_inc(s_act, 1)
                    nc.scalar.activation(wv[:, k, :], wv[:, k, :], ACT.Copy, scale=g[:, k:k + 1]).then_inc(s_act, 1)

                def stage_a(t, p, n):
                    h, m = n // UH, n % UH
                    bank = psA[n % 2]
                    if m < KC:
                        if m == 0:
                            peA.wait(act, t, f"u{UH-1}") if h else peA.wait(act, t, f"u{U-1}", 1)
                        peA.wait(act, t, f"u{n}")
                        actA.inc(nc.scalar.activation(hT[:, m, :], bank[:, :], ACT.Identity), f"hT{m}_{h}")
                    elif m < 10:
                        i = m - KC
                        peA.wait(act, t, f"u{n}")
                        if i >= 2:
                            dveA.wait(act, t, f"f{i-2}_{h}")
                        elif h:
                            dveA.wait(act, t, f"f{i+4}_0")
                        else:
                            dveA.wait(act, t, f"f{i+4}_1", 1)
                        actA.inc(nc.scalar.activation(er[:, i % 2], bank[:, :], ACT.Relu, scale=-1.0), f"n{i}_{h}")
                        actA.wait(act, t, f"n{i}_{h}")
                        actA.inc(nc.scalar.activation(er[:, i % 2], er[:, i % 2], ACT.Exp, scale=-1.0), f"e{i}_{h}")

                def stage_b(t, p, s, c):
                    if s == "x":
                        peB.wait(act, t, f"xt_{c}")
                        peB.wait(act, t, f"rt_{c-1}") if c else peB.wait(act, t, f"rt_{NC8-1}", 1)
                        actB.inc(nc.scalar.activation(xT[:, :], psT[0][:, :], ACT.Identity), f"xT_{c}")
                    if s == "r":
                        dveB.wait(act, t, f"nm_{c}")
                        actB.inc(nc.scalar.activation(lg[:, :], lg[:, :], ACT.Exp, bias=sx[:, 1:2], accum_out=sx[:, 2:3]), f"ex_{c}")

                walk(act, stage_a, stage_b)

            @block.vector
            def _(v):
                dveA.credit(v)
                dveB.credit(v)

                def stage_a(t, p, n):
                    h, m = n // UH, n % UH
                    bank = psA[n % 2]
                    if m == 0:
                        if h == 0:
                            v.wait_ge(tb_in[p], ((t - p) // 2 + 1) * 16)
                        dveA.wait(v, t, "mv_0") if h else dveA.wait(v, t, "mv_1", 1)
                        for c in range(CH):
                            ins = nc.vector.bn_stats(st6[:, c, :], tb[:, p, h * CH + c, :])
                        dveA.inc(ins, f"st_{h}")
                        dveA.wait(v, t, f"st_{h}")
                        settle(v, spare[1])
                        for c in range(CH):
                            ins = nc.vector.bn_aggr(mv[:, c, :], st6[:, c, :])
                        dveA.inc(ins, f"mv_{h}")
                        poolA.wait(v, t, f"r_{h}")
                        dveA.wait(v, t, f"mv_{h}")
                        peA.wait(v, t, f"u{KC-1}") if h else peA.wait(v, t, f"u{UH+KC-1}", 1)
                        for c in range(CH):
                            ins = nc.vector.tensor_scalar(hb[:, c, :], tb[:, p, h * CH + c, :], mv[:, c, 0:1], rs[:, c, 1:2], ALU.subtract, ALU.mult)
                        dveA.inc(ins, f"hb_{h}")
                    elif KC <= m < 10:
                        i = m - KC
                        actA.wait(v, t, f"e{i}_{h}")
                        dveA.inc(nc.vector.tensor_scalar(er[:, i % 2], er[:, i % 2], 0.01, None, ALU.max), f"c{i}_{h}")
                        dveA.wait(v, t, f"c{i}_{h}")
                        if i < KC:
                            if i == 0 and h == 0:
                                peB.wait(v, t, f"o_{NC8-1}", 2)
                            dveA.inc(nc.vector.scalar_tensor_tensor(q[:, p, i, h * BLK:(h + 1) * BLK], bank[:, :], 0.0, er[:, i % 2], ALU.max, ALU.add), f"f{i}_{h}")
                        else:
                            j = i - KC
                            dveB.wait(v, t, "kk1", 1)
                            dveA.inc(nc.vector.scalar_tensor_tensor(kf[:, j], bank[:, :], 0.0, er[:, i % 2], ALU.max, ALU.add, accum_out=ks[:, j, h:h + 1]), f"f{i}_{h}")
                    elif m >= 10:
                        j = m - 10
                        peA.wait(v, t, f"u{n}")
                        dveA.wait(v, t, "v0_" + str(h)) if j else dveA.wait(v, t, f"f{KC+j}_{h}")
                        dveA.inc(nc.vector.tensor_tensor_reduce(out=kvj[:, :], in0=kf[:, j], in1=bank[:, :], scale=1.0, scalar=0.0, op0=ALU.mult, op1=ALU.add,
                                                                accum_out=kv[:, j, h:h + 1]), f"v{j}_{h}")

                def stage_b(t, p, s, c):
                    if s == "prep":
                        dveA.wait(v, t, "v1_1")
                        peB.wait(v, t, "dup", 1)
                        dveB.inc(nc.vector.tensor_tensor(kk[:, :, 0], ks[:, :, 0], ks[:, :, 1], ALU.add), "kk0")
                        dveB.inc(nc.vector.tensor_tensor(kk[:, :, 1], kv[:, :, 0], kv[:, :, 1], ALU.add), "kk1")
                        peB.wait(v, t, "dup")
                        dveB.inc(nc.vector.tensor_copy(kd[:, :, :].rearrange("p k j -> p (k j)"), psT[0][:, 0:2 * KC]), "kd")
                        dveB.wait(v, t, "kd")
                        peB.wait(v, t, f"o_{NC8-1}", 1)
                        for k in range(KC):
                            ins = nc.vector.tensor_scalar(kb[:, k, :], headblk[:, :], kd[:, k, 0:1], None, ALU.mult)
                        dveB.inc(ins, "kb")
                        for k in range(KC):
                            ins = nc.vector.tensor_scalar(wop[:, k, :], wo[:, k, :], kd[:, k, 1:2], None, ALU.mult)
                        dveB.inc(ins, "wop")
                    if s == "z":
                        h, k = zs[c]
                        qq = q[:, p, k, h * BLK:(h + 1) * BLK]
                        peB.wait(v, t, f"z_{c}")
                        dveB.wait(v, t, f"y_{c-2}") if c >= 2 else dveB.wait(v, t, f"y_{len(zs)-2+c}", 1)
                        dveB.inc(nc.vector.tensor_scalar(zr[:, c % 2], psZ[c % 2][:, :], 1e-6, None, ALU.add), f"ze_{c}")
                        dveB.wait(v, t, f"ze_{c}")
                        dveB.inc(nc.vector.reciprocal(zr[:, c % 2], zr[:, c % 2]), f"zr_{c}")
                        dveB.wait(v, t, f"zr_{c}")
                        dveB.inc(nc.vector.tensor_tensor(qq, qq, zr[:, c % 2], ALU.mult), f"y_{c}")
                    if s == "o":
                        peB.wait(v, t, f"o_{c}")
                        dveB.inc(nc.vector.tensor_tensor(tb[:, p, c], psZ[c % 2][:, :], tb[:, p, c], ALU.add), f"t2_{c}")
                        dveB.wait(v, t, f"t2_{c}")
                        dveB.wait(v, t, f"mv_{c-1}") if c else dveB.wait(v, t, f"mv_{NC8-1}", 1)
                        dveB.inc(nc.vector.bn_stats(st1[:, :], tb[:, p, c]), f"st_{c}")
                        dveB.wait(v, t, f"st_{c}")
                        dveB.wait(v, t, f"xn_{c-2}") if c >= 2 else dveB.wait(v, t, f"xn_{NC8-2+c}", 1)
                        settle(v, spare[1])
                        dveB.inc(nc.vector.bn_aggr(mv1[:, c % 2], st1[:, :]), f"mv_{c}")
                    if s == "x":
                        poolB.wait(v, t, f"r_{c}")
                        v.wait_ge(row_out[c % 2], (t * (NC8 // 2) + c // 2 + 1) * 16)
                        dveB.inc(nc.vector.tensor_scalar(xrow[:, c % 2, 0:C], tb[:, p, c], mv1[:, c % 2, 0:1], rs1[:, c % 2, 1:2], ALU.subtract, ALU.mult), f"xn_{c}")
                    if s == "r":
                        peB.wait(v, t, f"rt_{c}")
                        dveB.wait(v, t, f"p_{c-1}") if c else dveB.wait(v, t, f"p_{NC8-1}", 1)
                        dveB.inc(nc.vector.tensor_tensor(lg[:, :], psT[1][:, 0:E], br[:, :], ALU.add), f"lg_{c}")
                        dveB.wait(v, t, f"lg_{c}")
                        dveB.inc(nc.vector.tensor_reduce(sx[:, 0:1], lg[:, :], AX.X, ALU.max), f"mx_{c}")
                        dveB.wait(v, t, f"mx_{c}")
                        dveB.inc(nc.vector.tensor_scalar(sx[:, 1:2], sx[:, 0:1], -1.0, None, ALU.mult), f"nm_{c}")
                        actB.wait(v, t, f"ex_{c}")
                        dveB.inc(nc.vector.reciprocal(sx[:, 3:4], sx[:, 2:3]), f"rc_{c}")
                        dveB.wait(v, t, f"rc_{c}")
                        dveB.inc(nc.vector.tensor_scalar(xrow[:, c % 2, C:ROW], lg[:, :], sx[:, 3:4], None, ALU.mult), f"p_{c}")
                        dveB.wait(v, t, f"p_{c}")
                        dveB.inc(nc.vector.tensor_copy(pall[:, p * NC8 + c, bass.ds((t - p) // 2, 1), :].rearrange("p a e -> p (a e)"), xrow[:, c % 2, C:ROW]), f"pa_{c}")

                walk(v, stage_a, stage_b)
                dveB.wait(v, NB - 1, f"pa_{NC8-1}")
                v.sem_inc(p_out, 1)
                for i in range(4):
                    v.wait_ge(s_pool, 2 + i)
                    nc.vector.tensor_copy(consts["probs"][:, i * 512:(i + 1) * 512], psA[0][:, :]).then_inc(p_out, 1)
def routing(nc, io, consts, keep):
    ctx = ExitStack()
    with ctx:
        def sb(name, shape, dt=F32):
            return ctx.enter_context(nc.sbuf_tensor(name, shape, dt))

        def sem(name):
            return ctx.enter_context(nc.semaphore(name))

        NQ = NT // 4
        QB = NQ // P
        TB = NT // P
        BITS = 30
        probs = consts["probs"]
        same, before = sb("same", [P, P]), sb("before", [P, P])
        slot, rowbase = keep["slot"], sb("rowbase", [P, E * 2])
        big = [sb(f"big{i}", [P, NQ]) for i in range(3)]
        cendb = sb("cendb", [P, E, TB])
        less = sb("less", [P, E, TB])
        cend = sb("cend", [P, QB])
        cand = sb("cand", [P, 1], I32)
        nxt = sb("nxt", [P, 1], I32)
        rej = sb("rej", [P, 1], I32)
        bitf = sb("bitf", [P, 1])
        cnt = sb("cnt", [P, 4])
        tot = sb("tot", [P, 4])
        rowf = sb("rowf", [P, E * 2])
        ps = [ctx.enter_context(nc.psum_tensor(f"rps{i}", [P, 512], F32)) for i in range(4)]
        c_in, st_out, ce_out, ce_in = sem("r_in"), sem("crow_out"), sem("cend_out"), sem("cend_in")
        s_dve, s_pe, own = sem("route_dve"), sem("route_pe"), sem("route_own")
        dve = Count(sem("search_dve"), ["cnt", "half", "next", "rej", "xor", "cand"])
        pe = Count(sem("search_pe"), ["tot"])
        with nc.Block() as block:
            @block.sync
            def _(sp):
                sp.dma_start(keep["wu"][:, :, :].rearrange("p k f -> p (k f)"), io["w_up"][0]).then_inc(keep["wu_in"], 16)
                for i in range(2):
                    sp.dma_start(keep["wd"][:, i].rearrange("p f n -> p (f n)"), io["w_down"][i]).then_inc(keep["wd_in"][i], 16)
                sp.dma_start(same[:, :], io["c_sameexp"]).then_inc(c_in, 16)
                sp.dma_start(before[:, :], io["c_segbefore"]).then_inc(c_in, 16)
                sp.dma_start(slot[:, :], io["slot"]).then_inc(c_in, 16)
                sp.dma_start(rowbase[:, :], io["rowbase"]).then_inc(c_in, 16)
                sp.wait_ge(s_dve, 6)
                for q in range(4):
                    sp.dma_start(io["cend"].rearrange("e (q r) -> q e r", q=4)[q], cend[q * E:(q + 1) * E, :]).then_inc(ce_out, 16)
                for q in range(4):
                    sp.dma_start(io["crow"].rearrange("(e q r) i -> q e (r i)", q=4, r=QB)[q], big[0][q * E:(q + 1) * E, :]).then_inc(st_out, 16)
                sp.wait_ge(ce_out, 64)
                sp.dma_start(cendb[:, :, :].rearrange("p e b -> p (e b)"), io["cend"].rearrange("e b -> (e b)").partition_broadcast(P)).then_inc(ce_in, 16)
                sp.wait_ge(st_out, 64)

            @block.tensor
            def _(t):
                pe.credit(t)
                t.wait_ge(c_in, 64)
                with t.Fori(0, BITS) as i:
                    dve.wait(t, i, "cnt")
                    dve.wait(t, i, "rej", 1)
                    pe.inc(nc.tensor.matmul(ps[0][:, 0:1], same[:, :], cnt[:, 0:1], start=True, stop=True), "tot")
                t.wait_ge(s_dve, 3)
                nc.tensor.matmul(ps[1][:, 0:1], same[:, :], cnt[:, 1:2], start=True, stop=True).then_inc(s_pe, 1)
                nc.tensor.matmul(ps[2][:, 0:1], before[:, :], cnt[:, 2:3], start=True, stop=True).then_inc(s_pe, 1)
                t.wait_ge(s_dve, 4)
                nc.tensor.matmul(ps[3][:, 0:1], before[:, :], cnt[:, 3:4], start=True, stop=True).then_inc(s_pe, 1)

            @block.vector
            def _(v):
                dve.credit(v)
                nc.vector.memset(cand[:, :], 1 << (BITS - 1)).then_inc(s_dve, 1)
                nc.vector.memset(nxt[:, :], 1 << (BITS - 1))
                nc.vector.memset(bitf[:, :], float(1 << BITS)).then_inc(s_dve, 1)
                v.wait_ge(c_in, 64)
                v.wait_ge(s_dve, 2)
                candf = cand[:, :].bitcast(F32)
                with v.Fori(0, BITS) as i:
                    dve.wait(v, i, "cand", 1)
                    pe.wait(v, i, "tot", 1)
                    dve.inc(nc.vector.tensor_scalar(big[0][:, :], probs[:, :], candf, None, ALU.is_ge, ALU.add, accum_out=cnt[:, 0:1]), "cnt")
                    dve.inc(nc.vector.tensor_scalar(bitf[:, :], bitf[:, :], 0.5, None, ALU.mult), "half")
                    dve.inc(nc.vector.tensor_scalar(nxt[:, :], nxt[:, :], 1, None, ALU.logical_shift_right), "next")
                    pe.wait(v, i, "tot")
                    dve.wait(v, i, "half")
                    dve.inc(nc.vector.tensor_scalar(rej[:, :], ps[0][:, 0:1], float(TOPK), bitf[:, 0:1], ALU.is_lt, ALU.mult), "rej")
                    dve.wait(v, i, "rej")
                    dve.inc(nc.vector.tensor_tensor(cand[:, :], cand[:, :], rej[:, :], ALU.bitwise_xor), "xor")
                    dve.wait(v, i, "xor")
                    dve.inc(nc.vector.tensor_tensor(cand[:, :], cand[:, :], nxt[:, :], ALU.bitwise_or), "cand")
                dve.wait(v, BITS - 1, "cand")
                nc.vector.tensor_scalar(big[1][:, :], probs[:, :], candf, None, ALU.is_gt, ALU.add, accum_out=cnt[:, 1:2])
                nc.vector.tensor_scalar(big[0][:, :], probs[:, :], candf, None, ALU.is_equal, ALU.add, accum_out=cnt[:, 2:3]).then_inc(s_dve, 1)
                v.wait_ge(s_pe, 2)
                v.wait_ge(s_dve, 3)
                nc.vector.tensor_scalar(tot[:, 0:1], ps[1][:, 0:1], -1.0, float(TOPK), ALU.mult, ALU.add).then_inc(own, 1)
                v.wait_ge(own, 1)
                nc.vector.tensor_tensor(tot[:, 1:2], tot[:, 0:1], ps[2][:, 0:1], ALU.subtract)
                nc.vector.tensor_tensor_scan(big[2][:, :], consts["ones"][:, 0:1].to_broadcast([P, NQ]), big[0][:, :], 0.0, ALU.mult, ALU.add).then_inc(own, 1)
                v.wait_ge(own, 2)
                nc.vector.scalar_tensor_tensor(big[2][:, :], big[2][:, :], tot[:, 1:2], big[0][:, :], ALU.is_le, ALU.mult).then_inc(own, 1)
                v.wait_ge(own, 3)
                nc.vector.tensor_tensor(big[1][:, :], big[1][:, :], big[2][:, :], ALU.add).then_inc(own, 1)
                v.wait_ge(own, 4)
                nc.vector.tensor_tensor_scan(big[2][:, :], consts["ones"][:, 0:1].to_broadcast([P, NQ]), big[1][:, :], 0.0, ALU.mult, ALU.add).then_inc(own, 1)
                v.wait_ge(own, 5)
                nc.vector.tensor_copy(cnt[:, 3:4], big[2][:, NQ - 1:NQ]).then_inc(s_dve, 1)
                v.wait_ge(s_pe, 3)
                nc.vector.tensor_scalar(big[0][:, :], big[2][:, :], ps[3][:, 0:1], None, ALU.add).then_inc(s_dve, 1)
                v.wait_ge(s_dve, 5)
                nc.vector.tensor_copy(cend[:, :], big[0][:, :].rearrange("p (r i) -> p r i", i=P)[:, :, P - 1]).then_inc(s_dve, 1)
                v.wait_ge(ce_in, 16)
                for a in range(2):
                    nc.vector.tensor_scalar(less[:, :, :], cendb[:, :, :], slot[:, a:a + 1], None, ALU.is_le).then_inc(own, 1)
                    v.wait_ge(own, 6 + 2 * a)
                    nc.vector.tensor_reduce(keep["blkf"][:, :, a], less[:, :, :], AX.X, ALU.add).then_inc(own, 1)
                    v.wait_ge(own, 7 + 2 * a)
                nc.vector.tensor_tensor(rowf[:, :], keep["blkf"][:, :, :].rearrange("p e a -> p (e a)"), rowbase[:, :], ALU.add).then_inc(own, 1)
                v.wait_ge(own, 10)
                nc.vector.tensor_copy(keep["rowi"][:, :], rowf[:, :])
def experts(nc, io, consts, keep):
    ctx = ExitStack()
    with ctx:
        def sb(name, shape, dt=F32):
            return ctx.enter_context(nc.sbuf_tensor(name, shape, dt))

        def sem(name):
            return ctx.enter_context(nc.semaphore(name))

        NG = 2 * GS
        wu, wd, slot, rowi, blkf = (keep[k] for k in ("wu", "wd", "slot", "rowi", "blkf"))
        wu_in, wd_in = keep["wu_in"], keep["wd_in"]
        bup = sb("bup", [P, GRP, FT])
        bias = sb("bias", [P, FT])
        cri = sb("cri", [P, NG], I32)
        bk = sb("bk", [P, NG])
        cr = sb("cr", [P, NG, P])
        below = sb("below", [P, 2, P])
        cn = sb("cn", [P, NG])
        tokf = sb("tokf", [P, NG])
        tok = sb("tok", [P, 2, NG], I32)
        gate = sb("gate", [P, 2, NG])
        xg = sb("xg", [P, NG, ROW])
        xT = sb("xgT", [P, KC, NG * P])
        act_t = sb("act_t", [P, FT, NG * P])
        ob = sb("ob", [P, 4, C])
        first = sb("first_s", [P, 2, 2])
        psU = [ctx.enter_context(nc.psum_tensor(f"psU{i}", [P, 512], F32)) for i in range(3)]
        psD = [ctx.enter_context(nc.psum_tensor(f"psD{i}", [P, 512], F32)) for i in range(3)]
        psR = [ctx.enter_context(nc.psum_tensor(f"psR{i}", [P, 512], F32)) for i in range(2)]
        spare = [sem(f"spare_f{i}") for i in range(2)]
        b_in, cr_in, xg_in, ones_set = sem("bup_in"), sem("cr_in"), sem("xg_in"), sem("ones_set")
        added = [sem(f"added{i}") for i in range(2)]

        dveR = Count(sem("dve_r"), ["idx", "bk", "bias"] + [f"c{n}" for n in range(NG)] + ["tb", "tok"] + [f"g{j}" for j in range(GS)] + [f"t{n}" for n in range(2 * KC)])
        peR = Count(sem("pe_r"), [f"t{n}" for n in range(2 * KC)])
        NU = 2 * FT
        peU = Count(sem("pe_u"), [f"u{n}" for n in range(NU)])
        actU = Count(sem("act_u"), [f"u{n}" for n in range(NU)])
        peD = Count(sem("pe_d"), [f"d{n}" for n in range(NG)])
        dveD = Count(sem("dve_d"), [f"o{n}" for n in range(NG)])

        fetch = {0: ["index"], 1: ["rows"], 3: ["gates", ("t", 0), ("t", 1)], 4: [("t", 2), ("t", 3)], 5: [("t", 4), ("t", 5)], 6: [("t", 6), ("t", 7)]}

        def last_of(n, count):
            return max(m for m in range(count) if m % 3 == n)

        def walk(engine, fetch_step, up, down):
            for n in range(NG):
                for s in fetch.get(n, []):
                    fetch_step(0, 0, *((s, 0) if isinstance(s, str) else s))
            for n in range(NU):
                up(0, 0, n)

            def step(t, p, last):
                for n in range(NG):
                    down(t, p, n)
                    if not last:
                        for s in fetch.get(n, []):
                            fetch_step(t + 1, 1 - p, *((s, 0) if isinstance(s, str) else s))
                if not last:
                    for n in range(NU):
                        up(t + 1, 1 - p, n)
            with engine.Fori(0, GRP // 2 - 1) as b:
                step(b * 2, 0, False)
                step(b * 2 + 1, 1, False)
            step(GRP - 2, 0, False)
            step(GRP - 1, 1, True)

        nothing = lambda *a: None
        y_rows = io["y"].rearrange("c p n -> (c p) n")
        table = io["table"].rearrange("c p n -> (c p) n")
        with nc.Block() as block:
            @block.sync
            def _(sp):
                sp.dma_start(bup[:, :, :], io["b_up"]).then_inc(b_in, 16)

                def down(t, p, n):
                    j, a = n // 2, n % 2
                    if n == 0 and not (isinstance(t, int) and t == GRP - 1):
                        peU.wait(sp, t, f"u{NU-1}")
                        sp.dma_start(wu[:, :, :].rearrange("p k f -> p (k f)"), io["w_up"][bass.ds(t + 1, 1)].rearrange("g p f -> p (g f)")).then_inc(wu_in, 16)
                    if a and not (isinstance(t, int) and t == GRP - 1 and j >= 2):
                        peD.wait(sp, t, f"d{n}")
                        sp.dma_start(wd[:, j % 2].rearrange("p f n -> p (f n)"), io["w_down"][bass.ds(GS * t + j + 2, 1)].rearrange("e p f -> p (e f)")).then_inc(wd_in[j % 2], 16)

                walk(sp, nothing, nothing, down)
                for i in range(2):
                    sp.wait_ge(added[i], 16 + 32 * E // 2)

            @block.gpsimd
            def _(pool):
                def fetch_step(t, p, s, i):
                    if s == "index":
                        dveR.wait(pool, t, "idx")
                        dveR.wait(pool, t, f"c{NG-1}", 1)
                        settle(pool, spare[0])
                        for n in range(NG):
                            pool.indirect_dma_start(out=cr[:, n, :], out_offset=None, in_=io["crow"], in_offset=bass.IndirectOffsetOnAxis(ap=cri[:, n:n + 1], axis=0)).then_inc(cr_in, 16)
                    if s == "rows":
                        dveR.wait(pool, t, "tok")
                        dveR.wait(pool, t, f"g{GS-1}", 1)
                        peR.wait(pool, t, f"t{2*KC-1}", 1)
                        settle(pool, spare[0])
                        for n in range(NG):
                            pool.indirect_dma_start(out=xg[:, n, :], out_offset=None, in_=table, in_offset=bass.IndirectOffsetOnAxis(ap=tok[:, p, n:n + 1], axis=0)).then_inc(xg_in, 16)

                def down(t, p, n):
                    j, a = n // 2, n % 2
                    dveD.wait(pool, t, f"o{n}")
                    if a == 0:
                        pool.wait_ge(added[(j - 1) % 2], 16 + 32 * (2 * t + (j + 1) // 2))
                    settle(pool, spare[0])
                    pool.indirect_dma_start(out=y_rows, out_offset=bass.IndirectOffsetOnAxis(ap=tok[:, p, n:n + 1], axis=0), in_=ob[:, n % 4, :], in_offset=None,
                                            compute_op=ALU.add).then_inc(added[j % 2], 16)

                for i in range(2):
                    pool.dma_start(first[:, i], io["slot"]).then_inc(added[i], 16)
                walk(pool, fetch_step, nothing, down)

            @block.tensor
            def _(pe):
                for c in (peR, peU, peD):
                    c.credit(pe)

                def fetch_step(t, p, s, i):
                    if s == "t":
                        k, h = i % KC, i // KC
                        if i == 0:
                            pe.wait_ge(xg_in, 16 * NG * t + 16 * NG)
                        dveR.wait(pe, t, f"t{i-2}") if i >= 2 else dveR.wait(pe, t, f"t{2*KC-2+i}", 1)
                        for q in range(4):
                            mm = nc.tensor.transpose(psR[i % 2][:, q * P:(q + 1) * P], xg[:, 4 * h + q, k * P:(k + 1) * P], consts["ident"][:, :])
                        peR.inc(mm, f"t{i}")

                def up(t, p, n):
                    h, f = n // FT, n % FT
                    m = min(P, FF - f * P)
                    if n == 0:
                        pe.wait_ge(wu_in, 16 * t + 16)
                        dveR.wait(pe, t, f"t{2*KC-1}")
                    actU.wait(pe, t, f"u{n-3}") if n >= 3 else actU.wait(pe, t, f"u{last_of(n, NU)}", 1)
                    for k in range(KC):
                        mm = nc.tensor.matmul(psU[n % 3][0:m, :], wu[:, k, f * P:f * P + m], xT[:, k, h * 512:(h + 1) * 512], start=(k == 0), stop=(k == KC - 1))
                    peU.inc(mm, f"u{n}")

                def down(t, p, n):
                    j, a = n // 2, n % 2
                    if a == 0:
                        pe.wait_ge(wd_in[j % 2], 16 * (2 * t + j // 2 + 1))
                    if n in (0, NG // 2):
                        actU.wait(pe, t, f"u{FT-1}" if n == 0 else f"u{NU-1}")
                    dveD.wait(pe, t, f"o{n-3}") if n >= 3 else dveD.wait(pe, t, f"o{last_of(n, NG)}", 1)
                    for f in range(FT):
                        mm = nc.tensor.matmul(psD[n % 3][:, :], act_t[:, f, n * P:(n + 1) * P], wd[:, j % 2, f, :], start=(f == 0), stop=(f == FT - 1))
                    peD.inc(mm, f"d{n}")

                walk(pe, fetch_step, up, down)

            @block.scalar
            def _(act):
                actU.credit(act)
                act.wait_ge(ones_set, 1)

                def up(t, p, n):
                    h, f = n // FT, n % FT
                    m = min(P, FF - f * P)
                    peU.wait(act, t, f"u{n}")
                    if n == 0:
                        dveR.wait(act, t, "bias")
                    if f == 0:
                        peD.wait(act, t, f"d{4*h+3}", 1)
                    actU.inc(nc.scalar.activation(act_t[0:m, f, h * 512:(h + 1) * 512], psU[n % 3][0:m, :], ACT.Silu, bias=bias[0:m, f:f + 1]), f"u{n}")

                walk(act, nothing, up, nothing)

            @block.vector
            def _(v):
                dveR.credit(v)
                dveD.credit(v)
                nc.vector.memset(act_t[:, FT - 1, :], 1.0).then_inc(ones_set, 1)
                v.wait_ge(b_in, 16)

                def fetch_step(t, p, s, i):
                    if s == "index":
                        if not isinstance(t, int) or t >= 2:
                            for x in added:
                                v.wait_ge(x, 16 + 64 * (t - 1))
                        dveR.inc(nc.vector.tensor_copy(cri[:, :], rowi[:, bass.ds(t * NG, NG)]), "idx")
                        dveR.wait(v, t, "tb", 1)
                        dveR.inc(nc.vector.tensor_copy(bk[:, :], blkf[:, bass.ds(t * GS, GS), :].rearrange("p e a -> p (e a)")), "bk")
                        actU.wait(v, t, f"u{NU-1}", 1)
                        dveR.inc(nc.vector.tensor_copy(bias[:, :], bup[:, bass.ds(t, 1), :].rearrange("p g f -> p (g f)")), "bias")
                    if s == "rows":
                        v.wait_ge(cr_in, 16 * NG * t + 16 * NG)
                        for n in range(NG):
                            dveR.wait(v, t, f"c{n-2}") if n >= 2 else dveR.wait(v, t, f"c{NG-2+n}", 1)
                            if n == 0:
                                dveR.wait(v, t, "tb", 1)
                            dveR.inc(nc.vector.tensor_scalar(below[:, n % 2], cr[:, n, :], slot[:, n % 2:n % 2 + 1], None, ALU.is_le, ALU.add, accum_out=cn[:, n:n + 1]), f"c{n}")
                        dveR.wait(v, t, f"c{NG-1}")
                        dveR.wait(v, t, "tok", 1)
                        dveR.inc(nc.vector.scalar_tensor_tensor(tokf[:, :], bk[:, :], float(P), cn[:, :], ALU.mult, ALU.add), "tb")
                        dveR.wait(v, t, "tb")
                        dveR.inc(nc.vector.tensor_copy(tok[:, p], tokf[:, :]), "tok")
                    if s == "gates":
                        v.wait_ge(xg_in, 16 * NG * t + 16 * NG)
                        dveD.wait(v, t, f"o{NG-1}", 2)
                        for j in range(GS):
                            dveR.inc(nc.vector.tensor_copy(gate[:, p, 2 * j:2 * j + 2], xg[:, 2 * j:2 * j + 2, bass.ds(C + GS * t + j, 1)].rearrange("p a o -> p (a o)")), f"g{j}")
                    if s == "t":
                        k, h = i % KC, i // KC
                        peR.wait(v, t, f"t{i}")
                        if i == 0:
                            peU.wait(v, t, f"u{NU-1}", 1)
                        dveR.inc(nc.vector.tensor_copy(xT[:, k, h * 512:(h + 1) * 512], psR[i % 2][:, :]), f"t{i}")

                def down(t, p, n):
                    j, a = n // 2, n % 2
                    peD.wait(v, t, f"d{n}")
                    if n == 0:
                        dveR.wait(v, t, f"g{GS-1}")
                    if a == 0:
                        v.wait_ge(added[j % 2], 16 + 32 * (2 * t + j // 2))
                    dveD.inc(nc.vector.tensor_scalar(ob[:, n % 4, :], psD[n % 3][:, :], gate[:, p, n:n + 1], None, ALU.mult), f"o{n}")

                walk(v, fetch_step, nothing, down)




def consts_np():
    i = np.arange(P)
    k, m = i[:, None], i[None, :]
    c = {
        "ident": k == m, "tri": k <= m, "ones": k >= 0 * m, "gmat": (k // 16 == m // 16) / 16.0,
        "sameexp": k % E == m % E, "segbefore": (k % E == m % E) & (k // E < m // E),
        "headblk": k // HD == m // HD, "dup0": k == m % HD, "dup1": k == HD + m % HD,
    }
    c = {n: np.ascontiguousarray(np.broadcast_to(x, (P, P)), np.float32) for n, x in c.items()}
    r = np.arange(48)[:, None] % NH == np.arange(NH * P)[None, :] // P
    c["selp"] = r.astype(np.float32)
    return c


def program(nc, io):
    ctx = ExitStack()
    with ctx:
        def sb(name, shape, dt=F32):
            return ctx.enter_context(nc.sbuf_tensor(name, shape, dt))
        consts = {k: sb("k_" + k, [P, P]) for k in _CONSTS1}
        first_layer(nc, io, consts, None)
        consts["probs"] = sb("probs", [P, NT // 4])
        attention(nc, io, consts)
        keep = {"wu": sb("wu", [P, KC, FF]), "wd": sb("wd", [P, 2, FT, C]), "slot": sb("slot", [P, 2]),
                "rowi": sb("rowi", [P, 2 * E], I32), "blkf": sb("blkf", [P, E, 2])}
        keep["wu_in"] = ctx.enter_context(nc.semaphore("wu_in"))
        keep["wd_in"] = [ctx.enter_context(nc.semaphore(f"wd_in{i}")) for i in range(2)]
        routing(nc, io, consts, keep)
        experts(nc, io, consts, keep)




def _layout(i):
    f = lambda n: np.ascontiguousarray(i[n])
    x = f("x").reshape(NB, C, L)
    col = lambda a: np.ascontiguousarray(a.reshape(-1, P).T)
    a = {
        "x_ch": x, "x_tok": np.ascontiguousarray(x.transpose(0, 2, 1)).reshape(NT // P, P, C),
        "win_t": np.ascontiguousarray(f("L0_conv_in_proj_w").T), "wo": f("L0_conv_out_proj_w"),
        "w2_t": np.ascontiguousarray(f("L0_conv_conv2d_w").T),
        "rms_w": col(f("L0_conv_rms_w")), "ln_w": col(f("L0_conv_ln_w")), "ln_b": col(f("L0_conv_ln_b")),
        "conv_w": np.ascontiguousarray(f("L0_conv_conv1d_w").reshape(-1, P, 4).transpose(1, 0, 2)), "conv_b": col(f("L0_conv_conv1d_b")),
        "D": f("L0_conv_D"), "A_log": f("L0_conv_A_log"), "dt_bias": f("L0_conv_dt_bias"),
        "bn_g": f("L0_conv_bn_g"), "bn_b": f("L0_conv_bn_b"), "bn_mean": f("L0_conv_bn_mean"), "bn_var": f("L0_conv_bn_var"), "c2b": f("L0_conv_conv2d_b"),
    }
    a |= {
        "wq_t": np.ascontiguousarray(f("L1_attn_wq").T), "wk_t": np.ascontiguousarray(f("L1_attn_wk").T),
        "wv_t": np.ascontiguousarray(f("L1_attn_wv").T), "wo_t": np.ascontiguousarray(f("L1_attn_wo").T),
        "wr": f("L1_ffn_W_router"), "br": f("L1_ffn_b_router"), "g": col(f("L1_attn_g")),
    }
    wd = np.zeros((E, FT * P, C), np.float32)
    wd[:, :FF], wd[:, FF] = f("L1_ffn_W_down"), f("L1_ffn_b_down")
    bu = np.zeros((GRP, FT * P), np.float32)
    bu[:, :FF] = f("L1_ffn_b_up")
    a |= {
        "w_up": np.ascontiguousarray(f("L1_ffn_W_up").reshape(GRP, KC, P, FF).transpose(0, 2, 1, 3)).reshape(GRP, P, KC * FF),
        "w_down": np.ascontiguousarray(wd.reshape(E, FT, P, C).transpose(0, 2, 1, 3)).reshape(E, P, FT * C),
        "b_up": np.ascontiguousarray(bu.reshape(GRP, FT, P).transpose(2, 0, 1)),
        "slot": np.ascontiguousarray(np.arange(2 * P, dtype=np.float32).reshape(2, P).T),
        "rowbase": np.ascontiguousarray(np.broadcast_to(np.repeat(np.arange(E) * (NT // P), 2).astype(np.float32), (P, 2 * E))),
    }
    for n, c in consts_np().items():
        a["selp" if n == "selp" else "c_" + n] = c
    return a


def kernel(**inputs):
    import concourse.bacc as _bacc
    from concourse.bass_utils import run_bass_kernel_spmd as _run

    nc = _bacc.Bacc("TRN2", target_bir_lowering=False, num_devices=1)
    arrays = _layout({n: np.asarray(v) for n, v in inputs.items()})
    io = {n: nc.dram_tensor("in_" + n, a.shape, F32, kind="ExternalInput").ap() for n, a in arrays.items()}
    io["t1"] = nc.dram_tensor("tokens_1", (NT // P, P, C), F32, kind="Internal").ap()
    io["table"] = nc.dram_tensor("rows", (NT // P, P, ROW), F32, kind="Internal").ap()
    io["crow"] = nc.dram_tensor("running", (E * NT // P, P), F32, kind="Internal").ap()
    io["cend"] = nc.dram_tensor("block_ends", (E, NT // P), F32, kind="Internal").ap()
    io["y"] = nc.dram_tensor("out_y", (NT // P, P, C), F32, kind="ExternalOutput").ap()
    program(nc, io)
    r = _run(nc, [{"in_" + n: a for n, a in arrays.items()}], core_ids=[0])
    t = r.results[0]["out_y"].reshape(NB, L, C)
    return np.ascontiguousarray(t.transpose(0, 2, 1)).reshape(NB, C, 32, 32)
```

```python
import concourse.bass as bass
import numpy as np
from concourse import mybir
from contextlib import ExitStack

F32 = mybir.dt.float32
F32R = mybir.dt.float32r
BF16 = mybir.dt.bfloat16
I32 = mybir.dt.int32
U32 = mybir.dt.uint32
ALU = mybir.AluOpType
ACT = mybir.ActivationFunctionType
AX = mybir.AxisListType

P = 128
NB, C, L = 8, 512, 1024
KC = C // P
DIN, NS, NH, HD = 1024, 64, 16, 64
DXBC = DIN + 2 * NS
BLK = 512
CH = BLK // P
NBLK = NB * L // BLK
NT = NB * L
E, TOPK = 32, 256
GRP, GS = 8, 4
FF = 1365
FT = (FF + P - 1) // P
FR = FF - (FT - 1) * P
ROW = C + E

_CONSTS1 = ("ident", "tri", "ones", "gmat")


class Count:

    def __init__(self, sem, names):
        self.sem, self.names, self.n = sem, list(names), len(names)
        self.at = {x: i for i, x in enumerate(self.names)}
        assert len(self.at) == self.n
        self.next = 0

    def credit(self, engine):
        engine.sem_inc(self.sem, 2 * self.n)

    def inc(self, ins, name):
        assert self.names[self.next % self.n] == name, (self.names[self.next % self.n], name)
        self.next += 1
        ins.then_inc(self.sem, 1)

    def wait(self, engine, t, name, back=0):
        engine.wait_ge(self.sem, (t + (2 - back)) * self.n + self.at[name] + 1)


def settle(engine, spare):
    engine.sem_inc(spare, 1)
def first_layer(nc, io, consts):
    ctx = ExitStack()
    with ctx:
        def sb(name, shape, dt=F32):
            return ctx.enter_context(nc.sbuf_tensor(name, shape, dt))

        def sem(name):
            return ctx.enter_context(nc.semaphore(name))

        ND = DXBC // P
        win = sb("win", [P, KC, 2192])
        wc = sb("wc", [P, DIN // P, C])
        bias_bc = sb("bias_bc", [P, C])
        gnab = sb("gnab", [P, 2, NB, KC])
        lnw = sb("lnw", [P, KC])
        lnb = sb("lnb", [P, KC])
        cw = sb("cw", [P, ND, 4])
        cb = sb("cb", [P, ND])
        abc = sb("abc", [P, CH, NH])
        dtb = sb("dtb", [P, CH, NH])
        dbc = sb("dbc", [P, NH])
        nhalf = sb("nhalf", [P, 1])
        sel = sb("sel", [48, NH * P], BF16)
        identb = sb("identb", [P, P], BF16)
        ident, tri, ones, gmat = consts["ident"], consts["tri"], consts["ones"], consts["gmat"]

        spare = [sem(f"spare{i}") for i in range(3)]
        with ExitStack() as c0:
            def sb0(name, shape, dt=F32):
                return c0.enter_context(nc.sbuf_tensor(name, shape, dt))
            wo_nat = sb0("wo_nat", [P, KC, DIN])
            w2t = sb0("w2t", [P, KC, C])
            bn = sb0("bn", [P, 5, C])
            bnv = sb0("bnv", [P, KC])
            rmsw = sb0("rmsw", [P, DIN // P])
            selp = sb0("selp", [48, NH * P])
            gx = sb0("gx", [P, 2, KC, L])
            gst = sb0("gst", [P, KC, 2, 6])
            cmv = sb0("cmv", [P, NB, KC, 2])
            cmv1 = sb0("cmv1", [P, KC, 2])
            gsm = sb0("gsm", [P, 4, NB * KC])
            gps = [c0.enter_context(nc.psum_tensor(f"gps{i}", [P, 512], F32)) for i in range(8)]
            w_in, gx_in, gx_in1 = (c0.enter_context(nc.semaphore(s)) for s in ("w_in", "gx_in0", "gx_in1"))
            gx_ins = [gx_in, gx_in1]
            gx_used = c0.enter_context(nc.semaphore("gx_used"))
            st_done = c0.enter_context(nc.semaphore("st_done"))
            d_s, a_s, p_s, t_s = (c0.enter_context(nc.semaphore(s)) for s in ("setup_dve", "setup_act", "setup_pool", "setup_pe"))
            with nc.Block() as block:
                loads = [
                    (win[:, :, :], io["win_t"].rearrange("(k p) d -> p k d", p=P)),
                    (wo_nat[:, :, :], io["wo"].rearrange("(k p) d -> p k d", p=P)),
                    (w2t[:, :, :], io["w2_t"].rearrange("(k p) d -> p k d", p=P)),
                    (rmsw[:, :], io["rms_w"]), (lnw[:, :], io["ln_w"]), (lnb[:, :], io["ln_b"]),
                    (cw[:, :, :], io["conv_w"]), (cb[:, :], io["conv_b"]),
                    (selp[:, :], io["selp"]),
                    (dbc[:, :], io["D"].partition_broadcast(P)),
                ]
                loads += [(bn[:, i, :], io[k].partition_broadcast(P)) for i, k in enumerate(("bn_g", "bn_b", "bn_mean", None, "c2b")) if k]
                loads += [(bnv[:, :], io["bn_var"])]
                loads += [(abc[:, c, :], io["A_log"].partition_broadcast(P)) for c in range(CH)]
                loads += [(dtb[:, c, :], io["dt_bias"].partition_broadcast(P)) for c in range(CH)]
                loads += [(consts[k][:, :], io["c_" + k]) for k in consts]

                @block.sync
                def _(sp):
                    with sp.Fori(0, NB // 2) as h:
                        for q in range(2):
                            sp.wait_ge(gx_used, 2 * h + q + 1)
                            sp.dma_start(gx[:, q], io["x_ch"][bass.ds(2 * h + q, 1)].rearrange("b (k p) n -> p (b k) n", p=P)).then_inc(gx_ins[q], 16)

                @block.gpsimd
                def _(pool):
                    for dst, src in loads:
                        pool.dma_start(dst, src).then_inc(w_in, 16)
                    nc.gpsimd.memset(nhalf[:, :], -0.5).then_inc(p_s, 1)
                    pool.wait_ge(w_in, 16 * len(loads))
                    pool.wait_ge(p_s, 1)
                    nc.gpsimd.tensor_scalar(bnv[:, :], bnv[:, :], 1e-5, None, ALU.add).then_inc(p_s, 1)
                    pool.wait_ge(p_s, 2)
                    nc.gpsimd.tensor_tensor(bnv[:, :], bnv[:, :], nhalf[:, 0:1].to_broadcast([P, KC]), ALU.pow).then_inc(p_s, 1)
                    pool.wait_ge(d_s, 5)
                    nc.gpsimd.tensor_scalar(gsm[:, 1, :], gsm[:, 1, :], 1e-5, None, ALU.add).then_inc(p_s, 1)
                    pool.wait_ge(p_s, 4)
                    nc.gpsimd.tensor_tensor(gnab[:, 0].rearrange("p b k -> p (b k)"), gsm[:, 1, :],
                                            nhalf[:, 0:1].to_broadcast([P, NB * KC]), ALU.pow).then_inc(p_s, 1)

                @block.scalar
                def _(act):
                    act.wait_ge(w_in, 16 * len(loads))
                    nc.scalar.activation(abc[:, :, :], abc[:, :, :], ACT.Exp).then_inc(a_s, 1)
                    nc.scalar.mul(win[:, :, 0:DIN], win[:, :, 0:DIN], 0.5).then_inc(a_s, 1)
                    nc.scalar.mul(cw[:, :, :], cw[:, :, :], 0.5).then_inc(a_s, 1)
                    nc.scalar.mul(cb[:, :], cb[:, :], 0.5).then_inc(a_s, 1)
                    nc.scalar.copy(sel[:, :], selp[:, :]).then_inc(a_s, 1)
                    nc.scalar.copy(identb[:, :], ident[:, :]).then_inc(a_s, 1)
                    act.wait_ge(p_s, 3)
                    for k in range(KC):
                        nc.scalar.activation(bn[:, 3, k * P:(k + 1) * P], ident[:, :], ACT.Copy, scale=bnv[:, k:k + 1]).then_inc(a_s, 1)
                    act.wait_ge(t_s, 1)
                    nc.scalar.copy(bn[:, 3, :], gps[0][:, :]).then_inc(a_s, 1)

                @block.tensor
                def _(pe):
                    pe.wait_ge(w_in, 16 * len(loads))
                    pe.wait_ge(a_s, 6 + KC)
                    nc.tensor.matmul(gps[0][:, :], ones[:, :], bn[:, 3, :], start=True, stop=True).then_inc(t_s, 1)
                    pe.wait_ge(a_s, 7 + KC)
                    for dk in range(DIN // P):
                        for k in range(KC):
                            mm = nc.tensor.matmul(gps[dk][:, :], wo_nat[:, k, dk * P:(dk + 1) * P], w2t[:, k, :], start=(k == 0), stop=(k == KC - 1))
                        mm.then_inc(t_s, 1)
                    pe.wait_ge(d_s, 2)
                    nc.tensor.matmul(gps[0][:, 0:NB * KC], gmat[:, :], gsm[:, 0, :], start=True, stop=True).then_inc(t_s, 1)
                    pe.wait_ge(d_s, 4)
                    nc.tensor.matmul(gps[1][:, 0:NB * KC], gmat[:, :], gsm[:, 3, :], start=True, stop=True).then_inc(t_s, 1)

                @block.vector
                def _(v):
                    v.sem_inc(gx_used, 2)
                    v.sem_inc(st_done, 2)
                    with v.Fori(0, NB // 2) as h:
                        for q in range(2):
                            v.wait_ge(gx_ins[q], 16 * (h + 1))
                            v.wait_ge(st_done, 2 * (2 * h + q) + 2)
                            for k in range(KC):
                                for j in range(2):
                                    ins = nc.vector.bn_stats(gst[:, k, j, :], gx[:, q, k, j * 512:(j + 1) * 512])
                            ins.then_inc(gx_used, 1)
                            v.wait_ge(gx_used, 2 * h + q + 3)
                            settle(v, spare[0])
                            for k in range(KC):
                                ins = nc.vector.bn_aggr(cmv1[:, k, :], gst[:, k].rearrange("p j s -> p (j s)"))
                            ins.then_inc(st_done, 1)
                            v.wait_ge(st_done, 2 * (2 * h + q) + 3)
                            nc.vector.tensor_copy(cmv[:, bass.ds(2 * h + q, 1)].rearrange("p b k t -> p (b k t)"), cmv1[:, :, :].rearrange("p k t -> p (k t)")).then_inc(st_done, 1)
                    v.wait_ge(p_s, 3)
                    v.wait_ge(st_done, 2 * NB + 2)
                    v.wait_ge(a_s, 7 + KC)
                    nc.vector.tensor_tensor(bn[:, 3, :], bn[:, 3, :], bn[:, 0, :], ALU.mult).then_inc(d_s, 1)
                    v.wait_ge(d_s, 1)
                    for dk in range(DIN // P):
                        v.wait_ge(t_s, dk + 2)
                        nc.vector.scalar_tensor_tensor(wc[:, dk, :], gps[dk][:, :], rmsw[:, dk:dk + 1], bn[:, 3, :], ALU.mult, ALU.mult)
                    nc.vector.tensor_copy(gsm[:, 0, :], cmv[:, :, :, 0].rearrange("p b k -> p (b k)")).then_inc(d_s, 1)
                    v.wait_ge(t_s, 10)
                    nc.vector.tensor_copy(gsm[:, 2, :], gps[0][:, 0:NB * KC]).then_inc(d_s, 1)
                    v.wait_ge(d_s, 3)
                    nc.vector.tensor_tensor(gsm[:, 3, :], gsm[:, 0, :], gsm[:, 2, :], ALU.subtract).then_inc(st_done, 1)
                    v.wait_ge(st_done, 2 * NB + 3)
                    nc.vector.tensor_tensor(gsm[:, 3, :], gsm[:, 3, :], gsm[:, 3, :], ALU.mult).then_inc(st_done, 1)
                    v.wait_ge(st_done, 2 * NB + 4)
                    nc.vector.tensor_tensor(gsm[:, 3, :], gsm[:, 3, :], cmv[:, :, :, 1].rearrange("p b k -> p (b k)"), ALU.add).then_inc(d_s, 1)
                    v.wait_ge(t_s, 11)
                    nc.vector.tensor_copy(gsm[:, 1, :], gps[1][:, 0:NB * KC]).then_inc(d_s, 1)
                    v.wait_ge(p_s, 5)
                    nc.vector.scalar_tensor_tensor(gnab[:, 1].rearrange("p b k -> p (b k)"), gsm[:, 2, :], -1.0,
                                                   gnab[:, 0].rearrange("p b k -> p (b k)"), ALU.mult, ALU.mult).then_inc(d_s, 1)
                    nc.vector.tensor_scalar(abc[:, :, :], abc[:, :, :], -1.0, None, ALU.mult)
                    nc.vector.tensor_tensor(bias_bc[:, :], bn[:, 4, :], bn[:, 2, :], ALU.subtract).then_inc(d_s, 1)
                    v.wait_ge(d_s, 7)
                    nc.vector.tensor_tensor(bias_bc[:, :], bias_bc[:, :], bn[:, 3, :], ALU.mult).then_inc(d_s, 1)
                    v.wait_ge(d_s, 8)
                    nc.vector.tensor_tensor(bias_bc[:, :], bias_bc[:, :], bn[:, 1, :], ALU.add).then_inc(d_s, 1)

        xc = sb("xc", [P, KC, BLK])
        tn = sb("tn", [P, CH, C])
        xn = sb("xn", [P, 2, KC, BLK])
        raw = sb("raw", [P, ND, 3 + BLK])
        cv = sb("cv", [P, 2, BLK])
        tha = sb("tha", [P, BLK])
        xs = sb("xs", [P, 2, ND - 1, BLK])
        bcm = sb("bcm", [NS, 2, 2, BLK])
        lst = sb("lst", [P, 6])
        lmv = sb("lmv", [P, CH, 2])
        lrs = sb("lrs", [P, CH, 2])
        dtu = sb("dtu", [P, 2, CH * NH])
        sm = sb("sm", [P, 9, CH * NH])
        smb = sb("smb", [P, 2, 4, CH * NH])
        sp3 = sb("sp3", [P, CH, 3 * NH], BF16)
        csT = sb("csT", [48, 2, CH * P], BF16)
        csN = sb("csN", [48, 2, CH * P], BF16)
        th = sb("th", [P, DIN])
        zs = sb("zs", [P, DIN])
        xdt = sb("xdt", [P, DIN])
        xw = th
        dx = sb("dx", [P, DIN])
        yo = sb("yo", [P, DIN])
        gm = sb("gm", [P, P])
        bt = sb("bt", [P, NS])
        es = sb("es", [P, 2, 4 * P])
        ms = sb("ms", [P, 2, 4 * P])
        st = sb("st", [NS, DIN])
        yT = sb("yT", [P, DIN // P, P])
        rr = sb("rr", [P, 4])
        o1 = sb("o1", [P, C])
        xres = sb("xres", [P, 2, C])
        junk = sb("junk", [P, 1])
        psA = [ctx.enter_context(nc.psum_tensor(f"psA{i}", [P, 512], F32)) for i in range(2)]
        psArg = ctx.enter_context(nc.psum_tensor("psArg", [P, 512], F32))
        psM = ctx.enter_context(nc.psum_tensor("psM", [P, 512], F32))
        psY = ctx.enter_context(nc.psum_tensor("psY", [P, DIN], F32))
        psX = ctx.enter_context(nc.psum_tensor("psX", [P, DIN], F32))
        psMb = psM[:, :].bitcast(BF16)
        DA, CSB, WD, E1, D2, SS, QQ, PP, MX = range(9)
        R1, R2 = MX, SS
        DTV, ECS, WEND, ETOT = range(4)

        U = 18
        peA = Count(sem("pe_a"), [f"u{n}" for n in range(U)])
        dveA = Count(sem("dve_a"), ["halo", "gn"] + ["st0", "mv0", "st1", "mv1", "tn0", "st2", "mv2", "tn1", "st3", "mv3", "tn2", "tn3", "dtu"]
                     + sum(([f"ca{d}", f"cb{d}", f"cc{d}"] + ([f"xs{d-1}"] if d else []) for d in range(ND)), []) + ["xsB", "xsC"])
        actA = Count(sem("act_a"), [f"xn{k}" for k in range(KC)] + sum(([f"raw{d}", f"cv{d}"] + ([f"th{d-1}"] if d else []) for d in range(ND)), []) + [f"th{ND-1}"])
        poolA = Count(sem("pool_a"), sum(([f"ve{c}", f"r{c}"] for c in range(CH)), []))
        stepsP = ["p1", "p2", "p3", "p4"]
        stepsB = []
        for c in range(CH):
            stepsB += [(f"s{i}", c) for i in range(1, 7)] + [("s0", c + 1)] * (c + 1 < CH) + [("s7", c), ("s8", c)]

        def names(**per):
            return [f"{x}_{c}" for s, c in stepsB for x in per.get(s, "").split()]
        peP = Count(sem("pe_p"), ["cs", "tr3", "z"])
        dveP = Count(sem("dve_p"), "mx d2 rc s q p15 p13 p11 p9 p7 p5 p3 p1 dt da csb w hi r1 mid r2 lo csT csN zs".split())
        actP = Count(sem("act_p"), "abs e etot ecs wend th".split())
        poolP = Count(sem("pool_p"), ["s0"])
        peB = Count(sem("pe_b"), names(s0="z", s1="a0 xt", s2="gb a1", s3="yoff a2", s4="yd0 a3", s5="yd1 yd2 st yd3", s7="yT", s8="out"))
        dveB = Count(sem("dve_b"), names(s0="zs", s1="xdt dx", s2="gm bt m0", s3="yo m1", s4="m2", s5="m3 s y1", s8="o1 o2"))
        actB = Count(sem("act_b"), names(s0="th", s1="n0 e0", s2="n1 e1", s3="n2 e2", s4="n3 e3", s6="sq", s7="yT"))
        poolB = Count(sem("pool_b"), names(s3="xw", s4="sdec t2", s6="yg", s7="ve r"))
        xc_in = sem("xc_in")
        xres_in = [sem(f"xres_in{i}") for i in range(2)]
        t1_out = [sem(f"t1_out{i}") for i in range(2)]

        after = {("s1", 0): [0], ("s2", 0): [1], ("s3", 0): [2], ("s4", 0): [3], ("s7", 0): [4, 5],
                 ("s1", 1): [6], ("s2", 1): [7], ("s4", 1): [8], ("s7", 1): [9],
                 ("s1", 2): [10], ("s2", 2): [11], ("s4", 2): [12], ("s6", 2): ["p1"], ("s7", 2): [13],
                 ("s1", 3): [14], ("s4", 3): [15], ("s5", 3): ["p2", 16], ("s6", 3): ["p3", 17, 18, "p4"]}

        def walk(engine, stage_a, stage_p, stage_b, before=None):
            if before:
                before()
            for n in ["norm"] + list(range(U + 1)):
                stage_a(0, 0, n)
            for s in stepsP:
                stage_p(0, 0, s)

            def step(t, p, last):
                if not last:
                    stage_a(t + 1, 1 - p, "norm")
                for s, c in stepsB:
                    stage_b(t, p, s, c)
                    for x in [] if last else after.get((s, c), []):
                        stage_p(t + 1, 1 - p, x) if x in stepsP else stage_a(t + 1, 1 - p, x)
            with engine.Fori(0, NB - 1) as b:
                step(b * 2, 0, False)
                step(b * 2 + 1, 1, False)
            step(NBLK - 2, 0, False)
            step(NBLK - 1, 1, True)

        x_ch, x_tok, t1 = io["x_ch"], io["x_tok"], io["t1"]

        def half(t, p):
            return (t - p) // 2

        with nc.Block() as block:
            @block.sync
            def _(sp):
                def load_x(t, p):
                    sp.dma_start(xc[:, :, :], x_ch[bass.ds(half(t, p), 1), :, p * BLK:(p + 1) * BLK].rearrange("b (k p) n -> p (b k) n", p=P)).then_inc(xc_in, 16)

                def before():
                    load_x(0, 0)
                    for i in range(2):
                        sp.dma_start(xres[:, i], x_tok[i]).then_inc(t1_out[i], 16)

                def load_res(t, c):
                    sp.wait_ge(t1_out[c % 2], (t * 2 + c // 2 + 1) * 16)
                    sp.dma_start(xres[:, c % 2], x_tok[bass.ds(t * CH + c, 1)].rearrange("a p n -> p (a n)")).then_inc(xres_in[c % 2], 16)

                def stage_p(t, p, s):
                    if s == "p1" and not (isinstance(t, int) and t + 1 >= NBLK):
                        peA.wait(sp, t, "u3")
                        load_x(t + 1, 1 - p)
                    if s == "p4":
                        load_res(t, 0)

                def stage_b(t, p, s, c):
                    if s == "s0":
                        load_res(t, c)
                    if s == "s8":
                        dveB.wait(sp, t, f"o2_{c}")
                        sp.dma_start(t1[bass.ds(t * CH + c, 1)].rearrange("a p n -> p (a n)"), xres[:, c % 2]).then_inc(t1_out[c % 2], 16)

                walk(sp, lambda t, p, n: None, stage_p, stage_b, before)
                for i in range(2):
                    sp.wait_ge(t1_out[i], 16 * (NBLK * CH // 2 + 1))

            @block.gpsimd
            def _(pool):
                for x in (poolA, poolP, poolB):
                    x.credit(pool)

                def stage_a(t, p, n):
                    if n != "norm" and n < CH:
                        dveA.wait(pool, t, f"mv{n}")
                        if n == 0:
                            dveA.wait(pool, t, "tn3", 1)
                        settle(pool, spare[1])
                        poolA.inc(nc.gpsimd.tensor_scalar(lrs[:, n, 0:1], lmv[:, n, 1:2], 1e-5, None, ALU.add), f"ve{n}")
                        poolA.wait(pool, t, f"ve{n}")
                        poolA.inc(nc.gpsimd.tensor_tensor(lrs[:, n, 1:2], lrs[:, n, 0:1], nhalf[:, :], ALU.pow), f"r{n}")

                def stage_p(t, p, s):
                    if s == "p4":
                        if p == 0:
                            dveB.wait(pool, t, f"s_{CH-1}", 1)
                            peB.wait(pool, t, f"yoff_{CH-1}", 1)
                            settle(pool, spare[1])
                            poolP.inc(nc.gpsimd.memset(st[:, :], 0.0), "s0")
                        else:
                            poolP.inc(nc.gpsimd.memset(junk[:, :], 0.0), "s0")

                def stage_b(t, p, s, c):
                    if s == "s3":
                        actP.wait(pool, t, "wend")
                        dveB.wait(pool, t, f"xdt_{c}")
                        peB.wait(pool, t, f"st_{c-1}") if c else peB.wait(pool, t, f"st_{CH-1}", 1)
                        w = smb[:, p, WEND, c * NH:(c + 1) * NH].unsqueeze(2).to_broadcast([P, NH, HD])
                        poolB.inc(nc.gpsimd.tensor_tensor(xw[:, :].rearrange("p (h d) -> p h d", h=NH), xdt[:, :].rearrange("p (h d) -> p h d", h=NH), w, ALU.mult), f"xw_{c}")
                    if s == "s4":
                        peB.wait(pool, t, f"yoff_{c}")
                        if c:
                            dveB.wait(pool, t, f"s_{c-1}")
                        elif p == 0:
                            poolP.wait(pool, t, "s0")
                        else:
                            dveB.wait(pool, t, f"s_{CH-1}", 1)
                        e = smb[0:NS, p, ETOT, c * NH:(c + 1) * NH].unsqueeze(2).to_broadcast([NS, NH, HD])
                        poolB.inc(nc.gpsimd.tensor_tensor(st[:, :].rearrange("p (h d) -> p h d", h=NH), st[:, :].rearrange("p (h d) -> p h d", h=NH), e, ALU.mult), f"sdec_{c}")
                        dveB.wait(pool, t, f"yo_{c}")
                        poolB.inc(nc.gpsimd.tensor_tensor(yo[:, :], yo[:, :], dx[:, :], ALU.add), f"t2_{c}")
                    if s == "s6":
                        dveB.wait(pool, t, f"y1_{c}")
                        poolB.inc(nc.gpsimd.tensor_tensor(yo[:, :], yo[:, :], zs[:, :], ALU.mult), f"yg_{c}")
                    if s == "s7":
                        actB.wait(pool, t, f"sq_{c}")
                        settle(pool, spare[1])
                        poolB.inc(nc.gpsimd.tensor_scalar(rr[:, 1:2], rr[:, 0:1], 1.0 / DIN, 1e-5, ALU.mult, ALU.add), f"ve_{c}")
                        poolB.wait(pool, t, f"ve_{c}")
                        dveB.wait(pool, t, f"o1_{c-1}") if c else dveB.wait(pool, t, f"o1_{CH-1}", 1)
                        poolB.inc(nc.gpsimd.tensor_tensor(rr[:, 2:3], rr[:, 1:2], nhalf[:, :], ALU.pow), f"r_{c}")

                walk(pool, stage_a, stage_p, stage_b)

            @block.tensor
            def _(pe):
                for x in (peA, peP, peB):
                    x.credit(pe)

                def free_a(t, n):
                    m, back = (n - 2, 0) if n >= 2 else (n - 2 + U, 1)
                    if m < CH:
                        dveA.wait(pe, t, f"tn{m}", back)
                    elif m < 2 * CH:
                        actA.wait(pe, t, f"xn{m - CH}", back)
                    elif m == 2 * CH:
                        dveA.wait(pe, t, "dtu", back)
                    else:
                        actA.wait(pe, t, f"cv{m - 2 * CH - 1}", back)

                def stage_a(t, p, n):
                    if n in ("norm", U):
                        return
                    bank = psA[n % 2]
                    free_a(t, n)
                    if n < CH:
                        if n == 0:
                            dveA.wait(pe, t, "gn")
                        for k in range(KC):
                            mm = nc.tensor.transpose(bank[:, k * P:(k + 1) * P], xc[:, k, n * P:(n + 1) * P], ident[:, :])
                    elif n < 2 * CH:
                        k = n - CH
                        if k == 0:
                            dveA.wait(pe, t, "tn3")
                        for c in range(CH):
                            mm = nc.tensor.transpose(bank[:, c * P:(c + 1) * P], tn[:, c, k * P:(k + 1) * P], ident[:, :])
                    elif n > 2 * CH:
                        d = n - 2 * CH - 1
                        for k in range(KC):
                            mm = nc.tensor.matmul(bank[:, :], win[:, k, DIN + d * P:DIN + (d + 1) * P], xn[:, p, k, :], start=(k == 0), stop=(k == KC - 1))
                    else:
                        actA.wait(pe, t, f"xn{KC-1}")
                        for c in range(CH):
                            for k in range(KC):
                                mm = nc.tensor.matmul(bank[:, c * NH:(c + 1) * NH], xn[:, p, k, c * P:(c + 1) * P], win[:, k, DIN + DXBC:],
                                                      start=(k == 0), stop=(k == KC - 1))
                    peA.inc(mm, f"u{n}")

                def args(t, p, c, g):
                    j, i = csN[:, p, c * P:(c + 1) * P], csT[:, p, c * P:(c + 1) * P]
                    nc.tensor.matmul(psArg[:, :], j, sel[:, g * 512:(g + 1) * 512], start=True, stop=False, skip_group_check=True)
                    for h in range(4):
                        mm = nc.tensor.matmul(psArg[:, h * P:(h + 1) * P], sel[:, (4 * g + h) * P:(4 * g + h + 1) * P], i, start=False, stop=True, skip_group_check=True)
                    peB.inc(mm, f"a{g}_{c}")

                def ydiag(t, c, g):
                    dveB.wait(pe, t, f"m{g}_{c}")
                    if g == 0:
                        actB.wait(pe, t, f"yT_{c-1}") if c else actB.wait(pe, t, f"yT_{CH-1}", 1)
                    for h in range(4):
                        hh = 4 * g + h
                        mm = nc.tensor.matmul(psY[:, hh * HD:(hh + 1) * HD], ms[:, g % 2, h * P:(h + 1) * P], xdt[:, hh * HD:(hh + 1) * HD], start=True, stop=True)
                    peB.inc(mm, f"yd{g}_{c}")

                def z_of(t, p, c):
                    for j in range(2):
                        for k in range(KC):
                            mm = nc.tensor.matmul(psX[:, j * 512:(j + 1) * 512], xn[:, p, k, c * P:(c + 1) * P], win[:, k, j * 512:(j + 1) * 512], start=(k == 0), stop=(k == KC - 1))
                    return mm

                def stage_p(t, p, s):
                    if s == "p2":
                        dveP.wait(pe, t, "da")
                        dveB.wait(pe, t, f"m0_{CH-1}", 1)
                        nc.tensor.matmul(psM[:, 0:64], tri[:, :], sm[:, DA, :], start=True, stop=True)
                        mm = nc.tensor.matmul(psM[:, 64:128], ones[:, :], sm[:, DA, :], start=True, stop=True)
                        peP.inc(mm, "cs")
                    if s == "p3":
                        dveP.wait(pe, t, "lo")
                        actP.wait(pe, t, "etot")
                        settle(pe, spare[2])
                        for q in range(CH):
                            mm = nc.tensor.transpose(psMb[0:48, q * P:(q + 1) * P], sp3[:, q, :], identb[:, :])
                        peP.inc(mm, "tr3")
                    if s == "p4":
                        dveP.wait(pe, t, "csN")
                        dveB.wait(pe, t, f"s_{CH-1}", 1)
                        peP.inc(z_of(t, p, 0), "z")

                def stage_b(t, p, s, c):
                    tok = slice(c * P, (c + 1) * P)
                    Bc, Cc = bcm[:, p, 0, tok], bcm[:, p, 1, tok]
                    if s == "s0":
                        dveB.wait(pe, t, f"s_{c-1}")
                        peB.inc(z_of(t, p, c), f"z_{c}")
                    if s == "s1":
                        if c == 0:
                            dveA.wait(pe, t, "xsC")
                        actB.wait(pe, t, f"n3_{c-1}") if c else actB.wait(pe, t, f"n3_{CH-1}", 1)
                        args(t, p, c, 0)
                        dveB.wait(pe, t, f"zs_{c}") if c else dveP.wait(pe, t, "zs")
                        for d in range(DIN // P):
                            mm = nc.tensor.transpose(psX[:, d * P:(d + 1) * P], xs[:, p, d, tok], ident[:, :])
                        peB.inc(mm, f"xt_{c}")
                    if s == "s2":
                        dveB.wait(pe, t, f"o1_{c-1}") if c else dveB.wait(pe, t, f"o1_{CH-1}", 1)
                        nc.tensor.matmul(psM[:, 0:P], Bc, Cc, start=True, stop=True)
                        peB.inc(nc.tensor.transpose(psM[:, P:P + NS], Bc, ident[0:NS, 0:NS]), f"gb_{c}")
                        actB.wait(pe, t, f"n0_{c}")
                        args(t, p, c, 1)
                    if s == "s3":
                        dveB.wait(pe, t, f"dx_{c}")
                        if c:
                            dveB.wait(pe, t, f"s_{c-1}")
                        elif p == 0:
                            poolP.wait(pe, t, "s0")
                        else:
                            dveB.wait(pe, t, f"s_{CH-1}", 1)
                        for j in range(2):
                            mm = nc.tensor.matmul(psX[:, j * 512:(j + 1) * 512], Cc, st[:, j * 512:(j + 1) * 512], start=True, stop=True)
                        peB.inc(mm, f"yoff_{c}")
                        actB.wait(pe, t, f"n1_{c}")
                        args(t, p, c, 2)
                    if s == "s4":
                        ydiag(t, c, 0)
                        actB.wait(pe, t, f"n2_{c}")
                        args(t, p, c, 3)
                    if s == "s5":
                        ydiag(t, c, 1)
                        ydiag(t, c, 2)
                        dveB.wait(pe, t, f"yo_{c}")
                        poolB.wait(pe, t, f"xw_{c}")
                        for j in range(2):
                            mm = nc.tensor.matmul(psX[0:NS, j * 512:(j + 1) * 512], bt[:, :], xw[:, j * 512:(j + 1) * 512], start=True, stop=True)
                        peB.inc(mm, f"st_{c}")
                        ydiag(t, c, 3)
                    if s == "s7":
                        poolB.wait(pe, t, f"yg_{c}")
                        for d in range(DIN // P):
                            mm = nc.tensor.transpose(psY[:, d * P:(d + 1) * P], yo[:, d * P:(d + 1) * P], ident[:, :])
                        peB.inc(mm, f"yT_{c}")
                    if s == "s8":
                        actB.wait(pe, t, f"yT_{c}")
                        for d in range(DIN // P):
                            mm = nc.tensor.matmul(psM[:, :], yT[:, d, :], wc[:, d, :], start=(d == 0), stop=(d == DIN // P - 1))
                        peB.inc(mm, f"out_{c}")

                walk(pe, stage_a, stage_p, stage_b)

            @block.scalar
            def _(act):
                for x in (actA, actP, actB):
                    x.credit(act)

                def tanh_a(t, p, d):
                    dveA.wait(act, t, f"cc{d}")
                    if d == 0:
                        peB.wait(act, t, f"xt_{CH-1}", 2)
                    if d == ND - 1:
                        dveA.wait(act, t, "xsC", 1)
                    out = xs[:, p, d, :] if d < ND - 1 else tha[:, :]
                    actA.inc(nc.scalar.activation(out, cv[:, d % 2], ACT.Tanh), f"th{d}")

                def stage_a(t, p, n):
                    if n == "norm" or n < CH or n == 2 * CH:
                        return
                    bank = psA[n % 2]
                    if n < 2 * CH:
                        k = n - CH
                        if k == 0:
                            peB.wait(act, t, f"z_{CH-1}", 2)
                        peA.wait(act, t, f"u{n}")
                        actA.inc(nc.scalar.activation(xn[:, p, k, :], bank[:, :], ACT.Identity, bias=lnb[:, k:k + 1], scale=lnw[:, k:k + 1]), f"xn{k}")
                    elif n < U:
                        d = n - 2 * CH - 1
                        peA.wait(act, t, f"u{n}")
                        dveA.wait(act, t, "halo")
                        actA.inc(nc.scalar.activation(raw[:, d, 3:], bank[:, :], ACT.Identity), f"raw{d}")
                        if d < 2:
                            dveA.wait(act, t, "xsC" if d == 0 else f"xs{ND-2}", 1)
                        else:
                            dveA.wait(act, t, f"xs{d-2}")
                        actA.inc(nc.scalar.activation(cv[:, d % 2], bank[:, :], ACT.Identity, bias=cb[:, d:d + 1], scale=cw[:, d, 3:4]), f"cv{d}")
                        if d:
                            tanh_a(t, p, d - 1)
                    else:
                        tanh_a(t, p, ND - 1)

                def exps(t, c, g):
                    peB.wait(act, t, f"a{g}_{c}")
                    if g >= 2:
                        dveB.wait(act, t, f"m{g-2}_{c}")
                    actB.inc(nc.scalar.activation(es[:, g % 2], psArg[:, :], ACT.Relu, scale=-1.0), f"n{g}_{c}")
                    actB.wait(act, t, f"n{g}_{c}")
                    actB.inc(nc.scalar.activation(es[:, g % 2], es[:, g % 2], ACT.Exp, scale=-1.0), f"e{g}_{c}")

                def stage_p(t, p, s):
                    if s == "p1":
                        dveA.wait(act, t, "dtu")
                        dveP.wait(act, t, "s", 1)
                        actP.inc(nc.scalar.activation(sm[:, E1, :], dtu[:, p], ACT.Abs), "abs")
                        actP.wait(act, t, "abs")
                        actP.inc(nc.scalar.activation(sm[:, E1, :], sm[:, E1, :], ACT.Exp, scale=-1.0), "e")
                    if s == "p2":
                        peP.wait(act, t, "cs")
                        actP.inc(nc.scalar.activation(smb[:, p, ETOT, :], psM[:, 64:128], ACT.Exp), "etot")
                        dveP.wait(act, t, "csb")
                        actP.inc(nc.scalar.activation(smb[:, p, ECS, :], sm[:, CSB, :], ACT.Exp), "ecs")
                        dveP.wait(act, t, "w")
                        actP.inc(nc.scalar.activation(smb[:, p, WEND, :], sm[:, WD, :], ACT.Exp), "wend")
                    if s == "p4":
                        peP.wait(act, t, "z")
                        actB.wait(act, t, f"sq_{CH-1}", 1)
                        actP.inc(nc.scalar.activation(th[:, :], psX[:, :], ACT.Tanh), "th")

                def stage_b(t, p, s, c):
                    if s == "s0":
                        peB.wait(act, t, f"z_{c}")
                        actB.wait(act, t, f"sq_{c-1}")
                        actB.inc(nc.scalar.activation(th[:, :], psX[:, :], ACT.Tanh), f"th_{c}")
                    if s in ("s1", "s2", "s3", "s4"):
                        exps(t, c, int(s[1]) - 1)
                    if s == "s6":
                        poolB.wait(act, t, f"yg_{c}")
                        actB.inc(nc.scalar.activation(th[:, :], yo[:, :], ACT.Square, accum_out=rr[:, 0:1]), f"sq_{c}")
                    if s == "s7":
                        peB.wait(act, t, f"yT_{c}")
                        actB.inc(nc.scalar.activation(yT[:, :, :].rearrange("p a b -> p (a b)"), psY[:, :], ACT.Identity), f"yT_{c}")

                walk(act, stage_a, stage_p, stage_b)

            @block.vector
            def _(v):
                for x in (dveA, dveP, dveB):
                    x.credit(v)

                def norm_tok(t, c):
                    poolA.wait(v, t, f"r{c}")
                    dveA.wait(v, t, f"mv{c}")
                    if c == 0:
                        peA.wait(v, t, f"u{2*CH-1}", 1)
                    dveA.inc(nc.vector.tensor_scalar(tn[:, c, :], psA[c % 2][:, :], lmv[:, c, 0:1], lrs[:, c, 1:2], ALU.subtract, ALU.mult), f"tn{c}")

                def silu_a(t, p, d):
                    actA.wait(v, t, f"th{d}")
                    if d < ND - 1:
                        dveA.inc(nc.vector.scalar_tensor_tensor(xs[:, p, d, :], xs[:, p, d, :], 1.0, cv[:, d % 2], ALU.add, ALU.mult), f"xs{d}")
                    else:
                        peB.wait(v, t, f"yoff_{CH-1}", 2)
                        for j, x in enumerate("BC"):
                            q = slice(j * NS, (j + 1) * NS)
                            dveA.inc(nc.vector.scalar_tensor_tensor(bcm[:, p, j, :], tha[q, :], 1.0, cv[q, d % 2], ALU.add, ALU.mult), f"xs{x}")

                def stage_a(t, p, n):
                    if n == "norm":
                        if p == 0:
                            dveA.inc(nc.vector.memset(raw[:, :, 0:3], 0.0), "halo")
                        else:
                            actA.wait(v, t, f"raw{ND-1}", 1)
                            dveA.inc(nc.vector.tensor_copy(raw[:, :, 0:3], raw[:, :, BLK:BLK + 3]), "halo")
                        v.wait_ge(xc_in, t * 16 + 16)
                        for k in range(KC):
                            ins = nc.vector.tensor_scalar(xc[:, k, :], xc[:, k, :], gnab[:, 0, bass.ds(half(t, p), 1), k],
                                                          gnab[:, 1, bass.ds(half(t, p), 1), k], ALU.mult, ALU.add)
                        dveA.inc(ins, "gn")
                    elif n < CH:
                        peA.wait(v, t, f"u{n}")
                        if n:
                            dveA.wait(v, t, f"mv{n-1}")
                        dveA.inc(nc.vector.bn_stats(lst[:, :], psA[n % 2][:, :]), f"st{n}")
                        dveA.wait(v, t, f"st{n}")
                        settle(v, spare[0])
                        dveA.inc(nc.vector.bn_aggr(lmv[:, n, :], lst[:, :]), f"mv{n}")
                        if n:
                            norm_tok(t, n - 1)
                    elif n == CH:
                        norm_tok(t, CH - 1)
                    elif n < 2 * CH:
                        pass
                    elif n == 2 * CH:
                        peA.wait(v, t, f"u{n}")
                        actP.wait(v, t, "abs", 2)
                        dveP.wait(v, t, "mx", 2)
                        dveA.inc(nc.vector.tensor_tensor(dtu[:, p], psA[n % 2][:, 0:CH * NH], dtb[:, :, :].rearrange("p c h -> p (c h)"), ALU.add), "dtu")
                    elif n < U:
                        d = n - 2 * CH - 1
                        actA.wait(v, t, f"cv{d}")
                        for j, x in enumerate("abc"):
                            if j:
                                dveA.wait(v, t, f"c{'abc'[j-1]}{d}")
                            dveA.inc(nc.vector.scalar_tensor_tensor(cv[:, d % 2], raw[:, d, j:j + BLK], cw[:, d, j:j + 1], cv[:, d % 2], ALU.mult, ALU.add), f"c{x}{d}")
                        if d:
                            silu_a(t, p, d - 1)
                    else:
                        silu_a(t, p, ND - 1)

                def tt(t, name, out, a, b, op):
                    dveP.inc(nc.vector.tensor_tensor(out, a, b, op), name)
                    dveP.wait(v, t, name)

                def mask(t, c, g):
                    actB.wait(v, t, f"e{g}_{c}")
                    if g >= 2:
                        peB.wait(v, t, f"yd{g-2}_{c}")
                    elif c:
                        peB.wait(v, t, f"yd{g+2}_{c-1}")
                    else:
                        peB.wait(v, t, f"yd{g+2}_{CH-1}", 1)
                    dveB.inc(nc.vector.tensor_tensor(ms[:, g % 2].rearrange("p (h i) -> p h i", h=4), es[:, g % 2].rearrange("p (h i) -> p h i", h=4),
                                                     gm[:, :].unsqueeze(1).to_broadcast([P, 4, P]), ALU.mult), f"m{g}_{c}")

                def heads(x):
                    return x.rearrange("p (h d) -> p h d", h=NH)

                def stage_p(t, p, s):
                    S = lambda i: sm[:, i, :]
                    if s == "p1":
                        dveA.wait(v, t, "dtu")
                        dveP.inc(nc.vector.tensor_scalar(S(MX), dtu[:, p], 0.0, None, ALU.max), "mx")
                        actP.wait(v, t, "e")
                        dveP.inc(nc.vector.tensor_scalar(S(D2), S(E1), 2.0, None, ALU.add), "d2")
                        dveP.wait(v, t, "d2")
                        dveP.inc(nc.vector.reciprocal(S(D2), S(D2)), "rc")
                        dveP.wait(v, t, "rc")
                        tt(t, "s", S(SS), S(E1), S(D2), ALU.mult)
                        tt(t, "q", S(QQ), S(SS), S(SS), ALU.mult)
                        dveP.inc(nc.vector.tensor_scalar(S(PP), S(QQ), 1.0 / 15, None, ALU.mult), "p15")
                        for i in (13, 11, 9, 7, 5, 3):
                            dveP.wait(v, t, f"p{i+2}")
                            dveP.inc(nc.vector.scalar_tensor_tensor(S(PP), S(PP), 1.0 / i, S(QQ), ALU.add, ALU.mult), f"p{i}")
                        dveP.wait(v, t, "p3")
                        dveP.inc(nc.vector.scalar_tensor_tensor(S(PP), S(PP), 1.0, S(SS), ALU.add, ALU.mult), "p1")
                        dveP.wait(v, t, "p1")
                        dveP.inc(nc.vector.scalar_tensor_tensor(smb[:, p, DTV, :], S(PP), 2.0, S(MX), ALU.mult, ALU.add), "dt")
                        dveP.wait(v, t, "dt")
                        tt(t, "da", S(DA), smb[:, p, DTV, :], abc[:, :, :].rearrange("p c h -> p (c h)"), ALU.mult)
                    if s == "p2":
                        peP.wait(v, t, "cs")
                        actP.wait(v, t, "ecs", 1)
                        actP.wait(v, t, "etot")
                        dveP.inc(nc.vector.tensor_copy(S(CSB), psM[:, 0:64]), "csb")
                        dveP.wait(v, t, "csb")
                        actP.wait(v, t, "wend", 1)
                        dveP.inc(nc.vector.tensor_tensor(S(WD), psM[:, 64:128], S(CSB), ALU.subtract), "w")
                        parts = lambda i: sp3[:, :, i * NH:(i + 1) * NH]
                        ch = lambda x: x.rearrange("p (c h) -> p c h", c=CH)
                        dveP.inc(nc.vector.tensor_copy(parts(0), ch(S(CSB))), "hi")
                        dveP.wait(v, t, "hi")
                        tt(t, "r1", ch(S(R1)), ch(S(CSB)), parts(0), ALU.subtract)
                        dveP.inc(nc.vector.tensor_copy(parts(1), ch(S(R1))), "mid")
                        dveP.wait(v, t, "mid")
                        tt(t, "r2", ch(S(R2)), ch(S(R1)), parts(1), ALU.subtract)
                        dveP.inc(nc.vector.tensor_copy(parts(2), ch(S(R2))), "lo")
                    if s == "p3":
                        peP.wait(v, t, "tr3")
                        dveP.inc(nc.vector.tensor_copy(csT[:, p], psMb[0:48, 0:CH * P]), "csT")
                        dveP.inc(nc.vector.tensor_scalar(csN[:, p], psMb[0:48, 0:CH * P], -1.0, None, ALU.mult), "csN")
                    if s == "p4":
                        actP.wait(v, t, "th")
                        poolB.wait(v, t, f"yg_{CH-1}", 1)
                        dveP.inc(nc.vector.scalar_tensor_tensor(zs[:, :], th[:, :], 1.0, psX[:, :], ALU.add, ALU.mult), "zs")

                def stage_b(t, p, s, c):
                    if s == "s0":
                        actB.wait(v, t, f"th_{c}")
                        poolB.wait(v, t, f"yg_{c-1}")
                        dveB.inc(nc.vector.scalar_tensor_tensor(zs[:, :], th[:, :], 1.0, psX[:, :], ALU.add, ALU.mult), f"zs_{c}")
                    if s == "s1":
                        peB.wait(v, t, f"xt_{c}")
                        d = smb[:, p, DTV, c * NH:(c + 1) * NH].unsqueeze(2).to_broadcast([P, NH, HD])
                        dveB.inc(nc.vector.tensor_tensor(heads(xdt[:, :]), heads(psX[:, :]), d, ALU.mult), f"xdt_{c}")
                        poolB.wait(v, t, f"t2_{c-1}") if c else poolB.wait(v, t, f"t2_{CH-1}", 1)
                        dveB.inc(nc.vector.tensor_tensor(heads(dx[:, :]), heads(psX[:, :]), dbc[:, :].unsqueeze(2).to_broadcast([P, NH, HD]), ALU.mult), f"dx_{c}")
                    if s == "s2":
                        peB.wait(v, t, f"gb_{c}")
                        dveB.inc(nc.vector.tensor_tensor(gm[:, :], psM[:, 0:P], tri[:, :], ALU.mult), f"gm_{c}")
                        dveB.inc(nc.vector.tensor_copy(bt[:, :], psM[:, P:P + NS]), f"bt_{c}")
                        dveB.wait(v, t, f"gm_{c}")
                        mask(t, c, 0)
                    if s == "s3":
                        peB.wait(v, t, f"yoff_{c}")
                        actP.wait(v, t, "ecs")
                        peB.wait(v, t, f"yT_{c-1}") if c else peB.wait(v, t, f"yT_{CH-1}", 1)
                        actB.wait(v, t, f"sq_{c-1}") if c else actB.wait(v, t, f"sq_{CH-1}", 1)
                        e = smb[:, p, ECS, c * NH:(c + 1) * NH].unsqueeze(2).to_broadcast([P, NH, HD])
                        dveB.inc(nc.vector.tensor_tensor(heads(yo[:, :]), heads(psX[:, :]), e, ALU.mult), f"yo_{c}")
                        mask(t, c, 1)
                    if s == "s4":
                        mask(t, c, 2)
                    if s == "s5":
                        mask(t, c, 3)
                        peB.wait(v, t, f"st_{c}")
                        poolB.wait(v, t, f"sdec_{c}")
                        dveB.inc(nc.vector.tensor_tensor(st[:, :], psX[0:NS, :], st[:, :], ALU.add), f"s_{c}")
                        peB.wait(v, t, f"yd3_{c}")
                        poolB.wait(v, t, f"t2_{c}")
                        dveB.inc(nc.vector.tensor_tensor(yo[:, :], psY[:, :], yo[:, :], ALU.add), f"y1_{c}")
                    if s == "s8":
                        peB.wait(v, t, f"out_{c}")
                        poolB.wait(v, t, f"r_{c}")
                        dveB.inc(nc.vector.scalar_tensor_tensor(o1[:, :], psM[:, :], rr[:, 2:3], bias_bc[:, :], ALU.mult, ALU.add), f"o1_{c}")
                        dveB.wait(v, t, f"o1_{c}")
                        v.wait_ge(xres_in[c % 2], (t * 2 + c // 2 + 1) * 16)
                        dveB.inc(nc.vector.scalar_tensor_tensor(xres[:, c % 2], o1[:, :], 0.0, xres[:, c % 2], ALU.max, ALU.add), f"o2_{c}")

                walk(v, stage_a, stage_p, stage_b)


def attention(nc, io, consts):
    ctx = ExitStack()
    with ctx:
        def sb(name, shape, dt=F32):
            return ctx.enter_context(nc.sbuf_tensor(name, shape, dt))

        def sem(name):
            return ctx.enter_context(nc.semaphore(name))

        NC8 = L // P
        RB = 4
        HQ = C // HD
        KV = 256
        wh = sb("wh", [P, KC, C + 2 * KV], F32R)
        wl = sb("wl", [P, KC, C + 2 * KV], F32R)
        wo = sb("wo_t", [P, KC, C])
        wr = sb("wr", [P, KC, E])
        br = sb("br", [P, E])
        g = sb("g", [P, KC])
        ag = sb("ag", [P, 2, KC])
        nhalf = sb("nhalf2", [P, 1])
        headof = sb("headof", [P, KC, HQ])
        headsel = sb("headsel", [HQ, C])
        headselr = sb("headselr", [HQ, C], F32R)
        dup = sb("dup", [P, 2, P])
        tb = sb("tb", [P, 2, NC8, C])
        hb = sb("hb", [P, CH, C])
        hTh = sb("hTh", [P, 2, KC, BLK], F32R)
        hTl = sb("hTl", [P, 2, KC, BLK], F32R)
        q = sb("q", [P, 2, KC, L])
        wq, wk, wv = q[:, 0, :, 0:C], q[:, 1, :, 0:KV], q[:, 1, :, KV:2 * KV]
        er = sb("er", [P, 2, BLK])
        kf = sb("kf", [P, 2, BLK])
        kvj = sb("kvj", [P, BLK])
        ks = sb("ks", [P, 2, 2])
        kv = sb("kv", [P, 2, 2])
        kk = sb("kk", [P, 2, 2])
        kd = sb("kd", [P, KC, 2])
        kb = sb("kb", [P, 2, KC, HQ])
        wop = sb("wop", [P, 2, KC, C])
        zr = sb("zr", [HQ, BLK])
        zh = sb("zh", [HQ, BLK], F32R)
        zl = sb("zl", [HQ, BLK], F32R)
        st6 = sb("st6", [P, CH, 6])
        mv = sb("mvq", [P, CH, 2])
        rs = sb("rsq", [P, CH, 2])
        st1 = sb("st1", [P, 6])
        mv1 = sb("mv1", [P, 4, 2])
        rs1 = sb("rs1", [P, 4, 2])
        xrow = sb("xrow", [P, RB, ROW])
        xT = sb("xTr", [P, 2, KC * P])
        lg = sb("lg", [P, E])
        sx = sb("sx", [P, 4])
        pall = consts["probs"][:, :].rearrange("p (r a e) -> p r a e", a=4, e=E)
        psA = [ctx.enter_context(nc.psum_tensor(f"qA{i}", [P, 512], F32)) for i in range(2)]
        psZ = [ctx.enter_context(nc.psum_tensor(f"qZ{i}", [P, 512], F32)) for i in range(2)]
        psO = [ctx.enter_context(nc.psum_tensor(f"qO{i}", [P, 512], F32)) for i in range(2)]
        psT = [ctx.enter_context(nc.psum_tensor(f"qT{i}", [P, 512], F32)) for i in range(2)]
        spare = [sem(f"spareq{i}") for i in range(3)]
        w_in, s_act, s_pool, s_split = sem("wq_in"), sem("fold_act"), sem("fold_pool"), sem("fold_dve")
        tb_in = [[sem(f"tb_in{i}{h}") for h in range(2)] for i in range(2)]
        y_out = [sem(f"y_out{h}") for h in range(2)]
        row_out = [sem(f"row_out{i}") for i in range(RB)]
        p_out = sem("p_out")

        UH = 12
        U = 2 * UH
        hs = range(2)
        peA = Count(sem("pe_qa"), [f"u{n}" for n in range(U)])
        dveA = Count(sem("dve_qa"), ["st_0", "mv_0", "hb_0"] + [f"hl{k}_0" for k in range(KC)] + ["st_1", "mv_1", "hb_1"]
                     + sum(([f"hl{k}_1" for k in range(KC)] * h + [f"{x}{m}_{h}" for m in range(6) for x in ("c", "f")] + [f"v{m}_{h}" for m in range(2)] for h in hs), []))
        actA = Count(sem("act_qa"), sum(([f"hT{k}_{h}" for k in range(KC)] + [f"{x}{m}_{h}" for m in range(6) for x in ("n", "e")] for h in hs), []))
        poolA = Count(sem("pool_qa"), sum(([f"ve_{h}", f"r_{h}"] for h in hs), []))
        zs = [(h, k) for h in hs for k in range(KC)]
        stepsP = [("prep", 0), ("z", 0)] + [("w", i) for i in range(KC)]
        stepsB = []
        for c in range(NC8 + 3):
            stepsB += [("o", c)] * (c < NC8) + [("z", 1)] * (c == 0) + [("w", KC + 2 * c - 2), ("w", KC + 2 * c - 1)] * (c in (1, 2)) + [("x", c - 2)] * (2 <= c < NC8 + 2) + [("r", c - 3)] * (c >= 3)

        def names(steps, **per):
            return [f"{x}_{i}" for s, i in steps for x in per.get(s, "").split()]
        peP = Count(sem("pe_qp"), names(stepsP, prep="dup", z="z", w="w"))
        dveP = Count(sem("dve_qp"), names(stepsP, prep="kk0 kk1 kd kb wop", z="ze zr zh zl", w="y"))
        peB = Count(sem("pe_qb"), names(stepsB, z="z", w="w", o="o", x="xt", r="rt"))
        dveB = Count(sem("dve_qb"), names(stepsB, z="ze zr zh zl", w="y", o="t2 st mv", x="xn", r="lg mx nm rc p pa"))
        actB = Count(sem("act_qb"), names(stepsB, x="xT", r="ex"))
        poolB = Count(sem("pool_qb"), names(stepsB, o="ve r"))

        def dve_w(i):
            return dveP if i < KC else dveB
        stepsA = [("n", 0)] + [("u", i) for i in range(4)] + [("n", 1)] + [("u", i) for i in range(4, U)]
        after, at = {}, 0
        for key, count in ((("o", 0), 1), (("o", 1), 2), (("w", 5), 2), (("o", 2), 3), (("x", 0), 3), (("o", 3), 2), (("x", 1), 3), (("o", 4), 2), (("x", 2), 2),
                           (("o", 5), 3), (("x", 3), 3)):
            after[key] = stepsA[at:at + count]
            at += count
        assert at == len(stepsA)
        after |= {("o", 6): stepsP[0:1], ("x", 4): stepsP[1:2], ("x", 5): stepsP[2:4], ("x", 6): stepsP[4:6]}

        def walk(engine, stage_a, stage_p, stage_b, before=None):
            def take(t, p, s, i):
                {"n": stage_a, "u": stage_a}.get(s, stage_p)(t, p, s, i)
            if before:
                before()
            for s, i in stepsA + stepsP:
                take(0, 0, s, i)

            def step(t, p, last):
                for s, i in stepsB:
                    stage_b(t, p, s, i)
                    for x in [] if last else after.get((s, i), []):
                        take(t + 1, 1 - p, *x)
            with engine.Fori(0, NB // 2 - 1) as b:
                step(b * 2, 0, False)
                step(b * 2 + 1, 1, False)
            step(NB - 2, 0, False)
            step(NB - 1, 1, True)

        t1, y, table = io["t1"], io["y"], io["table"]
        with nc.Block() as block:
            loads = [(wq, io["wq_t"].rearrange("(k p) d -> p k d", p=P)), (wk, io["wk_t"].rearrange("(k p) d -> p k d", p=P)),
                     (wv, io["wv_t"].rearrange("(k p) d -> p k d", p=P)), (wo[:, :, :], io["wo_t"].rearrange("(k p) d -> p k d", p=P)),
                     (wr[:, :, :], io["wr"].rearrange("(k p) d -> p k d", p=P)), (br[:, :], io["br"].partition_broadcast(P)), (g[:, :], io["g"]),
                     (headof[:, :, :], io["headof"]), (headsel[:, :], io["headsel"]), (dup[:, 0], io["c_dup0"]), (dup[:, 1], io["c_dup1"])]

            @block.sync
            def _(sp):
                def load_t(t, p, h):
                    sp.dma_start(tb[:, p, h * CH:(h + 1) * CH], t1[bass.ds(t * NC8 + h * CH, CH)].rearrange("c p n -> p c n")).then_inc(tb_in[p][h], 16)

                def before():
                    for dst, src in loads:
                        sp.dma_start(dst, src).then_inc(w_in, 16)
                    for t in range(2):
                        for h in hs:
                            load_t(t, t, h)
                    for i in range(RB):
                        sp.dma_start(xrow[:, i, 0:C], t1[i]).then_inc(row_out[i], 16)

                def stage_b(t, p, s, c):
                    if s == "o":
                        dveB.wait(sp, t, f"t2_{c}")
                        sp.dma_start(y[bass.ds(t * NC8 + c, 1)].rearrange("a p n -> p (a n)"), tb[:, p, c]).then_inc(y_out[c // CH], 16)
                    if s == "r":
                        dveB.wait(sp, t, f"p_{c}")
                        sp.dma_start(table[bass.ds(t * NC8 + c, 1)].rearrange("a p n -> p (a n)"), xrow[:, c % RB]).then_inc(row_out[c % RB], 16)
                    if s == "x" and c % CH == CH - 1 and not (isinstance(t, int) and t + 2 >= NB):
                        dveB.wait(sp, t, f"xn_{c}")
                        sp.wait_ge(y_out[c // CH], (t * CH + CH) * 16)
                        load_t(t + 2, p, c // CH)

                nothing = lambda *a: None
                walk(sp, nothing, nothing, stage_b, before)
                for i in range(RB):
                    sp.wait_ge(row_out[i], 16 * (NT // P // RB + 1))
                for h in hs:
                    sp.wait_ge(y_out[h], 16 * NT // P // 2)

            @block.gpsimd
            def _(pool):
                poolA.credit(pool)
                poolB.credit(pool)
                nc.gpsimd.memset(nhalf[:, :], -0.5).then_inc(s_pool, 1)
                pool.wait_ge(s_pool, 1)

                def stage_a(t, p, s, h):
                    if s == "n":
                        dveA.wait(pool, t, f"mv_{h}")
                        dveA.wait(pool, t, "hb_0") if h else dveA.wait(pool, t, "hb_1", 1)
                        settle(pool, spare[0])
                        poolA.inc(nc.gpsimd.tensor_scalar(rs[:, :, 0], mv[:, :, 1], 1.0 + 1e-6, 1e-11, ALU.mult, ALU.add), f"ve_{h}")
                        poolA.wait(pool, t, f"ve_{h}")
                        poolA.inc(nc.gpsimd.tensor_tensor(rs[:, :, 1], rs[:, :, 0], nhalf[:, 0:1].to_broadcast([P, CH]), ALU.pow), f"r_{h}")

                def stage_b(t, p, s, c):
                    if s == "o":
                        dveB.wait(pool, t, f"mv_{c}")
                        settle(pool, spare[0])
                        poolB.inc(nc.gpsimd.tensor_scalar(rs1[:, c % 4, 0:1], mv1[:, c % 4, 1:2], 1e-5, None, ALU.add), f"ve_{c}")
                        poolB.wait(pool, t, f"ve_{c}")
                        poolB.inc(nc.gpsimd.tensor_tensor(rs1[:, c % 4, 1:2], rs1[:, c % 4, 0:1], nhalf[:, :], ALU.pow), f"r_{c}")

                walk(pool, stage_a, lambda *a: None, stage_b)

            @block.tensor
            def _(pe):
                for x in (peA, peP, peB):
                    x.credit(pe)
                pe.wait_ge(w_in, 16 * len(loads))
                pe.wait_ge(s_split, 1)

                def taken(n):
                    h, m = n // UH, n % UH
                    return (dveA, f"hl{m}_{h}") if m < KC else (dveA, f"f{m-KC}_{h}") if m < 10 else (dveA, f"v{m-10}_{h}")

                def stage_a(t, p, s, n):
                    if s == "n":
                        return
                    h, m = n // UH, n % UH
                    bank = psA[n % 2]
                    count, name = taken(n - 2 if n >= 2 else n - 2 + U)
                    count.wait(pe, t, name, 0 if n >= 2 else 1)
                    if m < KC:
                        if m == 0:
                            dveA.wait(pe, t, f"hb_{h}")
                        for c in range(CH):
                            mm = nc.tensor.transpose(bank[:, c * P:(c + 1) * P], hb[:, c, m * P:(m + 1) * P], consts["ident"][:, :])
                    else:
                        if m == KC:
                            dveA.wait(pe, t, f"hl{KC-1}_{h}")
                        out = slice((m - KC) * P, (m - KC + 1) * P)
                        for k in range(KC):
                            nc.tensor.matmul(bank[:, :], wh[:, k, out], hTh[:, h, k, :], start=(k == 0), stop=False)
                            nc.tensor.matmul(bank[:, :], wh[:, k, out], hTl[:, h, k, :], start=False, stop=False)
                            mm = nc.tensor.matmul(bank[:, :], wl[:, k, out], hTh[:, h, k, :], start=False, stop=(k == KC - 1))
                    peA.inc(mm, f"u{n}")

                def z_of(t, p, h):
                    dveP.wait(pe, t, "kb_0")
                    dveP.wait(pe, t, f"y_{KC-1}") if h else dveB.wait(pe, t, f"y_{2*KC-1}", 1)
                    for k in range(KC):
                        mm = nc.tensor.matmul(psZ[0][0:HQ, :], kb[:, p, k, :], q[:, p, k, h * BLK:(h + 1) * BLK], start=(k == 0), stop=(k == KC - 1))
                    (peB if h else peP).inc(mm, f"z_{h}")

                def w_of(t, p, i):
                    k, h = i % KC, i // KC
                    (dveB if h else dveP).wait(pe, t, f"zl_{h}")
                    dve_w(i - 2).wait(pe, t, f"y_{i-2}") if i >= 2 else dveB.wait(pe, t, f"y_{2*KC-2+i}", 1)
                    nc.tensor.matmul(psZ[1 - i % 2][:, :], headselr[:, k * P:(k + 1) * P], zh[:, :], start=True, stop=False)
                    mm = nc.tensor.matmul(psZ[1 - i % 2][:, :], headselr[:, k * P:(k + 1) * P], zl[:, :], start=False, stop=True)
                    (peB if h else peP).inc(mm, f"w_{i}")

                def stage_p(t, p, s, i):
                    if s == "prep":
                        dveP.wait(pe, t, "kk1_0")
                        dveB.wait(pe, t, f"y_{2*KC-1}", 1)
                        for k in range(KC):
                            mm = nc.tensor.matmul(psZ[0][:, 2 * k:2 * k + 2], dup[:, k % 2], kk[:, k // 2, :], start=True, stop=True)
                        peP.inc(mm, "dup_0")
                    else:
                        {"z": z_of, "w": w_of}[s](t, p, i)

                def stage_b(t, p, s, c):
                    if s in "zw":
                        {"z": z_of, "w": w_of}[s](t, p, c)
                    if s == "o":
                        i = (c // CH) * KC + KC - 1
                        dve_w(i).wait(pe, t, f"y_{i}")
                        dveB.wait(pe, t, f"t2_{c-2}") if c >= 2 else dveB.wait(pe, t, f"t2_{NC8-2+c}", 1)
                        for k in range(KC):
                            mm = nc.tensor.matmul(psO[c % 2][:, :], q[:, p, k, c * P:(c + 1) * P], wop[:, p, k, :], start=(k == 0), stop=(k == KC - 1))
                        peB.inc(mm, f"o_{c}")
                    if s == "x":
                        dveB.wait(pe, t, f"xn_{c}")
                        actB.wait(pe, t, f"xT_{c-1}") if c else actB.wait(pe, t, f"xT_{NC8-1}", 1)
                        for k in range(KC):
                            mm = nc.tensor.transpose(psT[0][:, k * P:(k + 1) * P], xrow[:, c % RB, k * P:(k + 1) * P], consts["ident"][:, :])
                        peB.inc(mm, f"xt_{c}")
                    if s == "r":
                        actB.wait(pe, t, f"xT_{c}")
                        dveB.wait(pe, t, f"lg_{c-1}") if c else dveB.wait(pe, t, f"lg_{NC8-1}", 1)
                        for k in range(KC):
                            mm = nc.tensor.matmul(psT[1][:, 0:E], xT[:, c % 2, k * P:(k + 1) * P], wr[:, k, :], start=(k == 0), stop=(k == KC - 1))
                        peB.inc(mm, f"rt_{c}")

                walk(pe, stage_a, stage_p, stage_b)
                for i in range(4):
                    pe.wait_ge(p_out, i + 1)
                    for j in range(4):
                        r = 4 * i + j
                        mm = nc.tensor.transpose(psA[0][:, j * P:(j + 1) * P], pall[:, r].rearrange("p a e -> p (a e)"), consts["ident"][:, :])
                    mm.then_inc(s_pool, 1)

            @block.scalar
            def _(act):
                actA.credit(act)
                actB.credit(act)
                act.wait_ge(w_in, 16 * len(loads))
                nc.scalar.mul(ag[:, 0], g[:, :], float(HD) ** -0.5).then_inc(s_act, 1)
                act.wait_ge(s_act, 1)
                nc.scalar.copy(headselr[:, :], headsel[:, :]).then_inc(s_act, 1)
                for k in range(KC):
                    nc.scalar.activation(wq[:, k, :], wq[:, k, :], ACT.Copy, scale=ag[:, 0, k:k + 1]).then_inc(s_act, 1)
                    nc.scalar.activation(wk[:, k, :], wk[:, k, :], ACT.Copy, scale=ag[:, 0, k:k + 1]).then_inc(s_act, 1)
                    nc.scalar.activation(wv[:, k, :], wv[:, k, :], ACT.Copy, scale=g[:, k:k + 1]).then_inc(s_act, 1)
                act.wait_ge(s_act, 3 * KC + 2)
                nc.scalar.copy(wh[:, :, 0:C], wq).then_inc(s_act, 1)
                nc.scalar.copy(wh[:, :, C:], q[:, 1, :, 0:2 * KV]).then_inc(s_act, 1)

                def stage_a(t, p, s, n):
                    if s == "n":
                        return
                    h, m = n // UH, n % UH
                    bank = psA[n % 2]
                    if m < KC:
                        if m == 0:
                            peA.wait(act, t, f"u{h*UH+UH-1}", 1)
                        peA.wait(act, t, f"u{n}")
                        actA.inc(nc.scalar.activation(hTh[:, h, m, :], bank[:, :], ACT.Identity), f"hT{m}_{h}")
                    elif m < 10:
                        i = m - KC
                        peA.wait(act, t, f"u{n}")
                        if i >= 2:
                            dveA.wait(act, t, f"f{i-2}_{h}")
                        elif h:
                            dveA.wait(act, t, f"f{i+4}_0")
                        else:
                            dveA.wait(act, t, f"f{i+4}_1", 1)
                        actA.inc(nc.scalar.activation(er[:, i % 2], bank[:, :], ACT.Relu, scale=-1.0), f"n{i}_{h}")
                        actA.wait(act, t, f"n{i}_{h}")
                        actA.inc(nc.scalar.activation(er[:, i % 2], er[:, i % 2], ACT.Exp, scale=-1.0), f"e{i}_{h}")

                def stage_b(t, p, s, c):
                    if s == "x":
                        peB.wait(act, t, f"xt_{c}")
                        peB.wait(act, t, f"rt_{c-2}") if c >= 2 else peB.wait(act, t, f"rt_{NC8-2+c}", 1)
                        actB.inc(nc.scalar.activation(xT[:, c % 2], psT[0][:, :], ACT.Identity), f"xT_{c}")
                    if s == "r":
                        dveB.wait(act, t, f"nm_{c}")
                        actB.inc(nc.scalar.activation(lg[:, :], lg[:, :], ACT.Exp, bias=sx[:, 1:2], accum_out=sx[:, 2:3]), f"ex_{c}")

                walk(act, stage_a, lambda *a: None, stage_b)

            @block.vector
            def _(v):
                for x in (dveA, dveP, dveB):
                    x.credit(v)
                v.wait_ge(s_act, 3 * KC + 4)
                nc.vector.tensor_tensor(wl[:, :, 0:C], wq, wh[:, :, 0:C].bitcast(F32), ALU.subtract)
                nc.vector.tensor_tensor(wl[:, :, C:], q[:, 1, :, 0:2 * KV], wh[:, :, C:].bitcast(F32), ALU.subtract).then_inc(s_split, 1)
                v.wait_ge(s_split, 1)

                def stage_a(t, p, s, n):
                    h, m = (n, 0) if s == "n" else (n // UH, n % UH)
                    bank = psA[n % 2]
                    if s == "n":
                        v.wait_ge(tb_in[p][h], ((t - p) // 2 + 1) * 16)
                        dveA.wait(v, t, "mv_0") if h else dveA.wait(v, t, "mv_1", 1)
                        for c in range(CH):
                            ins = nc.vector.bn_stats(st6[:, c, :], tb[:, p, h * CH + c, :])
                        dveA.inc(ins, f"st_{h}")
                        dveA.wait(v, t, f"st_{h}")
                        settle(v, spare[1])
                        for c in range(CH):
                            ins = nc.vector.bn_aggr(mv[:, c, :], st6[:, c, :])
                        dveA.inc(ins, f"mv_{h}")
                        poolA.wait(v, t, f"r_{h}")
                        dveA.wait(v, t, f"mv_{h}")
                        peA.wait(v, t, f"u{KC-1}") if h else peA.wait(v, t, f"u{UH+KC-1}", 1)
                        for c in range(CH):
                            ins = nc.vector.tensor_scalar(hb[:, c, :], tb[:, p, h * CH + c, :], mv[:, c, 0:1], rs[:, c, 1:2], ALU.subtract, ALU.mult)
                        dveA.inc(ins, f"hb_{h}")
                    elif m < KC:
                        actA.wait(v, t, f"hT{m}_{h}")
                        dveA.inc(nc.vector.tensor_tensor(hTl[:, h, m, :], bank[:, :], hTh[:, h, m, :].bitcast(F32), ALU.subtract), f"hl{m}_{h}")
                    elif m < 10:
                        i = m - KC
                        actA.wait(v, t, f"e{i}_{h}")
                        dveA.inc(nc.vector.tensor_scalar(er[:, i % 2], er[:, i % 2], 0.01, None, ALU.max), f"c{i}_{h}")
                        dveA.wait(v, t, f"c{i}_{h}")
                        if i < KC:
                            if i == 0 and h == 0:
                                peB.wait(v, t, f"o_{NC8-1}", 2)
                            dveA.inc(nc.vector.scalar_tensor_tensor(q[:, p, i, h * BLK:(h + 1) * BLK], bank[:, :], 0.0, er[:, i % 2], ALU.max, ALU.add), f"f{i}_{h}")
                        else:
                            j = i - KC
                            dveP.wait(v, t, "kk1_0", 1)
                            dveA.inc(nc.vector.scalar_tensor_tensor(kf[:, j], bank[:, :], 0.0, er[:, i % 2], ALU.max, ALU.add, accum_out=ks[:, j, h:h + 1]), f"f{i}_{h}")
                    else:
                        j = m - 10
                        peA.wait(v, t, f"u{n}")
                        dveA.wait(v, t, "v0_" + str(h)) if j else dveA.wait(v, t, f"f{KC+j}_{h}")
                        dveA.inc(nc.vector.tensor_tensor_reduce(out=kvj[:, :], in0=kf[:, j], in1=bank[:, :], scale=1.0, scalar=0.0, op0=ALU.mult, op1=ALU.add,
                                                                accum_out=kv[:, j, h:h + 1]), f"v{j}_{h}")

                def z_of(t, p, h):
                    pz, dz = (peB, dveB) if h else (peP, dveP)
                    pz.wait(v, t, f"z_{h}")
                    peP.wait(v, t, f"w_{KC-1}") if h else peB.wait(v, t, f"w_{2*KC-1}", 1)
                    dz.inc(nc.vector.tensor_scalar(zr[:, :], psZ[0][0:HQ, :], 1e-6, None, ALU.add), f"ze_{h}")
                    dz.wait(v, t, f"ze_{h}")
                    dz.inc(nc.vector.reciprocal(zr[:, :], zr[:, :]), f"zr_{h}")
                    dz.wait(v, t, f"zr_{h}")
                    dz.inc(nc.vector.tensor_copy(zh[:, :], zr[:, :]), f"zh_{h}")
                    dz.wait(v, t, f"zh_{h}")
                    dz.inc(nc.vector.tensor_tensor(zl[:, :], zr[:, :], zh[:, :].bitcast(F32), ALU.subtract), f"zl_{h}")

                def w_of(t, p, i):
                    k, h = i % KC, i // KC
                    qq = q[:, p, k, h * BLK:(h + 1) * BLK]
                    (peB if h else peP).wait(v, t, f"w_{i}")
                    dve_w(i).inc(nc.vector.tensor_tensor(qq, qq, psZ[1 - i % 2][:, :], ALU.mult), f"y_{i}")

                def stage_p(t, p, s, i):
                    if s == "prep":
                        dveA.wait(v, t, "v1_1")
                        peP.wait(v, t, "dup_0", 1)
                        dveP.inc(nc.vector.tensor_tensor(kk[:, :, 0], ks[:, :, 0], ks[:, :, 1], ALU.add), "kk0_0")
                        dveP.inc(nc.vector.tensor_tensor(kk[:, :, 1], kv[:, :, 0], kv[:, :, 1], ALU.add), "kk1_0")
                        peP.wait(v, t, "dup_0")
                        dveP.inc(nc.vector.tensor_copy(kd[:, :, :].rearrange("p k j -> p (k j)"), psZ[0][:, 0:2 * KC]), "kd_0")
                        dveP.wait(v, t, "kd_0")
                        peB.wait(v, t, f"o_{NC8-1}", 2)
                        dveP.inc(nc.vector.tensor_tensor(kb[:, p], headof[:, :, :], kd[:, :, 0:1].to_broadcast([P, KC, HQ]), ALU.mult), "kb_0")
                        for k in range(KC):
                            ins = nc.vector.tensor_scalar(wop[:, p, k, :], wo[:, k, :], kd[:, k, 1:2], None, ALU.mult)
                        dveP.inc(ins, "wop_0")
                    else:
                        {"z": z_of, "w": w_of}[s](t, p, i)

                def stage_b(t, p, s, c):
                    if s in "zw":
                        {"z": z_of, "w": w_of}[s](t, p, c)
                    if s == "o":
                        peB.wait(v, t, f"o_{c}")
                        dveB.inc(nc.vector.tensor_tensor(tb[:, p, c], psO[c % 2][:, :], tb[:, p, c], ALU.add), f"t2_{c}")
                        dveB.wait(v, t, f"t2_{c}")
                        dveB.wait(v, t, f"mv_{c-1}") if c else dveB.wait(v, t, f"mv_{NC8-1}", 1)
                        dveB.inc(nc.vector.bn_stats(st1[:, :], tb[:, p, c]), f"st_{c}")
                        dveB.wait(v, t, f"st_{c}")
                        dveB.wait(v, t, f"xn_{c-4}") if c >= 4 else dveB.wait(v, t, f"xn_{NC8-4+c}", 1)
                        settle(v, spare[1])
                        dveB.inc(nc.vector.bn_aggr(mv1[:, c % 4], st1[:, :]), f"mv_{c}")
                    if s == "x":
                        poolB.wait(v, t, f"r_{c}")
                        v.wait_ge(row_out[c % RB], (t * (NC8 // RB) + c // RB + 1) * 16)
                        dveB.inc(nc.vector.tensor_scalar(xrow[:, c % RB, 0:C], tb[:, p, c], mv1[:, c % 4, 0:1], rs1[:, c % 4, 1:2], ALU.subtract, ALU.mult), f"xn_{c}")
                    if s == "r":
                        peB.wait(v, t, f"rt_{c}")
                        dveB.wait(v, t, f"p_{c-1}") if c else dveB.wait(v, t, f"p_{NC8-1}", 1)
                        dveB.inc(nc.vector.tensor_tensor(lg[:, :], psT[1][:, 0:E], br[:, :], ALU.add), f"lg_{c}")
                        dveB.wait(v, t, f"lg_{c}")
                        dveB.inc(nc.vector.tensor_reduce(sx[:, 0:1], lg[:, :], AX.X, ALU.max), f"mx_{c}")
                        dveB.wait(v, t, f"mx_{c}")
                        dveB.inc(nc.vector.tensor_scalar(sx[:, 1:2], sx[:, 0:1], -1.0, None, ALU.mult), f"nm_{c}")
                        actB.wait(v, t, f"ex_{c}")
                        dveB.inc(nc.vector.reciprocal(sx[:, 3:4], sx[:, 2:3]), f"rc_{c}")
                        dveB.wait(v, t, f"rc_{c}")
                        dveB.inc(nc.vector.tensor_scalar(xrow[:, c % RB, C:ROW], lg[:, :], sx[:, 3:4], None, ALU.mult), f"p_{c}")
                        dveB.wait(v, t, f"p_{c}")
                        dveB.inc(nc.vector.tensor_copy(pall[:, p * NC8 + c, bass.ds((t - p) // 2, 1), :].rearrange("p a e -> p (a e)"), xrow[:, c % RB, C:ROW]), f"pa_{c}")

                walk(v, stage_a, stage_p, stage_b)
                dveB.wait(v, NB - 1, f"pa_{NC8-1}")
                v.sem_inc(p_out, 1)
                for i in range(4):
                    v.wait_ge(s_pool, 2 + i)
                    nc.vector.tensor_copy(consts["probs"][:, i * 512:(i + 1) * 512], psA[0][:, :]).then_inc(p_out, 1)
def routing(nc, io, consts, keep):
    ctx = ExitStack()
    with ctx:
        def sb(name, shape, dt=F32):
            return ctx.enter_context(nc.sbuf_tensor(name, shape, dt))

        def sem(name):
            return ctx.enter_context(nc.semaphore(name))

        NQ = NT // 4
        QB = NQ // P
        TB = NT // P
        BITS = 30
        probs = consts["probs"]
        same, before = sb("same", [P, P]), sb("before", [P, P])
        slot, rowbase = keep["slot"], sb("rowbase", [P, E * 2])
        big = [sb(f"big{i}", [P, NQ]) for i in range(3)]
        cendb = sb("cendb", [P, E, TB])
        less = sb("less", [P, E, TB])
        cend = sb("cend", [P, QB])
        cand = sb("cand", [P, 1], I32)
        nxt = sb("nxt", [P, 1], I32)
        rej = sb("rej", [P, 1], I32)
        bitf = sb("bitf", [P, 1])
        cnt = sb("cnt", [P, 4])
        tot = sb("tot", [P, 4])
        rowf = sb("rowf", [P, E * 2])
        ps = [ctx.enter_context(nc.psum_tensor(f"rps{i}", [P, 512], F32)) for i in range(4)]
        c_in, st_out, ce_out, ce_in = sem("r_in"), sem("crow_out"), sem("cend_out"), sem("cend_in")
        s_dve, s_pe, own = sem("route_dve"), sem("route_pe"), sem("route_own")
        s_pool = sem("route_pool")
        dve = Count(sem("search_dve"), ["cnt", "half", "next", "rej", "xor", "cand"])
        pe = Count(sem("search_pe"), ["tot"])
        with nc.Block() as block:
            @block.sync
            def _(sp):
                sp.dma_start(same[:, :], io["c_sameexp"]).then_inc(c_in, 16)
                sp.dma_start(before[:, :], io["c_segbefore"]).then_inc(c_in, 16)
                sp.dma_start(slot[:, :], io["slot"]).then_inc(c_in, 16)
                sp.dma_start(rowbase[:, :], io["rowbase"]).then_inc(c_in, 16)
                sp.dma_start(keep["wur"][:, :], io["w_up"][0, :, 0:FF]).then_inc(keep["wu_in"], 16)
                for i in range(2):
                    sp.dma_start(keep["wd"][:, i].rearrange("p f n -> p (f n)"), io["w_down"][i]).then_inc(keep["wd_in"][i], 16)
                for k in range(1, KC):
                    sp.wait_ge(s_pool, 2 * k)
                    sp.dma_start(keep["wur"][:, :], io["w_up"][0, :, k * FF:(k + 1) * FF]).then_inc(keep["wu_in"], 16)
                sp.wait_ge(s_dve, 6)
                for q in range(4):
                    sp.dma_start(io["cend"].rearrange("e (q r) -> q e r", q=4)[q], cend[q * E:(q + 1) * E, :]).then_inc(ce_out, 16)
                for q in range(4):
                    sp.dma_start(io["crow"].rearrange("(e q r) i -> q e (r i)", q=4, r=QB)[q], big[0][q * E:(q + 1) * E, :]).then_inc(st_out, 16)
                sp.wait_ge(ce_out, 64)
                sp.dma_start(cendb[:, :, :].rearrange("p e b -> p (e b)"), io["cend"].rearrange("e b -> (e b)").partition_broadcast(P)).then_inc(ce_in, 16)
                sp.wait_ge(st_out, 64)

            @block.gpsimd
            def _(pool):
                wuh, wul, wur = keep["wuh"], keep["wul"], keep["wur"]
                for k in range(KC):
                    pool.wait_ge(keep["wu_in"], 16 * (k + 1))
                    nc.gpsimd.tensor_copy(wuh[:, k, :], wur[:, :]).then_inc(s_pool, 1)
                    pool.wait_ge(s_pool, 2 * k + 1)
                    nc.gpsimd.tensor_tensor(wul[:, k, :], wur[:, :], wuh[:, k, :].bitcast(F32), ALU.subtract).then_inc(s_pool, 1)

            @block.tensor
            def _(t):
                pe.credit(t)
                t.wait_ge(c_in, 64)
                with t.Fori(0, BITS) as i:
                    dve.wait(t, i, "cnt")
                    dve.wait(t, i, "rej", 1)
                    pe.inc(nc.tensor.matmul(ps[0][:, 0:1], same[:, :], cnt[:, 0:1], start=True, stop=True), "tot")
                t.wait_ge(s_dve, 3)
                nc.tensor.matmul(ps[1][:, 0:1], same[:, :], cnt[:, 1:2], start=True, stop=True).then_inc(s_pe, 1)
                nc.tensor.matmul(ps[2][:, 0:1], before[:, :], cnt[:, 2:3], start=True, stop=True).then_inc(s_pe, 1)
                t.wait_ge(s_dve, 4)
                nc.tensor.matmul(ps[3][:, 0:1], before[:, :], cnt[:, 3:4], start=True, stop=True).then_inc(s_pe, 1)

            @block.vector
            def _(v):
                dve.credit(v)
                nc.vector.memset(cand[:, :], 1 << (BITS - 1)).then_inc(s_dve, 1)
                nc.vector.memset(nxt[:, :], 1 << (BITS - 1))
                nc.vector.memset(bitf[:, :], float(1 << BITS)).then_inc(s_dve, 1)
                v.wait_ge(c_in, 64)
                v.wait_ge(s_dve, 2)
                candf = cand[:, :].bitcast(F32)
                with v.Fori(0, BITS) as i:
                    dve.wait(v, i, "cand", 1)
                    pe.wait(v, i, "tot", 1)
                    dve.inc(nc.vector.tensor_scalar(big[0][:, :], probs[:, :], candf, None, ALU.is_ge, ALU.add, accum_out=cnt[:, 0:1]), "cnt")
                    dve.inc(nc.vector.tensor_scalar(bitf[:, :], bitf[:, :], 0.5, None, ALU.mult), "half")
                    dve.inc(nc.vector.tensor_scalar(nxt[:, :], nxt[:, :], 1, None, ALU.logical_shift_right), "next")
                    pe.wait(v, i, "tot")
                    dve.wait(v, i, "half")
                    dve.inc(nc.vector.tensor_scalar(rej[:, :], ps[0][:, 0:1], float(TOPK), bitf[:, 0:1], ALU.is_lt, ALU.mult), "rej")
                    dve.wait(v, i, "rej")
                    dve.inc(nc.vector.tensor_tensor(cand[:, :], cand[:, :], rej[:, :], ALU.bitwise_xor), "xor")
                    dve.wait(v, i, "xor")
                    dve.inc(nc.vector.tensor_tensor(cand[:, :], cand[:, :], nxt[:, :], ALU.bitwise_or), "cand")
                dve.wait(v, BITS - 1, "cand")
                nc.vector.tensor_scalar(big[1][:, :], probs[:, :], candf, None, ALU.is_gt, ALU.add, accum_out=cnt[:, 1:2])
                nc.vector.tensor_scalar(big[0][:, :], probs[:, :], candf, None, ALU.is_equal, ALU.add, accum_out=cnt[:, 2:3]).then_inc(s_dve, 1)
                v.wait_ge(s_pe, 2)
                v.wait_ge(s_dve, 3)
                nc.vector.tensor_scalar(tot[:, 0:1], ps[1][:, 0:1], -1.0, float(TOPK), ALU.mult, ALU.add).then_inc(own, 1)
                v.wait_ge(own, 1)
                nc.vector.tensor_tensor(tot[:, 1:2], tot[:, 0:1], ps[2][:, 0:1], ALU.subtract)
                nc.vector.tensor_tensor_scan(big[2][:, :], consts["ones"][:, 0:1].to_broadcast([P, NQ]), big[0][:, :], 0.0, ALU.mult, ALU.add).then_inc(own, 1)
                v.wait_ge(own, 2)
                nc.vector.scalar_tensor_tensor(big[2][:, :], big[2][:, :], tot[:, 1:2], big[0][:, :], ALU.is_le, ALU.mult).then_inc(own, 1)
                v.wait_ge(own, 3)
                nc.vector.tensor_tensor(big[1][:, :], big[1][:, :], big[2][:, :], ALU.add).then_inc(own, 1)
                v.wait_ge(own, 4)
                nc.vector.tensor_tensor_scan(big[2][:, :], consts["ones"][:, 0:1].to_broadcast([P, NQ]), big[1][:, :], 0.0, ALU.mult, ALU.add).then_inc(own, 1)
                v.wait_ge(own, 5)
                nc.vector.tensor_copy(cnt[:, 3:4], big[2][:, NQ - 1:NQ]).then_inc(s_dve, 1)
                v.wait_ge(s_pe, 3)
                nc.vector.tensor_scalar(big[0][:, :], big[2][:, :], ps[3][:, 0:1], None, ALU.add).then_inc(s_dve, 1)
                v.wait_ge(s_dve, 5)
                nc.vector.tensor_copy(cend[:, :], big[0][:, :].rearrange("p (r i) -> p r i", i=P)[:, :, P - 1]).then_inc(s_dve, 1)
                v.wait_ge(ce_in, 16)
                for a in range(2):
                    nc.vector.tensor_scalar(less[:, :, :], cendb[:, :, :], slot[:, a:a + 1], None, ALU.is_le).then_inc(own, 1)
                    v.wait_ge(own, 6 + 2 * a)
                    nc.vector.tensor_reduce(keep["blkf"][:, :, a], less[:, :, :], AX.X, ALU.add).then_inc(own, 1)
                    v.wait_ge(own, 7 + 2 * a)
                nc.vector.tensor_tensor(rowf[:, :], keep["blkf"][:, :, :].rearrange("p e a -> p (e a)"), rowbase[:, :], ALU.add).then_inc(own, 1)
                v.wait_ge(own, 10)
                nc.vector.tensor_copy(keep["rowi"][:, :], rowf[:, :])
def experts(nc, io, consts, keep):
    ctx = ExitStack()
    with ctx:
        def sb(name, shape, dt=F32):
            return ctx.enter_context(nc.sbuf_tensor(name, shape, dt))

        def sem(name):
            return ctx.enter_context(nc.semaphore(name))

        NG = 2 * GS
        wur, wuh, wul, wd, slot, rowi, blkf = (keep[k] for k in ("wur", "wuh", "wul", "wd", "slot", "rowi", "blkf"))
        wu_in, wd_in = keep["wu_in"], keep["wd_in"]
        bup = sb("bup", [P, GRP, FT])
        bias = sb("bias", [P, FT])
        cri = sb("cri", [P, NG], I32)
        bk = sb("bk", [P, NG])
        cr = sb("cr", [P, NG, P])
        below = sb("below", [P, 2, P])
        cn = sb("cn", [P, NG])
        tokf = sb("tokf", [P, NG])
        tok = sb("tok", [P, 2, NG], I32)
        gate = sb("gate", [P, 2, NG])
        xg = sb("xg", [P, NG, ROW])
        xh = sb("xgh", [P, KC, NG * P], F32R)
        xl = sb("xgl", [P, KC, NG * P], F32R)
        act_t = sb("act_t", [P, FT, NG * P])
        ob = sb("ob", [P, 2, C])
        first = sb("first_s", [P, 2, 2])
        psU = [ctx.enter_context(nc.psum_tensor(f"psU{i}", [P, 512], F32)) for i in range(3)]
        psD = [ctx.enter_context(nc.psum_tensor(f"psD{i}", [P, 512], F32)) for i in range(3)]
        psR = [ctx.enter_context(nc.psum_tensor(f"psR{i}", [P, 512], F32)) for i in range(2)]
        spare = [sem(f"spare_f{i}") for i in range(2)]
        b_in, cr_in, xg_in, ones_set = sem("bup_in"), sem("cr_in"), sem("xg_in"), sem("ones_set")
        added = [sem(f"added{i}") for i in range(2)]

        dveR = Count(sem("dve_r"), ["idx", "bk", "bias"] + [f"c{n}" for n in range(NG)] + ["tb", "tok"] + [f"g{j}" for j in range(GS)] + sum(([f"th{n}", f"t{n}"] for n in range(2 * KC)), []))
        peR = Count(sem("pe_r"), [f"t{n}" for n in range(2 * KC)])
        dveW = Count(sem("dve_w"), sum(([f"h{k}", f"l{k}"] for k in range(KC)), []))
        NU = 2 * FT
        peU = Count(sem("pe_u"), [f"u{n}" for n in range(NU)])
        actU = Count(sem("act_u"), [f"u{n}" for n in range(NU)])
        peD = Count(sem("pe_d"), [f"d{n}" for n in range(NG)])
        dveD = Count(sem("dve_d"), [f"o{n}" for n in range(NG)])

        fetch = {0: ["index"], 1: ["rows"], 3: ["gates", ("t", 0), ("t", 1)], 4: [("t", 2), ("t", 3)], 5: [("t", 4), ("t", 5)], 6: [("t", 6), ("t", 7)]}

        def last_of(n, count):
            return max(m for m in range(count) if m % 3 == n)

        def walk(engine, fetch_step, up, down):
            for n in range(NG):
                for s in fetch.get(n, []):
                    fetch_step(0, 0, *((s, 0) if isinstance(s, str) else s))
            for n in range(NU):
                up(0, 0, n)

            def step(t, p, last):
                for n in range(NG):
                    down(t, p, n)
                    if not last:
                        for s in fetch.get(n, []):
                            fetch_step(t + 1, 1 - p, *((s, 0) if isinstance(s, str) else s))
                if not last:
                    for n in range(NU):
                        up(t + 1, 1 - p, n)
            with engine.Fori(0, GRP // 2 - 1) as b:
                step(b * 2, 0, False)
                step(b * 2 + 1, 1, False)
            step(GRP - 2, 0, False)
            step(GRP - 1, 1, True)

        nothing = lambda *a: None
        y_rows = io["y"].rearrange("c p n -> (c p) n")
        table = io["table"].rearrange("c p n -> (c p) n")
        with nc.Block() as block:
            @block.sync
            def _(sp):
                sp.dma_start(bup[:, :, :], io["b_up"]).then_inc(b_in, 16)

                def down(t, p, n):
                    j, a = n // 2, n % 2
                    if n % 2 == 0 and not (isinstance(t, int) and t == GRP - 1):
                        k = n // 2
                        dveW.wait(sp, t, f"l{k-1}") if k else dveW.wait(sp, t, f"l{KC-1}", 1)
                        sp.dma_start(wur[:, :], io["w_up"][bass.ds(t + 1, 1), :, k * FF:(k + 1) * FF].rearrange("g p f -> p (g f)")).then_inc(wu_in, 16)
                    if a and not (isinstance(t, int) and t == GRP - 1 and j >= 2):
                        peD.wait(sp, t, f"d{n}")
                        sp.dma_start(wd[:, j % 2].rearrange("p f n -> p (f n)"), io["w_down"][bass.ds(GS * t + j + 2, 1)].rearrange("e p f -> p (e f)")).then_inc(wd_in[j % 2], 16)

                walk(sp, nothing, nothing, down)
                for i in range(2):
                    sp.wait_ge(added[i], 16 + 32 * E // 2)

            @block.gpsimd
            def _(pool):
                def fetch_step(t, p, s, i):
                    if s == "index":
                        dveR.wait(pool, t, "idx")
                        dveR.wait(pool, t, f"c{NG-1}", 1)
                        settle(pool, spare[0])
                        for n in range(NG):
                            pool.indirect_dma_start(out=cr[:, n, :], out_offset=None, in_=io["crow"], in_offset=bass.IndirectOffsetOnAxis(ap=cri[:, n:n + 1], axis=0)).then_inc(cr_in, 16)
                    if s == "rows":
                        dveR.wait(pool, t, "tok")
                        dveR.wait(pool, t, f"g{GS-1}", 1)
                        peR.wait(pool, t, f"t{2*KC-1}", 1)
                        settle(pool, spare[0])
                        for n in range(NG):
                            pool.indirect_dma_start(out=xg[:, n, :], out_offset=None, in_=table, in_offset=bass.IndirectOffsetOnAxis(ap=tok[:, p, n:n + 1], axis=0)).then_inc(xg_in, 16)

                def down(t, p, n):
                    j, a = n // 2, n % 2
                    dveD.wait(pool, t, f"o{n}")
                    if a == 0:
                        pool.wait_ge(added[(j - 1) % 2], 16 + 32 * (2 * t + (j + 1) // 2))
                    settle(pool, spare[0])
                    pool.indirect_dma_start(out=y_rows, out_offset=bass.IndirectOffsetOnAxis(ap=tok[:, p, n:n + 1], axis=0), in_=ob[:, n % 2, :], in_offset=None,
                                            compute_op=ALU.add).then_inc(added[j % 2], 16)

                for i in range(2):
                    pool.dma_start(first[:, i], io["slot"]).then_inc(added[i], 16)
                walk(pool, fetch_step, nothing, down)

            @block.tensor
            def _(pe):
                for c in (peR, peU, peD):
                    c.credit(pe)

                def fetch_step(t, p, s, i):
                    if s == "t":
                        k, h = i % KC, i // KC
                        if i == 0:
                            pe.wait_ge(xg_in, 16 * NG * t + 16 * NG)
                        dveR.wait(pe, t, f"t{i-2}") if i >= 2 else dveR.wait(pe, t, f"t{2*KC-2+i}", 1)
                        for q in range(4):
                            mm = nc.tensor.transpose(psR[i % 2][:, q * P:(q + 1) * P], xg[:, 4 * h + q, k * P:(k + 1) * P], consts["ident"][:, :])
                        peR.inc(mm, f"t{i}")

                def up(t, p, n):
                    h, f = n // FT, n % FT
                    m = min(P, FF - f * P)
                    if n == 0:
                        dveW.wait(pe, t - 1, f"l{KC-1}")
                        dveR.wait(pe, t, f"t{2*KC-1}")
                    actU.wait(pe, t, f"u{n-3}") if n >= 3 else actU.wait(pe, t, f"u{last_of(n, NU)}", 1)
                    for k in range(KC):
                        fs, ts = slice(f * P, f * P + m), slice(h * 512, (h + 1) * 512)
                        nc.tensor.matmul(psU[n % 3][0:m, :], wuh[:, k, fs], xh[:, k, ts], start=(k == 0), stop=False)
                        nc.tensor.matmul(psU[n % 3][0:m, :], wuh[:, k, fs], xl[:, k, ts], start=False, stop=False)
                        mm = nc.tensor.matmul(psU[n % 3][0:m, :], wul[:, k, fs], xh[:, k, ts], start=False, stop=(k == KC - 1))
                    peU.inc(mm, f"u{n}")

                def down(t, p, n):
                    j, a = n // 2, n % 2
                    if a == 0:
                        pe.wait_ge(wd_in[j % 2], 16 * (2 * t + j // 2 + 1))
                    if n in (0, NG // 2):
                        actU.wait(pe, t, f"u{FT-1}" if n == 0 else f"u{NU-1}")
                    dveD.wait(pe, t, f"o{n-3}") if n >= 3 else dveD.wait(pe, t, f"o{last_of(n, NG)}", 1)
                    for f in range(FT):
                        mm = nc.tensor.matmul(psD[n % 3][:, :], act_t[:, f, n * P:(n + 1) * P], wd[:, j % 2, f, :], start=(f == 0), stop=(f == FT - 1))
                    peD.inc(mm, f"d{n}")

                walk(pe, fetch_step, up, down)

            @block.scalar
            def _(act):
                actU.credit(act)
                act.wait_ge(ones_set, 1)

                def up(t, p, n):
                    h, f = n // FT, n % FT
                    m = min(P, FF - f * P)
                    peU.wait(act, t, f"u{n}")
                    if n == 0:
                        dveR.wait(act, t, "bias")
                    if f == 0:
                        peD.wait(act, t, f"d{4*h+3}", 1)
                    actU.inc(nc.scalar.activation(act_t[0:m, f, h * 512:(h + 1) * 512], psU[n % 3][0:m, :], ACT.Silu, bias=bias[0:m, f:f + 1]), f"u{n}")

                walk(act, nothing, up, nothing)

            @block.vector
            def _(v):
                for x in (dveR, dveW, dveD):
                    x.credit(v)
                nc.vector.memset(act_t[:, FT - 1, :], 1.0).then_inc(ones_set, 1)
                v.wait_ge(b_in, 16)

                def fetch_step(t, p, s, i):
                    if s == "index":
                        if not isinstance(t, int) or t >= 2:
                            for x in added:
                                v.wait_ge(x, 16 + 64 * (t - 1))
                        dveR.inc(nc.vector.tensor_copy(cri[:, :], rowi[:, bass.ds(t * NG, NG)]), "idx")
                        dveR.wait(v, t, "tb", 1)
                        dveR.inc(nc.vector.tensor_copy(bk[:, :], blkf[:, bass.ds(t * GS, GS), :].rearrange("p e a -> p (e a)")), "bk")
                        actU.wait(v, t, f"u{NU-1}", 1)
                        dveR.inc(nc.vector.tensor_copy(bias[:, :], bup[:, bass.ds(t, 1), :].rearrange("p g f -> p (g f)")), "bias")
                    if s == "rows":
                        v.wait_ge(cr_in, 16 * NG * t + 16 * NG)
                        for n in range(NG):
                            dveR.wait(v, t, f"c{n-2}") if n >= 2 else dveR.wait(v, t, f"c{NG-2+n}", 1)
                            if n == 0:
                                dveR.wait(v, t, "tb", 1)
                            dveR.inc(nc.vector.tensor_scalar(below[:, n % 2], cr[:, n, :], slot[:, n % 2:n % 2 + 1], None, ALU.is_le, ALU.add, accum_out=cn[:, n:n + 1]), f"c{n}")
                        dveR.wait(v, t, f"c{NG-1}")
                        dveR.wait(v, t, "tok", 1)
                        dveR.inc(nc.vector.scalar_tensor_tensor(tokf[:, :], bk[:, :], float(P), cn[:, :], ALU.mult, ALU.add), "tb")
                        dveR.wait(v, t, "tb")
                        dveR.inc(nc.vector.tensor_copy(tok[:, p], tokf[:, :]), "tok")
                    if s == "gates":
                        v.wait_ge(xg_in, 16 * NG * t + 16 * NG)
                        dveD.wait(v, t, f"o{NG-1}", 2)
                        for j in range(GS):
                            dveR.inc(nc.vector.tensor_copy(gate[:, p, 2 * j:2 * j + 2], xg[:, 2 * j:2 * j + 2, bass.ds(C + GS * t + j, 1)].rearrange("p a o -> p (a o)")), f"g{j}")
                    if s == "t":
                        k, h = i % KC, i // KC
                        peR.wait(v, t, f"t{i}")
                        if i == 0:
                            peU.wait(v, t, f"u{NU-1}", 1)
                        ts = slice(h * 512, (h + 1) * 512)
                        dveR.inc(nc.vector.tensor_copy(xh[:, k, ts], psR[i % 2][:, :]), f"th{i}")
                        dveR.wait(v, t, f"th{i}")
                        dveR.inc(nc.vector.tensor_tensor(xl[:, k, ts], psR[i % 2][:, :], xh[:, k, ts].bitcast(F32), ALU.subtract), f"t{i}")

                def down(t, p, n):
                    j, a = n // 2, n % 2
                    peD.wait(v, t, f"d{n}")
                    if n == 0:
                        dveR.wait(v, t, f"g{GS-1}")
                    if a == 0:
                        v.wait_ge(added[(j - 1) % 2], 16 + 32 * (2 * t + (j + 1) // 2))
                    dveD.inc(nc.vector.tensor_scalar(ob[:, n % 2, :], psD[n % 3][:, :], gate[:, p, n:n + 1], None, ALU.mult), f"o{n}")

                    if a == 0 and not (isinstance(t, int) and t == GRP - 1):
                        v.wait_ge(wu_in, 16 * KC + 16 * KC * t + 16 * (j + 1))
                        peU.wait(v, t, f"u{NU-1}")
                        dveW.inc(nc.vector.tensor_copy(wuh[:, j, :], wur[:, :]), f"h{j}")
                        dveW.wait(v, t, f"h{j}")
                        dveW.inc(nc.vector.tensor_tensor(wul[:, j, :], wur[:, :], wuh[:, j, :].bitcast(F32), ALU.subtract), f"l{j}")

                walk(v, fetch_step, nothing, down)




def consts_np():
    i = np.arange(P)
    k, m = i[:, None], i[None, :]
    c = {
        "ident": k == m, "tri": k <= m, "ones": k >= 0 * m, "gmat": (k // 16 == m // 16) / 16.0,
        "sameexp": k % E == m % E, "segbefore": (k % E == m % E) & (k // E < m // E),
        "dup0": k == m % HD, "dup1": k == HD + m % HD,
    }
    c = {n: np.ascontiguousarray(np.broadcast_to(x, (P, P)), np.float32) for n, x in c.items()}
    r = np.arange(48)[:, None] % NH == np.arange(NH * P)[None, :] // P
    c["selp"] = r.astype(np.float32)
    ch = np.arange(C)
    c["headof"] = (ch[:, None] // HD == np.arange(C // HD)).astype(np.float32).reshape(KC, P, -1).transpose(1, 0, 2).copy()
    c["headsel"] = (ch // HD == np.arange(C // HD)[:, None]).astype(np.float32)
    return c


def program(nc, io):
    ctx = ExitStack()
    with ctx:
        def sb(name, shape, dt=F32):
            return ctx.enter_context(nc.sbuf_tensor(name, shape, dt))
        consts = {k: sb("k_" + k, [P, P]) for k in _CONSTS1}
        first_layer(nc, io, consts)
        consts["probs"] = sb("probs", [P, NT // 4])
        attention(nc, io, consts)
        keep = {"wur": sb("wur", [P, FF]), "wuh": sb("wuh", [P, KC, FF], F32R), "wul": sb("wul", [P, KC, FF], F32R), "wd": sb("wd", [P, 2, FT, C]), "slot": sb("slot", [P, 2]),
                "rowi": sb("rowi", [P, 2 * E], I32), "blkf": sb("blkf", [P, E, 2])}
        keep["wu_in"] = ctx.enter_context(nc.semaphore("wu_in"))
        keep["wd_in"] = [ctx.enter_context(nc.semaphore(f"wd_in{i}")) for i in range(2)]
        routing(nc, io, consts, keep)
        experts(nc, io, consts, keep)




def _layout(i):
    f = lambda n: np.ascontiguousarray(i[n])
    x = f("x").reshape(NB, C, L)
    col = lambda a: np.ascontiguousarray(a.reshape(-1, P).T)
    a = {
        "x_ch": x, "x_tok": np.ascontiguousarray(x.transpose(0, 2, 1)).reshape(NT // P, P, C),
        "win_t": np.ascontiguousarray(f("L0_conv_in_proj_w").T), "wo": f("L0_conv_out_proj_w"),
        "w2_t": np.ascontiguousarray(f("L0_conv_conv2d_w").T),
        "rms_w": col(f("L0_conv_rms_w")), "ln_w": col(f("L0_conv_ln_w")), "ln_b": col(f("L0_conv_ln_b")),
        "conv_w": np.ascontiguousarray(f("L0_conv_conv1d_w").reshape(-1, P, 4).transpose(1, 0, 2)), "conv_b": col(f("L0_conv_conv1d_b")),
        "D": f("L0_conv_D"), "A_log": f("L0_conv_A_log"), "dt_bias": f("L0_conv_dt_bias"),
        "bn_g": f("L0_conv_bn_g"), "bn_b": f("L0_conv_bn_b"), "bn_mean": f("L0_conv_bn_mean"), "bn_var": col(f("L0_conv_bn_var")), "c2b": f("L0_conv_conv2d_b"),
    }
    a |= {
        "wq_t": np.ascontiguousarray(f("L1_attn_wq").T), "wk_t": np.ascontiguousarray(f("L1_attn_wk").T),
        "wv_t": np.ascontiguousarray(f("L1_attn_wv").T), "wo_t": np.ascontiguousarray(f("L1_attn_wo").T),
        "wr": f("L1_ffn_W_router"), "br": f("L1_ffn_b_router"), "g": col(f("L1_attn_g")),
    }
    wd = np.zeros((E, FT * P, C), np.float32)
    wd[:, :FF], wd[:, FF] = f("L1_ffn_W_down"), f("L1_ffn_b_down")
    bu = np.zeros((GRP, FT * P), np.float32)
    bu[:, :FF] = f("L1_ffn_b_up")
    a |= {
        "w_up": np.ascontiguousarray(f("L1_ffn_W_up").reshape(GRP, KC, P, FF).transpose(0, 2, 1, 3)).reshape(GRP, P, KC * FF),
        "w_down": np.ascontiguousarray(wd.reshape(E, FT, P, C).transpose(0, 2, 1, 3)).reshape(E, P, FT * C),
        "b_up": np.ascontiguousarray(bu.reshape(GRP, FT, P).transpose(2, 0, 1)),
        "slot": np.ascontiguousarray(np.arange(2 * P, dtype=np.float32).reshape(2, P).T),
        "rowbase": np.ascontiguousarray(np.broadcast_to(np.repeat(np.arange(E) * (NT // P), 2).astype(np.float32), (P, 2 * E))),
    }
    for n, c in consts_np().items():
        a[n if n in ("selp", "headof", "headsel") else "c_" + n] = c
    return a


def kernel(**inputs):
    import concourse.bacc as _bacc
    from concourse.bass_utils import run_bass_kernel_spmd as _run

    nc = _bacc.Bacc("TRN2", target_bir_lowering=False, num_devices=1)
    arrays = _layout({n: np.asarray(v) for n, v in inputs.items()})
    io = {n: nc.dram_tensor("in_" + n, a.shape, F32, kind="ExternalInput").ap() for n, a in arrays.items()}
    io["t1"] = nc.dram_tensor("tokens_1", (NT // P, P, C), F32, kind="Internal").ap()
    io["table"] = nc.dram_tensor("rows", (NT // P, P, ROW), F32, kind="Internal").ap()
    io["crow"] = nc.dram_tensor("running", (E * NT // P, P), F32, kind="Internal").ap()
    io["cend"] = nc.dram_tensor("block_ends", (E, NT // P), F32, kind="Internal").ap()
    io["y"] = nc.dram_tensor("out_y", (NT // P, P, C), F32, kind="ExternalOutput").ap()
    program(nc, io)
    r = _run(nc, [{"in_" + n: a for n, a in arrays.items()}], core_ids=[0])
    t = r.results[0]["out_y"].reshape(NB, L, C)
    return np.ascontiguousarray(t.transpose(0, 2, 1)).reshape(NB, C, 32, 32)
```
